# Optimizing a Trainium2 kernel written in Bass

```python
import numpy as np
import jax
import jax.numpy as jnp

def _softmax(x, axis=-1):
    return jax.nn.softmax(x, axis=axis)

def _gelu(x):
    return jax.nn.gelu(x, approximate=True)

def _silu(x):
    return jax.nn.silu(x)

def _sigmoid(x):
    return jax.nn.sigmoid(x)

def _layernorm(x, axis=-1, eps=1e-05):
    m = jnp.mean(x, axis=axis, keepdims=True)
    v = jnp.var(x, axis=axis, keepdims=True)
    return (x - m) / jnp.sqrt(v + eps)

def _scatter_add(tgt, idx, src, axis=0):
    return tgt.at[idx].add(src)

def _segment_sum(src, seg, n):
    return jax.ops.segment_sum(src, seg, n)
kernel_name = 'mk_gnn_ffn_d1_gnn_r8_6a5747'

def setup_inputs(seed: int=0):
    np.random.seed(seed)
    _w = jnp.asarray

    def _rec_inputs():
        import jax
        import jax.numpy as jnp
        _gk = jax.random.key(seed)
        x = -8.776e-05 + 1 * jax.random.normal(jax.random.fold_in(_gk, 1), (1250, 512), jnp.float32)
        _s = jax.random.randint(jax.random.fold_in(_gk, 2), (20000,), 0, 1250, jnp.int32)
        _d = jax.random.randint(jax.random.fold_in(_gk, 3), (20000,), 0, 1250, jnp.int32)
        _loop = jnp.arange(1250, dtype=jnp.int32)
        src = jnp.concatenate([_s, _d, _loop])
        dst = jnp.concatenate([_d, _s, _loop])
        _o = jnp.argsort(dst, stable=True)
        src = src[_o]
        dst = dst[_o]
        edge_attr_128 = 0.000283511 + 1.00007 * jax.random.normal(jax.random.fold_in(_gk, 11), (41250, 128), jnp.float32)
        return (x, src, dst, edge_attr_128)
    x, src, dst, edge_attr_128 = _rec_inputs()

    def _L0_gnn_setup():
        import jax, jax.numpy as jnp
        import numpy as np
        N, E = (1250, 18750)
        HD, ED = (512, 128)
        BN_EPS = 1e-05
        key = jax.random.key(seed)
        ks = jax.random.split(key, 16)
        s = 0.02
        return {'h': jax.random.normal(ks[0], (N, HD), jnp.float32), 'edge_index': jax.random.randint(ks[1], (2, E), 0, N, jnp.int32), 'edge_attr': jax.random.normal(ks[2], (E, ED), jnp.float32), 'W1': jax.random.normal(ks[3], (HD, HD + ED), jnp.float32) * s, 'b1': jnp.zeros((HD,), jnp.float32), 'W2': jax.random.normal(ks[4], (HD, HD), jnp.float32) * s, 'b2': jnp.zeros((HD,), jnp.float32), 'W_ih': jax.random.normal(ks[5], (3 * HD, HD), jnp.float32) * s, 'W_hh': jax.random.normal(ks[6], (3 * HD, HD), jnp.float32) * s, 'b_ih': jnp.zeros((3 * HD,), jnp.float32), 'b_hh': jnp.zeros((3 * HD,), jnp.float32), 'gamma': jnp.ones((HD,), jnp.float32), 'beta': jnp.zeros((HD,), jnp.float32), 'run_mean': jnp.zeros((HD,), jnp.float32), 'run_var': jnp.ones((HD,), jnp.float32)}
    _L0_gnn_all = _L0_gnn_setup()
    _L0_gnn_in = {k: v for k, v in _L0_gnn_all.items() if k in ('W1', 'b1', 'W2', 'b2', 'W_ih', 'W_hh', 'b_ih', 'b_hh', 'gamma', 'beta', 'run_mean', 'run_var')}
    del _L0_gnn_all

    def _L0_ffn_setup():
        import jax, jax.numpy as jnp
        import numpy as np
        E, TOPK, H, DK, DV, D = (4, 2, 8, 64, 64, 512)
        B, L = (4, 1024)
        VDIM = H * DV

        def _silu(x):
            return x * jax.nn.sigmoid(x)

        def _l2norm(x):
            return x * jax.lax.rsqrt(jnp.sum(x * x, axis=-1, keepdims=True) + 1e-06)

        def _forward(h, Wq, Wgate, Wk, Wv, Wb, Wa, A_log, dt_bias, Wg, o_norm_weight, Wo):
            Bs, Ls, _ = h.shape
            scores = jax.nn.softmax((h @ Wgate).astype(jnp.float32), axis=-1)
            rw, sel = jax.lax.top_k(scores, TOPK)
            rw = rw / jnp.sum(rw, axis=-1, keepdims=True)
            bi = jnp.arange(Bs)[:, None, None]
            li = jnp.arange(Ls)[None, :, None]
            w_full = jnp.zeros((Bs, Ls, E), jnp.float32).at[bi, li, sel].set(rw)
            m = jnp.transpose(w_full > 0, (2, 0, 1))
            q = _l2norm(_silu(h @ Wq).reshape(Bs, Ls, H, DK))
            k = _l2norm(_silu(h @ Wk).reshape(Bs, Ls, H, DK))
            v = _silu(h @ Wv).reshape(Bs, Ls, H, DV)
            beta = jax.nn.sigmoid(h @ Wb)
            g = -jnp.exp(A_log) * jax.nn.softplus((h @ Wa).astype(jnp.float32) + dt_bias)
            beta_e = beta[None] * m[..., None]
            g_e = jnp.where(m[..., None], g[None], 0.0)
            scale = DK ** (-0.5)
            xs = (jnp.moveaxis(q, 1, 0), jnp.moveaxis(k, 1, 0), jnp.moveaxis(v, 1, 0), jnp.moveaxis(beta_e, 2, 0), jnp.moveaxis(g_e, 2, 0))

            def step(S, x):
                qt, kt, vt, bt, gt = x
                S = S * jnp.exp(gt)[..., None, None]
                kv = jnp.einsum('bhk,ebhkv->ebhv', kt, S)
                delta = (vt[None] - kv) * bt[..., None]
                S = S + kt[None, :, :, :, None] * delta[..., None, :]
                ot = jnp.einsum('bhk,ebhkv->ebhv', qt * scale, S)
                return (S, ot)
            S0 = jnp.zeros((E, Bs, H, DK, DV), jnp.float32)
            _, o = jax.lax.scan(step, S0, xs)
            o = jnp.moveaxis(o, 0, 2)
            core = jnp.einsum('ble,eblhv->blhv', w_full, o)
            gate = _silu((h @ Wg).reshape(Bs, Ls, H, DV))
            core = core * jax.lax.rsqrt(jnp.mean(core * core, axis=-1, keepdims=True) + 1e-05)
            core = core * o_norm_weight * gate
            return core.reshape(Bs, Ls, VDIM) @ Wo
        key = jax.random.key(seed)
        ks = jax.random.split(key, 12)
        std = 0.02
        h = jax.random.normal(ks[0], (B, L, D), jnp.float32)
        Wq = jax.random.normal(ks[1], (D, H * DK), jnp.float32) * std
        Wgate = jax.random.normal(ks[2], (D, E), jnp.float32) * std
        Wk = jax.random.normal(ks[3], (D, H * DK), jnp.float32) * std
        Wv = jax.random.normal(ks[4], (D, VDIM), jnp.float32) * std
        Wb = jax.random.normal(ks[5], (D, H), jnp.float32) * std
        Wa = jax.random.normal(ks[6], (D, H), jnp.float32) * std
        Wg = jax.random.normal(ks[7], (D, VDIM), jnp.float32) * std
        Wo = jax.random.normal(ks[8], (VDIM, D), jnp.float32) * std
        A = jax.random.uniform(ks[9], (H,), jnp.float32, 0.0001, 16.0)
        A_log = jnp.log(A)
        dt = jnp.exp(jax.random.uniform(ks[10], (H,), jnp.float32) * (np.float32(np.log(0.1)) - np.float32(np.log(0.001))) + np.float32(np.log(0.001)))
        dt = jnp.maximum(dt, 0.0001)
        dt_bias = dt + jnp.log(-jnp.expm1(-dt))
        o_norm_weight = jnp.ones((DV,), jnp.float32)
        return {'hidden_states': h, 'Wq': Wq, 'Wgate': Wgate, 'Wk': Wk, 'Wv': Wv, 'Wb': Wb, 'Wa': Wa, 'A_log': A_log, 'dt_bias': dt_bias, 'Wg': Wg, 'o_norm_weight': o_norm_weight, 'Wo': Wo}
    _L0_ffn_all = _L0_ffn_setup()
    _L0_ffn_in = {k: v for k, v in _L0_ffn_all.items() if k in ('Wq', 'Wgate', 'Wk', 'Wv', 'Wb', 'Wa', 'A_log', 'dt_bias', 'Wg', 'o_norm_weight', 'Wo')}
    del _L0_ffn_all
    return {'x': x, 'src': src, 'dst': dst, 'edge_attr_128': edge_attr_128, 'L0_gnn_W1': _L0_gnn_in['W1'], 'L0_gnn_b1': _L0_gnn_in['b1'], 'L0_gnn_W2': _L0_gnn_in['W2'], 'L0_gnn_b2': _L0_gnn_in['b2'], 'L0_gnn_W_ih': _L0_gnn_in['W_ih'], 'L0_gnn_W_hh': _L0_gnn_in['W_hh'], 'L0_gnn_b_ih': _L0_gnn_in['b_ih'], 'L0_gnn_b_hh': _L0_gnn_in['b_hh'], 'L0_gnn_gamma': _L0_gnn_in['gamma'], 'L0_gnn_beta': _L0_gnn_in['beta'], 'L0_gnn_run_mean': _L0_gnn_in['run_mean'], 'L0_gnn_run_var': _L0_gnn_in['run_var'], 'L0_ffn_Wq': _L0_ffn_in['Wq'], 'L0_ffn_Wgate': _L0_ffn_in['Wgate'], 'L0_ffn_Wk': _L0_ffn_in['Wk'], 'L0_ffn_Wv': _L0_ffn_in['Wv'], 'L0_ffn_Wb': _L0_ffn_in['Wb'], 'L0_ffn_Wa': _L0_ffn_in['Wa'], 'L0_ffn_A_log': _L0_ffn_in['A_log'], 'L0_ffn_dt_bias': _L0_ffn_in['dt_bias'], 'L0_ffn_Wg': _L0_ffn_in['Wg'], 'L0_ffn_o_norm_weight': _L0_ffn_in['o_norm_weight'], 'L0_ffn_Wo': _L0_ffn_in['Wo']}

def reference(x, src, dst, edge_attr_128, L0_gnn_W1, L0_gnn_b1, L0_gnn_W2, L0_gnn_b2, L0_gnn_W_ih, L0_gnn_W_hh, L0_gnn_b_ih, L0_gnn_b_hh, L0_gnn_gamma, L0_gnn_beta, L0_gnn_run_mean, L0_gnn_run_var, L0_ffn_Wq, L0_ffn_Wgate, L0_ffn_Wk, L0_ffn_Wv, L0_ffn_Wb, L0_ffn_Wa, L0_ffn_A_log, L0_ffn_dt_bias, L0_ffn_Wg, L0_ffn_o_norm_weight, L0_ffn_Wo):
    import jax
    import jax.numpy as jnp

    def _L0_gnn_ref(h, edge_index, edge_attr, W1, b1, W2, b2, W_ih, W_hh, b_ih, b_hh, gamma, beta, run_mean, run_var):
        import jax, jax.numpy as jnp
        import numpy as np
        N, E = (1250, 18750)
        HD, ED = (512, 128)
        BN_EPS = 1e-05
        src, dst = (edge_index[0], edge_index[1])
        m_in = jnp.concatenate([h[src], edge_attr], axis=1)
        m = jax.nn.relu(m_in @ W1.T + b1) @ W2.T + b2
        agg = jax.ops.segment_sum(m, dst, num_segments=h.shape[0])
        gi = agg @ W_ih.T + b_ih
        gh = h @ W_hh.T + b_hh
        i_r, i_z, i_n = jnp.split(gi, 3, axis=1)
        h_r, h_z, h_n = jnp.split(gh, 3, axis=1)
        r = jax.nn.sigmoid(i_r + h_r)
        z = jax.nn.sigmoid(i_z + h_z)
        n = jnp.tanh(i_n + r * h_n)
        h_new = (1.0 - z) * n + z * h
        bn = gamma * (h_new - run_mean) * jax.lax.rsqrt(run_var + BN_EPS) + beta
        return h + bn

    def _L0_ffn_ref(hidden_states, Wq, Wgate, Wk, Wv, Wb, Wa, A_log, dt_bias, Wg, o_norm_weight, Wo):
        import jax, jax.numpy as jnp
        import numpy as np
        E, TOPK, H, DK, DV, D = (4, 2, 8, 64, 64, 512)
        B, L = (4, 1024)
        VDIM = H * DV

        def _silu(x):
            return x * jax.nn.sigmoid(x)

        def _l2norm(x):
            return x * jax.lax.rsqrt(jnp.sum(x * x, axis=-1, keepdims=True) + 1e-06)

        def _forward(h, Wq, Wgate, Wk, Wv, Wb, Wa, A_log, dt_bias, Wg, o_norm_weight, Wo):
            Bs, Ls, _ = h.shape
            scores = jax.nn.softmax((h @ Wgate).astype(jnp.float32), axis=-1)
            rw, sel = jax.lax.top_k(scores, TOPK)
            rw = rw / jnp.sum(rw, axis=-1, keepdims=True)
            bi = jnp.arange(Bs)[:, None, None]
            li = jnp.arange(Ls)[None, :, None]
            w_full = jnp.zeros((Bs, Ls, E), jnp.float32).at[bi, li, sel].set(rw)
            m = jnp.transpose(w_full > 0, (2, 0, 1))
            q = _l2norm(_silu(h @ Wq).reshape(Bs, Ls, H, DK))
            k = _l2norm(_silu(h @ Wk).reshape(Bs, Ls, H, DK))
            v = _silu(h @ Wv).reshape(Bs, Ls, H, DV)
            beta = jax.nn.sigmoid(h @ Wb)
            g = -jnp.exp(A_log) * jax.nn.softplus((h @ Wa).astype(jnp.float32) + dt_bias)
            beta_e = beta[None] * m[..., None]
            g_e = jnp.where(m[..., None], g[None], 0.0)
            scale = DK ** (-0.5)
            xs = (jnp.moveaxis(q, 1, 0), jnp.moveaxis(k, 1, 0), jnp.moveaxis(v, 1, 0), jnp.moveaxis(beta_e, 2, 0), jnp.moveaxis(g_e, 2, 0))

            def step(S, x):
                qt, kt, vt, bt, gt = x
                S = S * jnp.exp(gt)[..., None, None]
                kv = jnp.einsum('bhk,ebhkv->ebhv', kt, S)
                delta = (vt[None] - kv) * bt[..., None]
                S = S + kt[None, :, :, :, None] * delta[..., None, :]
                ot = jnp.einsum('bhk,ebhkv->ebhv', qt * scale, S)
                return (S, ot)
            S0 = jnp.zeros((E, Bs, H, DK, DV), jnp.float32)
            _, o = jax.lax.scan(step, S0, xs)
            o = jnp.moveaxis(o, 0, 2)
            core = jnp.einsum('ble,eblhv->blhv', w_full, o)
            gate = _silu((h @ Wg).reshape(Bs, Ls, H, DV))
            core = core * jax.lax.rsqrt(jnp.mean(core * core, axis=-1, keepdims=True) + 1e-05)
            core = core * o_norm_weight * gate
            return core.reshape(Bs, Ls, VDIM) @ Wo
        return _forward(hidden_states, Wq, Wgate, Wk, Wv, Wb, Wa, A_log, dt_bias, Wg, o_norm_weight, Wo)
    edge_index = jnp.stack([src, dst])
    x = x + _L0_gnn_ref(_layernorm(x, axis=-1), edge_index, edge_attr_128, L0_gnn_W1, L0_gnn_b1, L0_gnn_W2, L0_gnn_b2, L0_gnn_W_ih, L0_gnn_W_hh, L0_gnn_b_ih, L0_gnn_b_hh, L0_gnn_gamma, L0_gnn_beta, L0_gnn_run_mean, L0_gnn_run_var)
    x = x + _L0_ffn_ref(_layernorm(x, axis=-1)[None], L0_ffn_Wq, L0_ffn_Wgate, L0_ffn_Wk, L0_ffn_Wv, L0_ffn_Wb, L0_ffn_Wa, L0_ffn_A_log, L0_ffn_dt_bias, L0_ffn_Wg, L0_ffn_o_norm_weight, L0_ffn_Wo)[0]
    return x

_drawn_inputs = setup_inputs


def setup_inputs(seed=0):
    import zlib

    import numpy as np

    out = dict(_drawn_inputs(seed))
    spreads = {'L0_gnn_b1': (0.0, 0.1),
     'L0_gnn_b2': (0.0, 0.1),
     'L0_gnn_b_ih': (0.0, 0.518),
     'L0_gnn_b_hh': (0.0, 0.73),
     'L0_gnn_gamma': (1.0, 0.2),
     'L0_gnn_beta': (0.0, 0.1),
     'L0_gnn_run_mean': (0.0, 0.1),
     'L0_gnn_run_var': (1.0, 0.534),
     'L0_ffn_o_norm_weight': (1.0, 0.6)}
    factors = {'L0_ffn_Wgate': 10.743,
     'L0_ffn_Wb': 8.0,
     'L0_ffn_Wa': 36.687,
     'L0_ffn_A_log': 27.583,
     'L0_ffn_dt_bias': 24.582}
    for name, (base, spread) in spreads.items():
        noise = np.random.default_rng([zlib.crc32(name.encode()), seed]).standard_normal(out[name].shape)
        drawn = base * np.exp(spread * noise) if base else spread * noise
        out[name] = jnp.asarray(drawn.astype(out[name].dtype))
    for name, factor in factors.items():
        out[name] = (out[name] * factor).astype(out[name].dtype)
    return out
```

```python
from contextlib import ExitStack

import numpy as np

import concourse.bass as bass
from concourse import mybir

F32 = mybir.dt.float32
I32 = mybir.dt.int32
ALU = mybir.AluOpType
ACT = mybir.ActivationFunctionType
AX = mybir.AxisListType
RMAX = bass.bass_isa.ReduceOp.max

N = 1250
D = 512
KC = D // 128
TP = 125
NT = N // TP
E = 41250
ED = 128
ET = E // TP
GT = 5
G = ET // GT
BODY = 2 * GT
RB = 5
NB = ET // BODY
W = 32
NPAD = N + W
C = 32
NC = 40
NTOK = C * NC
TT = NTOK // 128
H = 8
DK = 64
X = 4
SG = 2 * X
TB = 4
TBW = NTOK // TB
QG = 5
LOG_TERMS = 10
LOADS = 16 * 9
G_FLOOR = -200.0
LN_EPS = 1e-5
BN_EPS = 1e-5


class Steps:

    def __init__(self, eng, sem):
        self.eng, self.sem, self.n = eng, sem, 0

    def did(self, ins):
        ins.then_inc(self.sem, 1)
        self.n += 1
        return self.n

    def settle(self):
        self.eng.wait_ge(self.sem, self.n)

    def then(self, ins):
        self.did(ins)
        self.settle()


def build(nc, io):
    with ExitStack() as ctx:
        def sb(name, shape, dt=F32):
            return ctx.enter_context(nc.sbuf_tensor(name, shape, dt))

        def sem(name):
            return ctx.enter_context(nc.semaphore(name))

        psum = ctx.enter_context(nc.psum_tensor("psum", [128, 8, 512], F32))

        ident = sb("ident", [128, 128])
        xt = sb("xt", [TP, NT, D])
        ht = sb("ht", [128, NT, D])
        hT = sb("hT", [128, KC, NTOK])
        accT = sb("accT", [128, KC + 1, NPAD])
        stats = sb("stats", [TP, NT, 6])
        mv = sb("mv", [TP, NT, 2])
        rows = sb("rows", [1, D])
        rstd = sb("rstd", [TP, NT])
        ARENA = 24700
        arena = sb("arena", [128, ARENA])

        def carve(spec):
            out, at = {}, 0
            for name, rows, n in spec:
                out[name] = arena[0:rows, at:at + n]
                at += n
            assert at <= ARENA, at
            return out

        a = carve([("w2", 128, KC * D), ("w1h", 128, KC * D), ("w1e", 128, D), ("b1", TP, D),
                   ("ea", 128, 2 * GT * TP), ("pg", TP, BODY * D), ("rl", TP, RB * D), ("oh", TP, 2 * GT * W),
                   ("pw", TP, 2 * D), ("rel", TP, ET), ("dstf", TP, ET), ("dsti", TP, ET), ("srci", TP, ET),
                   ("base", TP, G), ("high", TP, G), ("start", TP, G), ("starti", TP, G), ("iota", TP, W),
                   ("ones", TP, 1), ("idx", TP, BODY), ("span", TP, 1), ("npass", TP, 1)])
        w1h = a["w1h"].rearrange("p (k n) -> p k n", k=KC)
        w2 = a["w2"].rearrange("p (k n) -> p k n", k=KC)
        ea = a["ea"].rearrange("p (g n) -> p g n", g=2)
        pg = a["pg"].rearrange("p (s n) -> p s n", s=BODY)
        rl = a["rl"].rearrange("p (s n) -> p s n", s=RB)
        oh = a["oh"].rearrange("p (g t w) -> p g t w", g=2, t=GT)
        pw = a["pw"].rearrange("p (s n) -> p s n", s=2)
        rel, dstf = a["rel"], a["dstf"]
        dsti, srci, starti, idx, npass = (a[x].bitcast(I32) for x in ("dsti", "srci", "starti", "idx", "npass"))

        bo = carve([("w2", 128, KC * D), ("whh", 128, KC * 3 * D), ("aggT", 128, KC * N), ("rz", TP, 2 * D),
                    ("hn", TP, D), ("in", TP, D), ("new", TP, D), ("gap", 128, 1700), ("wih", 128, KC * 3 * D)])
        wih = bo["wih"].rearrange("p (k n) -> p k n", k=KC)
        whh = bo["whh"].rearrange("p (k n) -> p k n", k=KC)
        aggT = bo["aggT"].rearrange("p (k n) -> p k n", k=KC)
        accf = accT[:, :, :].rearrange("p c n -> p (c n)")
        vec = accf[0:TP, 0:10 * D]

        f = carve([("kqT", 128, 4 * NC * 2 * C), ("wq", 128, KC * D), ("wk", 128, KC * D), ("wv", 128, KC * D),
                   ("wg", 128, KC * D), ("wo", 128, KC * D), ("wsm", 128, KC * 20), ("dbuf", 128, 2720),
                   ("gt", 128, 128), ("leb", 128, 128), ("bd", 128, 128), ("s0", 128, 128), ("s1", 128, 128),
                   ("bd64", 128, 128), ("le", 128, C), ("eye", 128, C), ("mask2", 128, 2 * C), ("lt4", 128, 16),
                   ("alog", 128, H), ("dtb", 128, H), ("onorm", 128, DK)])
        kqT = f["kqT"].rearrange("p (h q c i) -> p h q c i", h=4, c=NC, q=2)
        proj = {n: f[n].rearrange("p (k n) -> p k n", k=KC) for n in ("wq", "wk", "wv", "wg", "wo")}
        wsm = f["wsm"].rearrange("p (k n) -> p k n", k=KC)
        dbuf = f["dbuf"]
        wreg = arena[:, 4 * NC * 2 * C:4 * NC * 2 * C + 8192]
        gw = wreg[:, 5632:5632 + NC * 24].rearrange("p (c n) -> p c n", c=NC)
        dec = wreg[:, 6592:6592 + 1600]
        Gam, bDC, wGam = (dec[:, k * 320:(k + 1) * 320].rearrange("p (c n) -> p c n", c=NC) for k in range(3))
        GamC = dec[:, 960:1600].rearrange("p (s c n) -> p s c n", s=2, c=NC)
        hTf = hT[:, :, :].rearrange("p k n -> p (k n)")
        Lsys = hTf.rearrange("p (q j i) -> p q j i", q=QG, j=C)
        XTs = accf[:, 0:QG * C * C].rearrange("p (q n i) -> p q n i", q=QG, n=C)
        Prod = wreg[:, 0:QG * 31 * 31]

        KV_dram = nc.dram_tensor("KV_scratch", [NC, 128, 384], F32, kind="Internal").ap()
        GW_dram = nc.dram_tensor("GW_scratch", [NC, 128, 24], F32, kind="Internal").ap()
        L_dram = nc.dram_tensor("L_scratch", [NC * SG * 4, C * C], F32, kind="Internal").ap()
        X_dram = nc.dram_tensor("X_scratch", [NC * SG * 4, C * C], F32, kind="Internal").ap()
        A_dram = nc.dram_tensor("A_scratch", [NC, 128, SG * C], F32, kind="Internal").ap()
        O_dram = nc.dram_tensor("O_scratch", [4, NTOK, 128], F32, kind="Internal").ap()

        P_dram = nc.dram_tensor("P_scratch", [N, D], F32, kind="Internal").ap()

        def take(base, at, n):
            return base[:, at:at + n]

        rg = take(dbuf, 0, 256).rearrange("p (g i) -> p g i", g=SG)
        wd = take(dbuf, 256, 128).rearrange("p (e i) -> p e i", e=X)
        ex = take(dbuf, 384, 256).rearrange("p (g i) -> p g i", g=SG)
        kkm = take(dbuf, 640, 128).rearrange("p (h q i) -> p h q i", h=2, q=2)
        at1 = take(dbuf, 768, 256).rearrange("p (g i) -> p g i", g=SG)
        kqc = [take(dbuf, 1024 + 256 * q, 256).rearrange("p (h n) -> p h n", h=4) for q in range(2)]
        lt = [take(dbuf, 1536 + 256 * q, 256).rearrange("p (g i) -> p g i", g=SG) for q in range(2)]
        at = [take(dbuf, 2048 + 256 * q, 256).rearrange("p (g i) -> p g i", g=SG) for q in range(2)]
        xbd = [take(accf, 1024 * q, 1024).rearrange("p (g i) -> p g i", g=SG) for q in range(2)]
        abd = [take(accf, 2048 + 1024 * q, 1024).rearrange("p (g i) -> p g i", g=SG) for q in range(2)]
        state = take(accf, 4096, 1024)
        sdec = take(accf, 5120, 1024)
        state4, sdec4 = (x.rearrange("p (s h e v) -> p s h e v", s=2, h=2, e=X) for x in (state, sdec))
        kvc = [take(wreg, 384 * q, 384) for q in range(2)]
        kbd = [kvc[q][:, 0:256].rearrange("p (h n) -> p h n", h=2) for q in range(2)]
        vch = [kvc[q][:, 256:384] for q in range(2)]
        kqb = [take(wreg, 768 + 512 * q, 512).rearrange("p (h q n) -> p h q n", h=4, q=2) for q in range(2)]
        resid, ksd, usb, ups, qsd = (take(wreg, 1792 + 512 * k, 512) for k in range(5))
        osb = [take(wreg, 4352 + 128 * q, 128) for q in range(2)]
        qsr = take(wreg, 4608, 128)
        core = hTf.rearrange("p (t n) -> p t n", t=TT)
        sqb = wreg[:, 0:512]
        cstat = wreg[:, 512:592].rearrange("p (t h) -> p t h", t=TT)
        coreT = accf[:, 0:KC * NTOK].rearrange("p (k n) -> p k n", k=KC)

        rt, at_ = {}, 2048
        for name, shape in (("mx", [TT]), ("lg", [TT, X]), ("p", [TT, X]), ("gt", [TT, X, X]), ("eq", [TT, X, X])):
            n = int(np.prod(shape))
            v_ = dbuf[:, at_:at_ + n]
            rt[name] = v_ if len(shape) == 1 else v_.rearrange("p (t e) -> p t e", t=TT) if len(shape) == 2 else \
                v_.rearrange("p (t e g) -> p t e g", t=TT, e=X)
            at_ += n
        small = sb("small", [128, 5 * TT * H + H])
        for k, name in enumerate(("a", "b", "ax", "eb", "y")):
            rt[name] = small[:, k * 80:(k + 1) * 80].rearrange("p (t h) -> p t h", t=TT)
        rt["ea"] = small[:, 400:408]
        rt["t1"] = sb("t1", [128, TT, H])[:, :, :]
        rt["sq"] = [accf[:, k * TBW:(k + 1) * TBW] for k in range(2)]
        ktb = [accf[:, 1280 + 1024 * k:2304 + 1024 * k] for k in range(2)]
        rt["nrm"] = [accf[:, (2 + k) * TBW:(3 + k) * TBW] for k in range(2)]

        S = {n: sem(n) for n in (
            "x_in", "w1_in", "ids_in", "consts", "dve", "act", "pool", "ln_mv", "ln_std", "ln_h", "ln_T", "ln_hT",
            "P_mm", "P_sb", "P_out0", "P_out1", "spans", "base_ok", "pass_ok", "tables",
            "ea_in0", "ea_in1", "ea_free", "pre_mm", "pre_add", "relu", "relu_free", "oh_ok", "acc_mm", "acc_add",
            "pg_free", "idx_ok", "out_d", "w1_free", "iota_ok", "gather_go", "b2_in", "wih_in", "whh_in", "vec_in",
            "agg_mm", "agg_sb", "gate_mm", "gate_rd", "rz_pre", "rz", "n_pre", "n_ok", "x1_ok", "ln2_mv", "ln2_std", "ln2_h", "ln2_T",
            "ln2_hT", "ffnw_in", "cst_in", "z_mm", "z_ok", "sq_ok", "ss_mm", "ss_ok", "nrm_ok", "kq_ok", "kT_mm", "kt_ok", "kt_st0", "kt_st1",
            "sm_mm", "lg_pre", "p_ok", "ab_pre", "ab_ok", "gw_ok", "gw_st", "gw_in", "v_mm", "v_ok", "v_st0", "v_st1", "gt_mm", "gt_ok",
            "dec_mm", "dec_ok", "dec_all", "rg_ok", "dkq_ok", "dw_mm", "d_mm", "e_ok", "kk_ok", "lt_ok", "at_ok", "lt_st0", "lt_st1", "at_st0", "at_st1",
            "l_in", "x_ok", "x_st", "ld0", "ld1", "bdz", "kqs", *(f"{x}{hh}" for x in ("ks_mm", "r_ok", "u_mm", "u_ok", "up_ok", "su_mm", "sd_ok", "s_ok", "o_mm") for hh in range(2)),
            "o_ok", "o_st0", "o_st1", "core_in", "cn_a", "cn_b", "core_ok", "cT_mm", "cT_ok", "out_mm", "out_ok", "out_st0", "out_st1", "pad_ok", "dbg", "dve2", "bn_std", "bn_pre", "xs_go")}
        gath = [sem(f"gathered{k}") for k in range(BODY)]
        block = ctx.enter_context(nc.Block())

        def passes(eng):
            eng.wait_ge(S["pass_ok"], 1)
            return eng.value_load(npass[0:1, 0:1], min_val=0, max_val=(N + W - 1) // W)

        @block.sync
        def _(sp):
            sp.dma_start(xt[:, :, :], io["x"].rearrange("(t p) n -> p t n", p=TP)).then_inc(S["x_in"], 16)
            sp.dma_start(dsti, io["dst_t"]).then_inc(S["ids_in"], 16)
            sp.dma_start(srci, io["src_t"]).then_inc(S["ids_in"], 16)
            sp.dma_start(w1h, io["w1h_T"].rearrange("(k p) n -> p k n", p=128)).then_inc(S["w1_in"], 16)
            sp.dma_start(a["w1e"], io["w1e_T"]).then_inc(S["w1_in"], 16)
            sp.dma_start(a["b1"], io["b1"].to_broadcast([TP, D])).then_inc(S["w1_in"], 16)
            sp.dma_start(w2, io["w2_T"].rearrange("(k p) n -> p k n", p=128)).then_inc(S["w1_in"], 16)
            for t in range(NT):
                sp.wait_ge(S["P_sb"], t + 1)
                sp.dma_start(P_dram[t * TP:(t + 1) * TP, :], pw[:, t % 2, :]).then_inc(S[f"P_out{t % 2}"], 16)
            n = passes(sp)
            with sp.Fori(0, n + 1) as p:
                with sp.Fori(0, NB) as i:
                    for h in range(2):
                        sp.wait_ge(S["pre_mm"], p * ET + i * BODY + (h + 1) * GT)
                        sp.dma_start(ea[:, h, :], io["ea_T"][:, bass.ds(i * (BODY * TP) + h * GT * TP, GT * TP)])\
                            .then_inc(S[f"ea_in{h}"], 16)
            sp.dma_start(rows[:, :], io["b2"]).then_inc(S["b2_in"], 16)
            sp.dma_start(wih, io["wih_T"].rearrange("(k p) n -> p k n", p=128)).then_inc(S["wih_in"], 16)
            sp.wait_ge(S["out_d"], 1)
            sp.dma_start(whh, io["whh_T"].rearrange("(k p) n -> p k n", p=128)).then_inc(S["whh_in"], 16)
            sp.wait_ge(S["agg_sb"], 12)
            for k, name in enumerate(("b_ih", "b_hh")):
                sp.dma_start(vec[:, k * 3 * D:(k + 1) * 3 * D], io[name].to_broadcast([TP, 3 * D])).then_inc(S["vec_in"], 16)
            for k, name in enumerate(("gamma", "beta", "run_mean", "run_var")):
                sp.dma_start(vec[:, (6 + k) * D:(7 + k) * D], io[name].to_broadcast([TP, D])).then_inc(S["vec_in"], 16)
            sp.wait_ge(S["x1_ok"], NT)
            for name in ("wk", "wq", "wv", "wg", "wo"):
                sp.dma_start(proj[name], io[name].rearrange("(k p) n -> p k n", p=128)).then_inc(S["ffnw_in"], 16)
            sp.dma_start(wsm, io["wsm"].rearrange("(k p) n -> p k n", p=128)).then_inc(S["ffnw_in"], 16)
            lo = 20480 + KC * 20 + 2720
            sp.dma_start(arena[:, lo:lo + io["cst"].shape[1]], io["cst"]).then_inc(S["cst_in"], 16)
            sp.dma_start(f["alog"], io["alog"].to_broadcast([128, H])).then_inc(S["cst_in"], 16)
            sp.dma_start(f["dtb"], io["dtb"].to_broadcast([128, H])).then_inc(S["cst_in"], 16)
            sp.dma_start(f["onorm"], io["onorm"].to_broadcast([128, DK])).then_inc(S["cst_in"], 16)

            def by_chunk(dram, t, q, tile, n, done):
                sp.dma_start(dram[4 * t + q].rearrange("(h i) n -> i h n", h=4),
                             tile[32 * q:32 * q + 32, :].rearrange("p (h n) -> p h n", h=4)).then_inc(done, 16)

            for t in range(TT):
                sp.wait_ge(S["v_ok"], t + 1)
                for q in range(4):
                    by_chunk(KV_dram[:, :, 256:384], t, q, dbuf[:, (t % 2) * D:(t % 2 + 1) * D], 128, S[f"v_st{t % 2}"])
            for t in range(TT):
                sp.wait_ge(S["kt_ok"], 2 * (t + 1))
                for q in range(4):
                    by_chunk(KV_dram[:, :, 0:256], t, q, ktb[t % 2], 256, S[f"kt_st{t % 2}"])
            sp.wait_ge(S["gw_ok"], 12)
            gwt = hTf[:, 0:TT * 96].rearrange("p (t n) -> p t n", t=TT)
            for t in range(TT):
                for q in range(4):
                    by_chunk(GW_dram, t, q, gwt[:, t, :], 24, S["gw_st"])
            sp.wait_ge(S["gw_st"], 16 * 4 * TT)
            sp.wait_ge(S["gt_mm"], NT)
            sp.wait_ge(S["sm_mm"], 1)
            sp.dma_start(gw, GW_dram.rearrange("c p n -> p c n")).then_inc(S["gw_in"], 16)
            with sp.Fori(0, NC // 2) as i:
                for q in range(2):
                    sp.wait_ge(S["lt_ok"], i * 2 + (q + 1))
                    sp.dma_start(L_dram[bass.ds((i * 2 + q) * (SG * 4), SG * 4), :].rearrange("(g h) (j i) -> (h j) g i", h=4, j=C),
                                 lt[q]).then_inc(S[f"lt_st{q}"], 16)
                    sp.wait_ge(S["at_ok"], i * 2 + (q + 3))
                    sp.dma_start(A_dram[bass.ds(i * 2 + q, 1), :, :].rearrange("c p n -> p (c n)"),
                                 at[q].rearrange("p g i -> p (g i)")).then_inc(S[f"at_st{q}"], 16)
            for q in range(2):
                sp.wait_ge(S[f"lt_st{q}"], 16 * NC // 2 + 16)
            for hf in range(2):
                if hf:
                    sp.wait_ge(S["x_ok"], hf)
                sp.wait_ge(S["at_ok"], NC + 2)
                if hf:
                    sp.wait_ge(S["x_st"], 16 * hf)
                sp.sem_inc(S["xs_go"], 1)
                sp.dma_start(Lsys.rearrange("p q j i -> p q (j i)"), L_dram[hf * QG * 128:(hf + 1) * QG * 128, :].rearrange("(q p) n -> p q n", p=128))\
                    .then_inc(S["l_in"], 16)
                sp.wait_ge(S["x_ok"], hf + 1)
                sp.dma_start(X_dram[hf * QG * 128:(hf + 1) * QG * 128, :].rearrange("(q p) n -> p q n", p=128), XTs.rearrange("p q n i -> p q (n i)"))\
                    .then_inc(S["x_st"], 16)
            sp.wait_ge(S["x_st"], 32)
            for q in range(2):
                sp.wait_ge(S[f"at_st{q}"], 16 * NC // 2 + 16)
            for q in range(2):
                sp.wait_ge(S[f"kt_st{q}"], 16 * 4 * TT // 2)
                sp.wait_ge(S[f"v_st{q}"], 16 * 4 * TT // 2)
            sp.wait_ge(S["bdz"], 2)
            def load(i, q):
                c = i * 2 + q
                for h in range(4):
                    rows_, cols = slice(32 * h, 32 * h + 32), slice(32 * h, 32 * h + 32)
                    sp.dma_start(xbd[q][rows_, :, cols],
                                 X_dram[bass.ds(c * (SG * 4), SG * 4), :].rearrange("(g h) (j i) -> h j g i", h=4, j=C)[h])\
                        .then_inc(S[f"ld{q}"], 16)
                    sp.dma_start(abd[q][rows_, :, cols],
                                 A_dram[bass.ds(c, 1), 32 * h:32 * h + 32, :].rearrange("c p (g i) -> p (c g) i", g=SG))\
                        .then_inc(S[f"ld{q}"], 16)
                sp.dma_start(kvc[q], KV_dram[bass.ds(c, 1), :, :].rearrange("c p n -> p (c n)")).then_inc(S[f"ld{q}"], 16)

            for q in range(2):
                load(0, q)

            def store(i, q):
                c = i * 2 + q
                sp.wait_ge(S["o_ok"], c * 2 + 6)
                for h in range(4):
                    sp.dma_start(O_dram[h, bass.ds(c * C, C), :], osb[q][32 * h:32 * h + 32, :]).then_inc(S[f"o_st{q}"], 16)

            with sp.Fori(0, NC // 2 - 1) as i:
                for q in range(2):
                    store(i, q)
                    load(i + 1, q)
            for q in range(2):
                store(NC // 2 - 1, q)
                sp.wait_ge(S[f"o_st{q}"], 16 * 4 * NC // 2 + 64)
            for t in range(TT):
                sp.dma_start(core[:, t, :].rearrange("p (h n) -> p h n", h=4),
                             O_dram[:, t * 128:(t + 1) * 128, :].rearrange("h p n -> p h n")).then_inc(S["core_in"], 16)
            for t in range(NT):
                sp.wait_ge(S["out_ok"], t + 1)
                sp.dma_start(io["out"][t * TP:(t + 1) * TP, :], xt[:, t, :]).then_inc(S["out_st0"], 16)
            sp.wait_ge(S["out_st0"], 16 * NT)

        @block.gpsimd
        def _(pool):
            st = Steps(pool, S["pool"])
            nc.gpsimd.iota(a["iota"].bitcast(I32), [[1, W]], base=0, channel_multiplier=0).then_inc(S["iota_ok"], 1)
            st.then(nc.gpsimd.memset(ident[:, :], 0.0))
            nc.gpsimd.memset(a["ones"], 1.0).then_inc(S["consts"], 1)
            nc.gpsimd.affine_select(out=ident[:, :], in_=ident[:, :], compare_op=ALU.not_equal, fill=1.0, base=0,
                                    pattern=[[-1, 128]], channel_multiplier=1).then_inc(S["consts"], 1)
            nc.gpsimd.memset(accT[:, :, :], 0.0).then_inc(S["consts"], 1)
            pool.wait_ge(S["spans"], 2)
            nc.gpsimd.partition_all_reduce(a["base"], a["start"], TP, RMAX).then_inc(S["base_ok"], 1)
            nc.gpsimd.partition_all_reduce(a["high"], a["high"], TP, RMAX).then_inc(S["base_ok"], 1)
            n = passes(pool)
            pool.wait_ge(S["P_out0"], 16 * (NT // 2))
            pool.wait_ge(S["P_out1"], 16 * (NT // 2))
            pool.wait_ge(S["ids_in"], 32)
            with pool.Fori(0, n + 1) as p:
                with pool.Fori(0, NB) as i:
                    for h in range(2):
                        pool.wait_ge(S["pg_free"], p * ET + i * BODY + (h + 1) * GT)
                        pool.sem_inc(S["gather_go"], 1)
                        nc.gpsimd.tensor_copy(idx[:, h * GT:h * GT + GT],
                                              srci[:, bass.ds(i * BODY + h * GT, GT)]).then_inc(S["idx_ok"], 1)
                        pool.wait_ge(S["idx_ok"], p * (2 * NB) + i * 2 + (h + 1))
                        pool.sem_inc(S["gather_go"], 1)
                        for k in range(h * GT, h * GT + GT):
                            nc.gpsimd.indirect_dma_start(
                                pg[:, k, :], None, P_dram, bass.IndirectOffsetOnAxis(ap=idx[:, k:k + 1], axis=0)
                            ).then_inc(gath[k], 16)

            pool.wait_ge(S["out_d"], 1)
            nc.gpsimd.memset(hT[:, :, N:NTOK], 0.0).then_inc(S["pad_ok"], 1)
            pool.wait_ge(S["gw_in"], 16)
            with pool.Fori(0, NC) as c:
                pool.wait_ge(S["dw_mm"], c + 1)
                pool.sem_inc(S["gather_go"], 1)
                gch = gw[:, bass.ds(c, 1), :].rearrange("p c n -> p (c n)")
                nc.gpsimd.tensor_tensor(rg, gch[:, 0:SG][:, :, None].to_broadcast([128, SG, C]),
                                        f["le"][:, None, :].to_broadcast([128, SG, C]), ALU.mult).then_inc(S["rg_ok"], 1)
                nc.gpsimd.tensor_tensor(wd, gch[:, 16:16 + X][:, :, None].to_broadcast([128, X, C]),
                                        f["eye"][:, None, :].to_broadcast([128, X, C]), ALU.mult).then_inc(S["rg_ok"], 1)
            pool.wait_ge(S["x_st"], 32)
            nc.gpsimd.memset(accf[:, 0:6144], 0.0).then_inc(S["bdz"], 1)
            nc.gpsimd.memset(wreg[:, 768:1792], 0.0).then_inc(S["bdz"], 1)
            with pool.Fori(0, NC) as c:
                for hh in range(2):
                    pool.wait_ge(S[f"s_ok{hh}"], c + 1)
                    pool.sem_inc(S["gather_go"], 1)
                    nc.gpsimd.tensor_tensor(sdec4[:, :, hh], state4[:, :, hh],
                                            GamC[:, :, bass.ds(c, 1), hh * X:(hh + 1) * X].rearrange("p s c n -> p s (c n)")[:, :, :, None]
                                            .to_broadcast([128, 2, X, DK]), ALU.mult).then_inc(S[f"sd_ok{hh}"], 1)

        @block.scalar
        def _(act):
            st = Steps(act, S["act"])
            act.wait_ge(S["ln_mv"], 1)
            nc.scalar.activation(rstd[:, :], rstd[:, :], ACT.Sqrt).then_inc(S["ln_std"], 1)
            act.sem_inc(S["pg_free"], BODY)
            n = passes(act)
            with act.Fori(0, n + 1) as p:
                with act.Fori(0, NB) as i:
                    for k in range(BODY):
                        act.wait_ge(S["pre_add"], p * ET + i * BODY + (RB + k + 1))
                        act.wait_ge(S["relu_free"], p * ET + i * BODY + (k + 1))
                        nc.scalar.activation(rl[:, k % RB, :], pg[:, k, :], ACT.Relu).then_inc(S["pg_free"], 1)

            for m_ in range(12):
                act.wait_ge(S["agg_mm"], m_ + 1)
                c_, b_ = m_ // 3, m_ % 3
                lo, hi = N * b_ // 3, N * (b_ + 1) // 3
                nc.scalar.activation(aggT[:, c_, lo:hi], psum[:, m_ % 8, 0:hi - lo], ACT.Copy).then_inc(S["agg_sb"], 1)
            act.wait_ge(S["bn_pre"], 1)
            nc.scalar.activation(vec[:, 9 * D:10 * D], vec[:, 9 * D:10 * D], ACT.Sqrt).then_inc(S["bn_std"], 1)
            for t in range(NT):
                act.wait_ge(S["rz_pre"], t + 1)
                nc.scalar.activation(bo["rz"], bo["rz"], ACT.Sigmoid).then_inc(S["rz"], 1)
                act.wait_ge(S["n_pre"], t + 1)
                nc.scalar.activation(bo["in"], bo["in"], ACT.Tanh).then_inc(S["n_ok"], 1)
            act.wait_ge(S["ln2_mv"], 1)
            nc.scalar.activation(rstd[:, :], rstd[:, :], ACT.Sqrt).then_inc(S["ln2_std"], 1)
            for m_ in range(32):
                q, hp, tb = m_ // 16, m_ // 4 % 4, m_ % 4
                act.wait_ge(S["z_mm"], m_ + 1)
                nc.scalar.activation(kqT[:, hp, q, tb * 10:tb * 10 + 10, :],
                                     psum[:, m_ % 4, 0:TBW].rearrange("p (c i) -> p c i", c=10), ACT.Silu).then_inc(S["z_ok"], 1)
            for t in range(TT):
                act.wait_ge(S["v_mm"], t + 1)
                if t >= 2:
                    act.wait_ge(S[f"v_st{t % 2}"], 16 * 4 * (t // 2))
                nc.scalar.activation(dbuf[:, (t % 2) * D:(t % 2 + 1) * D], psum[:, t % 4, :], ACT.Silu).then_inc(S["v_ok"], 1)
            for t in range(TT):
                act.wait_ge(S["gt_mm"], t + 1)
                nc.scalar.activation(ht[:, t, :], psum[:, t % 4, :], ACT.Silu).then_inc(S["gt_ok"], 1)
            act.wait_ge(S["lg_pre"], 1)
            nc.scalar.activation(rt["p"], rt["lg"], ACT.Exp).then_inc(S["p_ok"], 1)
            act.wait_ge(S["ab_pre"], 2)
            nc.scalar.activation(rt["eb"], rt["b"], ACT.Exp, scale=-1.0).then_inc(S["ab_ok"], 1)
            nc.scalar.activation(rt["y"], rt["ax"], ACT.Exp, scale=-1.0).then_inc(S["ab_ok"], 1)
            act.wait_ge(S["cst_in"], 64)
            nc.scalar.activation(rt["ea"], f["alog"], ACT.Exp).then_inc(S["ab_ok"], 1)
            for m_ in range(32):
                act.wait_ge(S["ss_ok"], m_ + 1)
                r_ = rt["nrm"][m_ % 2]
                nc.scalar.activation(r_, r_, ACT.Sqrt).then_inc(S["nrm_ok"], 1)
            act.wait_ge(S["dec_mm"], 4)
            for k_, dst_ in enumerate((Gam, bDC, GamC[:, 0], GamC[:, 1])):
                nc.scalar.activation(dst_, psum[:, k_, 0:NC * SG].rearrange("p (c n) -> p c n", c=NC), ACT.Exp)\
                    .then_inc(S["dec_ok"], 1)
            def stage_kq(i, q):
                nc.scalar.activation(kqc[q].rearrange("p h (q i) -> p h q i", q=2), kqT[:, :, :, bass.ds(i * 2 + q, 1), :].rearrange("p h q c i -> p h q (c i)"),
                                     ACT.Copy).then_inc(S["dkq_ok"], 1)
            with act.Fori(0, NC // 2) as i:
                for q in range(2):
                    act.wait_ge(S["dw_mm"], i * 2 + (q + 1))
                    stage_kq(i, q)
                    act.wait_ge(S["d_mm"], i * 2 + (q + 1))
                    act.wait_ge(S["at_ok"], i * 2 + (q + 2))
                    nc.scalar.activation(ex, psum[:, 2 * q, 0:256].rearrange("p (g i) -> p g i", g=SG), ACT.Exp).then_inc(S["e_ok"], 1)
            act.wait_ge(S["bdz"], 2)
            with act.Fori(0, NC // 2) as i:
                for q in range(2):
                    act.wait_ge(S["o_mm1"], i * 2 + (q + 1))
                    for h2 in range(2):
                        nc.scalar.activation(kqb[q][64 * h2:64 * h2 + 64, :, :, 32 * h2:32 * h2 + 32],
                                             kqT[64 * h2:64 * h2 + 64, :, :, bass.ds(i * 2 + q, 1), :].rearrange("p h q c i -> p h q (c i)"),
                                             ACT.Copy).then_inc(S["kqs"], 1)
                    for hh in range(2):
                        act.wait_ge(S[f"o_mm{hh}"], i * 2 + (q + 2))
                        act.wait_ge(S[f"up_ok{hh}"], i * 2 + (q + 1))
                        nc.scalar.activation(usb[:, hh * 256:(hh + 1) * 256], psum[:, 4 * hh + 2, 0:256], ACT.Copy)\
                            .then_inc(S[f"u_ok{hh}"], 1)
            act.wait_ge(S["cn_a"], 1)
            nc.scalar.activation(cstat, cstat, ACT.Sqrt).then_inc(S["cn_b"], 1)
            for t in range(NT):
                act.wait_ge(S["cT_mm"], t + 1)
                nc.scalar.activation(coreT[:, :, t * 128:(t + 1) * 128], psum[:, t % 2, :].rearrange("p (k n) -> p k n", k=KC), ACT.Copy)\
                    .then_inc(S["cT_ok"], 1)

        @block.tensor
        def _(pe):
            pe.wait_ge(S["consts"], 2)
            for t in range(NT):
                pe.wait_ge(S["ln_h"], t + 1)
                if t >= 2:
                    pe.wait_ge(S["ln_hT"], t - 1)
                for k in range(KC):
                    m = nc.tensor.transpose(psum[:, t % 2, k * TP:(k + 1) * TP], ht[0:TP, t, k * 128:(k + 1) * 128],
                                            ident[0:TP, 0:TP])
                m.then_inc(S["ln_T"], 1)
            pe.wait_ge(S["w1_in"], 64)
            for t in range(NT):
                pe.wait_ge(S["ln_hT"], t + 1)
                if t >= 2:
                    pe.wait_ge(S["P_sb"], t - 1)
                for k in range(KC):
                    m = nc.tensor.matmul(psum[0:TP, 2 + t % 2, :], hT[:, k, t * TP:(t + 1) * TP], w1h[:, k, :],
                                         start=(k == 0), stop=(k == KC - 1))
                m.then_inc(S["P_mm"], 1)
            pe.sem_inc(S["pre_mm"], BODY)
            pe.sem_inc(S["relu_free"], RB)
            n = passes(pe)

            def pre(t0, k, tiles, bodies):
                kk = k % BODY
                if kk % GT == 0:
                    pe.wait_ge(S[f"ea_in{kk // GT}"], bodies + 16 * (k // BODY + 1))
                pe.wait_ge(S["pre_add"], tiles + k + 1)
                return nc.tensor.matmul(psum[0:TP, kk % RB, :],
                                        ea[:, kk // GT, (kk % GT) * TP:(kk % GT + 1) * TP], a["w1e"],
                                        start=True, stop=True)

            def acc(k, tiles, groups):
                g = k // GT
                if k % GT == 0:
                    pe.wait_ge(S["acc_add"], groups + g + 1)
                    pe.wait_ge(S["oh_ok"], groups + g + 1)
                pe.wait_ge(S["pg_free"], tiles + (BODY + k + 1))
                for c in range(KC + 1):
                    lhsT = rl[:, k % RB, c * 128:(c + 1) * 128] if c < KC else a["ones"]
                    m = nc.tensor.matmul(psum[0:128 if c < KC else 1, 5 + g, c * W:(c + 1) * W], lhsT, oh[:, g, k % GT, :],
                                         start=(k % GT == 0 and c == 0), stop=(k % GT == GT - 1 and c == KC),
                                         skip_group_check=True)
                m.then_inc(S["relu_free"], 1)

            pe.wait_ge(S["P_sb"], NT)
            with pe.Fori(0, n + 1) as p:
                for k in range(2):
                    pre(0, k, p * ET, p * (NB * 16)).then_inc(S["pre_mm"], 1)

                def body(i, last):
                    for k in range(BODY):
                        if not (last and k + 2 >= BODY):
                            m = pre(0, k + 2, p * ET + i * BODY, p * (NB * 16) + i * 16)
                            m.then_inc(S["pre_mm"], 1)
                        acc(k, p * ET + i * BODY, p * G + i * 2)

                with pe.Fori(0, NB - 1) as i:
                    body(i, False)
                body(NB - 1, True)

            pe.wait_ge(S["out_d"], 1)
            pe.wait_ge(S["b2_in"], 16)
            for m_ in range(12):
                c_, b_ = m_ // 3, m_ % 3
                lo, hi = N * b_ // 3, N * (b_ + 1) // 3
                if m_ >= 8:
                    pe.wait_ge(S["agg_sb"], m_ - 7)
                for k in range(KC):
                    nc.tensor.matmul(psum[:, m_ % 8, 0:hi - lo], w2[:, k, c_ * 128:(c_ + 1) * 128], accT[:, k, lo:hi],
                                     start=(k == 0), stop=False)
                nc.tensor.matmul(psum[:, m_ % 8, 0:hi - lo], rows[0:1, c_ * 128:(c_ + 1) * 128], accT[0:1, KC, lo:hi],
                                 start=False, stop=True).then_inc(S["agg_mm"], 1)
            pe.wait_ge(S["agg_sb"], 12)
            pe.wait_ge(S["wih_in"], 16)
            pe.wait_ge(S["whh_in"], 16)
            for t in range(NT):
                if t >= 2:
                    pe.wait_ge(S["gate_rd"], 3 * (t - 1))
                q = 4 * (t % 2)
                rows_ = slice(t * TP, (t + 1) * TP)
                for g_ in range(3):
                    for k in range(KC):
                        m = nc.tensor.matmul(psum[0:TP, q + g_, :], aggT[:, k, rows_], wih[:, k, g_ * D:(g_ + 1) * D],
                                             start=(k == 0), stop=(g_ == 2 and k == KC - 1))
                    for k in range(KC):
                        m = nc.tensor.matmul(psum[0:TP, q + g_ + (g_ == 2), :], hT[:, k, rows_], whh[:, k, g_ * D:(g_ + 1) * D],
                                             start=(g_ == 2 and k == 0), stop=(k == KC - 1))
                m.then_inc(S["gate_mm"], 1)
            for t in range(NT):
                pe.wait_ge(S["ln2_h"], t + 1)
                if t >= 2:
                    pe.wait_ge(S["ln2_hT"], t - 1)
                for k in range(KC):
                    m = nc.tensor.transpose(psum[:, t % 2, k * TP:(k + 1) * TP], ht[0:TP, t, k * 128:(k + 1) * 128],
                                            ident[0:TP, 0:TP])
                m.then_inc(S["ln2_T"], 1)
            pe.wait_ge(S["ffnw_in"], 16 * 6)
            pe.wait_ge(S["ln2_hT"], NT)
            pe.wait_ge(S["pad_ok"], 1)
            for m_ in range(32):
                q, hp, tb = m_ // 16, m_ // 4 % 4, m_ % 4
                if m_ >= 4:
                    pe.wait_ge(S["z_ok"], m_ - 3)
                for k in range(KC):
                    m = nc.tensor.matmul(psum[:, m_ % 4, 0:TBW], proj["wq" if q else "wk"][:, k, hp * 128:(hp + 1) * 128],
                                         hT[:, k, tb * TBW:(tb + 1) * TBW], start=(k == 0), stop=(k == KC - 1))
                m.then_inc(S["z_mm"], 1)
            for t in range(TT):
                pe.wait_ge(*((S["z_ok"], 29 + t) if t < 4 else (S["v_ok"], t - 3)))
                for k in range(KC):
                    m = nc.tensor.matmul(psum[:, t % 4, :], hT[:, k, t * 128:(t + 1) * 128], proj["wv"][:, k, :],
                                         start=(k == 0), stop=(k == KC - 1))
                m.then_inc(S["v_mm"], 1)
            pe.wait_ge(S["v_ok"], TT)
            for t in range(NT):
                if t >= 4:
                    pe.wait_ge(S["gt_ok"], t - 3)
                for k in range(KC):
                    m = nc.tensor.matmul(psum[:, t % 4, :], hT[:, k, t * 128:(t + 1) * 128], proj["wg"][:, k, :],
                                         start=(k == 0), stop=(k == KC - 1))
                m.then_inc(S["gt_mm"], 1)
            for t in range(TT):
                for k in range(KC):
                    m = nc.tensor.matmul(psum[:, 4, t * 20:(t + 1) * 20], hT[:, k, t * 128:(t + 1) * 128], wsm[:, k, :],
                                         start=(k == 0), stop=(k == KC - 1), skip_group_check=True)
            m.then_inc(S["sm_mm"], 1)
            pe.wait_ge(S["cst_in"], 64)
            pe.wait_ge(S["gt_ok"], NT)
            for m_ in range(32):
                pe.wait_ge(S["sq_ok"], m_ + 1)
                nc.tensor.matmul(psum[:, 5 + m_ % 2, 0:TBW], f["bd64"], rt["sq"][m_ % 2], start=True, stop=True).then_inc(S["ss_mm"], 1)
            pe.wait_ge(S["kq_ok"], 32)
            for t in range(TT):
                if t >= 2:
                    pe.wait_ge(S["kt_ok"], 2 * (t - 1))
                for hp in range(4):
                    m = nc.tensor.transpose(psum[:, t % 2, hp * 128:(hp + 1) * 128], kqT[:, hp, 0, 4 * t:4 * t + 4, :].rearrange("p c i -> p (c i)"), ident[:, :])
                m.then_inc(S["kT_mm"], 1)
            pe.wait_ge(S["kt_ok"], 2 * TT)
            pe.wait_ge(S["gw_in"], 16)
            for k_, name in enumerate(("leb", "gt", "s0", "s1")):
                nc.tensor.matmul(psum[:, k_, 0:NC * SG], f[name], gw[:, :, 0:SG], start=True, stop=True).then_inc(S["dec_mm"], 1)
            pe.wait_ge(S["dec_ok"], 4)
            pe.sem_inc(S["dw_mm"], 1)
            with pe.Fori(0, NC // 2) as i:
                for q in range(2):
                    pe.wait_ge(S["rg_ok"], i * 4 + (2 * q + 2))
                    pe.wait_ge(S["dkq_ok"], i * 2 + (q + 1))
                    pe.wait_ge(S["at_ok"], i * 2 + (q + 1))
                    nc.tensor.matmul(psum[:, 2 * q, 0:256], f["gt"], rg.rearrange("p g i -> p (g i)"), start=True, stop=True,
                                     skip_group_check=True).then_inc(S["d_mm"], 1)
                    nc.tensor.matmul(psum[:, 2 * q + 1, 0:128], f["bd"], wd.rearrange("p e i -> p (e i)"), start=True, stop=True,
                                     skip_group_check=True)
                    for hd in range(H):
                        hh, h4 = hd // 4, hd % 4
                        s_, h2 = h4 // 2, h4 % 2
                        part = slice(64 * h2, 64 * h2 + 64)
                        m = nc.tensor.matmul(psum[32 * h4:32 * h4 + 32, 4 + h2 + 2 * q, hh * 64:hh * 64 + 64],
                                             kqc[q][part, 2 * hh + s_, 0:32], kqc[q][part, 2 * hh + s_, :],
                                             start=True, stop=True, skip_group_check=True)
                    m.then_inc(S["dw_mm"], 1)
            for hh in range(2):
                pe.sem_inc(S[f"o_mm{hh}"], 2)
            pe.wait_ge(S["bdz"], 2)
            with pe.Fori(0, NC // 2) as i:
                for q in range(2):
                    c = i * 2 + q
                    pe.wait_ge(S["kqs"], c * 2 + 2)
                    for hh in range(2):
                        pe.wait_ge(S[f"s_ok{hh}"], c + 1)
                        for w_ in range(2):
                            for s_ in range(2):
                                m = nc.tensor.matmul(psum[64 * s_:64 * s_ + 64, 4 * hh + w_, 0:256], kqb[q][:, 2 * hh + s_, w_, :],
                                                     state[:, (2 * s_ + hh) * 256:(2 * s_ + hh) * 256 + 256],
                                                     start=True, stop=True, skip_group_check=True)
                            m.then_inc(S[f"ks_mm{hh}"], 1)
                    pe.wait_ge(S[f"ld{q}"], i * LOADS + LOADS)
                    for hh in range(2):
                        pe.wait_ge(S[f"r_ok{hh}"], c + 1)
                        for g_ in range(hh * X, hh * X + X):
                            m = nc.tensor.matmul(psum[:, 4 * hh + 2, g_ % X * 64:(g_ % X + 1) * 64], xbd[q][:, g_, :],
                                                 resid[:, g_ * 64:(g_ + 1) * 64], start=True, stop=True, skip_group_check=True)
                        m.then_inc(S[f"u_mm{hh}"], 1)
                    for hh in range(2):
                        pe.wait_ge(S[f"up_ok{hh}"], c + 1)
                        for s_ in range(2):
                            m = nc.tensor.matmul(psum[:, 4 * hh + s_, 256:512], kbd[q][64 * s_:64 * s_ + 64, hh, :],
                                                 ups[64 * s_:64 * s_ + 64, hh * 256:hh * 256 + 256],
                                                 start=True, stop=True, skip_group_check=True)
                        m.then_inc(S[f"su_mm{hh}"], 1)
                        pe.wait_ge(S[f"u_ok{hh}"], c + 1)
                        pe.wait_ge(S["o_ok"], c * 2 + (hh + 3))
                        for e in range(X):
                            g_ = hh * X + e
                            m = nc.tensor.matmul(psum[:, 4 * hh + 3, 0:64], abd[q][:, g_, :], usb[:, g_ * 64:(g_ + 1) * 64],
                                                 start=(e == 0), stop=(e == X - 1), skip_group_check=True)
                        m.then_inc(S[f"o_mm{hh}"], 1)
            for t in range(TT):
                pe.wait_ge(S["core_ok"], t + 1)
                if t >= 2:
                    pe.wait_ge(S["cT_ok"], t - 1)
                for k in range(KC):
                    m = nc.tensor.transpose(psum[:, t % 2, k * 128:(k + 1) * 128], core[:, t, k * 128:(k + 1) * 128], ident[:, :])
                m.then_inc(S["cT_mm"], 1)
                pe.wait_ge(S["cT_ok"], t + 1)
                if t >= 2:
                    pe.wait_ge(S["out_ok"], t - 1)
                for k in range(KC):
                    m = nc.tensor.matmul(psum[0:TP, 3 + t % 2, :], coreT[:, k, t * TP:(t + 1) * TP], proj["wo"][:, k, :],
                                         start=(k == 0), stop=(k == KC - 1))
                m.then_inc(S["out_mm"], 1)

        @block.vector
        def _(v):
            st = Steps(v, S["dve"])
            v.wait_ge(S["x_in"], 16)
            for t in range(NT):
                st.did(nc.vector.bn_stats(stats[:, t, :], xt[:, t, :]))
            st.settle()
            for t in range(NT):
                st.did(nc.vector.bn_aggr(mv[:, t, :], stats[:, t, :]))
            st.settle()
            nc.vector.tensor_scalar(rstd[:, :], mv[:, :, 1], LN_EPS, None, ALU.add).then_inc(S["ln_mv"], 1)
            v.wait_ge(S["ln_std"], 1)
            st.then(nc.vector.reciprocal(rstd[:, :], rstd[:, :]))
            for t in range(NT):
                nc.vector.tensor_scalar(ht[0:TP, t, :], xt[:, t, :], mv[:, t, 0:1], rstd[:, t:t + 1],
                                        ALU.subtract, ALU.mult).then_inc(S["ln_h"], 1)
            v.wait_ge(S["ids_in"], 32)
            st.then(nc.vector.tensor_copy(dstf, dsti))
            st.then(nc.vector.tensor_scalar(rel, dstf, -1.0, None, ALU.mult))
            nc.vector.tensor_reduce(a["start"], rel.rearrange("p (g t) -> p g t", t=GT), AX.X, ALU.max)\
                .then_inc(S["spans"], 1)
            nc.vector.tensor_reduce(a["high"], dstf.rearrange("p (g t) -> p g t", t=GT), AX.X, ALU.max)\
                .then_inc(S["spans"], 1)
            for t in range(NT):
                v.wait_ge(S["ln_T"], t + 1)
                nc.vector.tensor_copy(hT[:, :, t * TP:(t + 1) * TP],
                                      psum[:, t % 2, 0:KC * TP].rearrange("p (k n) -> p k n", k=KC))\
                    .then_inc(S["ln_hT"], 1)
            v.wait_ge(S["base_ok"], 2)
            st.then(nc.vector.tensor_tensor(a["high"], a["high"], a["base"], ALU.add))
            st.then(nc.vector.tensor_reduce(a["span"], a["high"], AX.X, ALU.max))
            st.then(nc.vector.tensor_copy(npass, a["span"]))
            nc.vector.tensor_scalar(npass, npass, W.bit_length() - 1, None, ALU.logical_shift_right)\
                .then_inc(S["pass_ok"], 1)
            v.wait_ge(S["iota_ok"], 1)
            st.then(nc.vector.tensor_copy(a["iota"], a["iota"].bitcast(I32)))
            st.then(nc.vector.tensor_scalar(a["start"], a["base"], -1.0, None, ALU.mult))
            for t in range(NT):
                v.wait_ge(S["P_mm"], t + 1)
                if t >= 2:
                    v.wait_ge(S[f"P_out{t % 2}"], 16 * (t // 2))
                nc.vector.tensor_tensor(pw[:, t % 2, :], psum[0:TP, 2 + t % 2, :], a["b1"], ALU.add)\
                    .then_inc(S["P_sb"], 1)
            v.sem_inc(S["pre_add"], RB)
            v.sem_inc(S["acc_add"], 2)
            v.wait_ge(S["consts"], 3)
            n = passes(v)
            base_n = st.n
            with v.Fori(0, n + 1) as p:
                PER_PASS = 4
                c0 = base_n + p * PER_PASS

                def chain(ins, k):
                    ins.then_inc(S["dve"], 1)
                    v.wait_ge(S["dve"], c0 + k)

                startb = a["start"][:, :, None].to_broadcast([TP, G, GT])
                chain(nc.vector.tensor_tensor(rel.rearrange("p (g t) -> p g t", t=GT),
                                              dstf.rearrange("p (g t) -> p g t", t=GT), startb, ALU.subtract), 1)
                chain(nc.vector.tensor_copy(starti[0:1, :], a["start"][0:1, :]), 2)
                chain(nc.vector.tensor_scalar(a["start"], a["start"], float(W), float(N), ALU.add, ALU.min), 3)
                chain(nc.vector.tensor_copy(a["span"], a["span"]), 4)

                def add(i, k):
                    v.wait_ge(S["pre_mm"], p * ET + i * BODY + (BODY + k + 1))
                    v.wait_ge(gath[k], p * (NB * 16) + i * 16 + 16)
                    nc.vector.tensor_tensor(pg[:, k, :], psum[0:TP, k % RB, :], pg[:, k, :], ALU.add)\
                        .then_inc(S["pre_add"], 1)

                def onehot(i, g):
                    nc.vector.tensor_tensor(
                        oh[:, g, :, :],
                        a["iota"][:, None, :].to_broadcast([TP, GT, W]),
                        rel[:, bass.ds(i * BODY + g * GT, GT)][:, :, None].to_broadcast([TP, GT, W]),
                        ALU.is_equal).then_inc(S["oh_ok"], 1)

                def acc_add(i, g):
                    s = v.value_load(starti[0:1, bass.ds(i * 2 + g, 1)], min_val=0, max_val=N)
                    v.wait_ge(S["relu_free"], p * ET + i * BODY + (RB + GT * (g + 1)))
                    v.wait_ge(S["acc_add"], p * G + i * 2 + (g + 2))
                    nc.vector.tensor_tensor(accT[:, 0:KC, bass.ds(s, W)], accT[:, 0:KC, bass.ds(s, W)],
                                            psum[:, 5 + g, 0:KC * W].rearrange("p (c w) -> p c w", w=W), ALU.add)
                    nc.vector.tensor_tensor(accT[0:1, KC, bass.ds(s, W)], accT[0:1, KC, bass.ds(s, W)],
                                            psum[0:1, 5 + g, KC * W:(KC + 1) * W], ALU.add).then_inc(S["acc_add"], 1)

                def body(i, first):
                    for k in range(GT):
                        add(i, k)
                    if not first:
                        acc_add(i - 1, 1)
                    onehot(i, 1)
                    for k in range(GT, BODY):
                        add(i, k)
                    acc_add(i, 0)

                onehot(0, 0)
                body(0, True)
                with v.Fori(1, NB) as i:
                    onehot(i, 0)
                    body(i, False)
                acc_add(NB - 1, 1)
            st = Steps(v, S["dve2"])
            v.wait_ge(S["acc_add"], n * G + (G + 2))
            v.sem_inc(S["out_d"], 1)
            v.wait_ge(S["vec_in"], 16 * 6)
            bias_rz, bias_in, bias_hn = vec[:, 0:2 * D], vec[:, 2 * D:3 * D], vec[:, 5 * D:6 * D]
            gamma, beta, rmean, rvar = (vec[:, (6 + k) * D:(7 + k) * D] for k in range(4))
            nc.vector.tensor_scalar(rvar, rvar, BN_EPS, None, ALU.add).then_inc(S["bn_pre"], 1)
            st.then(nc.vector.tensor_tensor(bias_rz, bias_rz, vec[:, 3 * D:5 * D], ALU.add))
            v.wait_ge(S["bn_std"], 1)
            st.then(nc.vector.reciprocal(rvar, rvar))
            st.then(nc.vector.tensor_tensor(gamma, gamma, rvar, ALU.mult))
            st.then(nc.vector.tensor_tensor(rmean, rmean, gamma, ALU.mult))
            st.then(nc.vector.tensor_tensor(beta, beta, rmean, ALU.subtract))
            for t in range(NT):
                q = 4 * (t % 2)
                new, hn, nn, rz = bo["new"], bo["hn"], bo["in"], bo["rz"]
                v.wait_ge(S["gate_mm"], t + 1)
                nc.vector.tensor_tensor(rz.rearrange("p (g n) -> p g n", g=2), psum[0:TP, q:q + 2, :],
                                        bias_rz.rearrange("p (g n) -> p g n", g=2), ALU.add).then_inc(S["rz_pre"], 1)
                nc.vector.tensor_tensor(hn, psum[0:TP, q + 3, :], bias_hn, ALU.add).then_inc(S["gate_rd"], 1)
                nc.vector.tensor_tensor(nn, psum[0:TP, q + 2, :], bias_in, ALU.add).then_inc(S["gate_rd"], 1)
                v.wait_ge(S["rz"], t + 1)
                v.wait_ge(S["gate_rd"], 3 * t + 2)
                nc.vector.tensor_tensor(hn, hn, rz[:, 0:D], ALU.mult).then_inc(S["gate_rd"], 1)
                v.wait_ge(S["gate_rd"], 3 * t + 3)
                nc.vector.tensor_tensor(nn, nn, hn, ALU.add).then_inc(S["n_pre"], 1)
                v.wait_ge(S["n_ok"], t + 1)
                st.then(nc.vector.tensor_tensor(new, ht[0:TP, t, :], nn, ALU.subtract))
                st.then(nc.vector.tensor_tensor(new, new, rz[:, D:2 * D], ALU.mult))
                st.then(nc.vector.tensor_tensor(new, new, nn, ALU.add))
                st.then(nc.vector.tensor_tensor(new, new, gamma, ALU.mult))
                st.then(nc.vector.tensor_tensor(new, new, beta, ALU.add))
                st.then(nc.vector.tensor_tensor(new, new, ht[0:TP, t, :], ALU.add))
                nc.vector.tensor_tensor(xt[:, t, :], xt[:, t, :], new, ALU.add).then_inc(S["x1_ok"], 1)
                v.wait_ge(S["x1_ok"], t + 1)
                st.then(nc.vector.bn_stats(stats[:, t, :], xt[:, t, :]))
                st.then(nc.vector.bn_aggr(mv[:, t, :], stats[:, t, :]))
            nc.vector.tensor_scalar(rstd[:, :], mv[:, :, 1], LN_EPS, None, ALU.add).then_inc(S["ln2_mv"], 1)
            v.wait_ge(S["ln2_std"], 1)
            st.then(nc.vector.reciprocal(rstd[:, :], rstd[:, :]))
            for t in range(NT):
                nc.vector.tensor_scalar(ht[0:TP, t, :], xt[:, t, :], mv[:, t, 0:1], rstd[:, t:t + 1],
                                        ALU.subtract, ALU.mult).then_inc(S["ln2_h"], 1)
            for t in range(NT):
                v.wait_ge(S["ln2_T"], t + 1)
                nc.vector.tensor_copy(hT[:, :, t * TP:(t + 1) * TP],
                                      psum[:, t % 2, 0:KC * TP].rearrange("p (k n) -> p k n", k=KC))\
                    .then_inc(S["ln2_hT"], 1)
            v.wait_ge(S["sm_mm"], 1)
            v.wait_ge(S["cst_in"], 64)
            sm = psum[:, 4, 0:TT * 20].rearrange("p (t n) -> p t n", t=TT)

            def over(x, *shape):
                return x.to_broadcast([128, *shape])

            st.then(nc.vector.tensor_reduce(rt["mx"], sm[:, :, 16:20], AX.X, ALU.max))
            nc.vector.tensor_tensor(rt["lg"], sm[:, :, 16:20], over(rt["mx"][:, :, None], TT, X), ALU.subtract).then_inc(S["lg_pre"], 1)
            st.then(nc.vector.tensor_tensor(rt["a"], sm[:, :, 0:8], over(f["dtb"][:, None, :], TT, H), ALU.add))
            st.then(nc.vector.tensor_scalar(rt["t1"], rt["a"], -1.0, None, ALU.mult))
            nc.vector.tensor_tensor(rt["ax"], rt["a"], rt["t1"], ALU.max).then_inc(S["ab_pre"], 1)
            nc.vector.tensor_copy(rt["b"], sm[:, :, 8:16]).then_inc(S["ab_pre"], 1)
            v.wait_ge(S["p_ok"], 1)
            p_ = rt["p"]
            st.then(nc.vector.tensor_reduce(rt["mx"], p_, AX.X, ALU.add))
            st.then(nc.vector.reciprocal(rt["mx"], rt["mx"]))
            st.then(nc.vector.tensor_tensor(p_, p_, over(rt["mx"][:, :, None], TT, X), ALU.mult))
            other, own = over(p_[:, :, None, :], TT, X, X), over(p_[:, :, :, None], TT, X, X)
            st.did(nc.vector.tensor_tensor(rt["gt"], other, own, ALU.is_gt))
            st.then(nc.vector.tensor_tensor(rt["eq"], other, own, ALU.is_equal))
            st.then(nc.vector.tensor_tensor(rt["eq"], rt["eq"], over(f["lt4"].rearrange("p (a b) -> p a b", a=X)[:, None], TT, X, X), ALU.mult))
            st.then(nc.vector.tensor_tensor(rt["gt"], rt["gt"], rt["eq"], ALU.add))
            st.then(nc.vector.tensor_reduce(rt["lg"], rt["gt"], AX.X, ALU.add))
            st.then(nc.vector.tensor_scalar(rt["lg"], rt["lg"], 2.0, None, ALU.is_lt))
            st.then(nc.vector.tensor_tensor(p_, p_, rt["lg"], ALU.mult))
            st.then(nc.vector.tensor_reduce(rt["mx"], p_, AX.X, ALU.add))
            st.then(nc.vector.reciprocal(rt["mx"], rt["mx"]))
            st.then(nc.vector.tensor_tensor(p_, p_, over(rt["mx"][:, :, None], TT, X), ALU.mult))
            st.then(nc.vector.tensor_scalar(rt["lg"], p_, 0.0, None, ALU.is_gt))
            v.wait_ge(S["ab_ok"], 3)
            st.then(nc.vector.tensor_scalar(rt["eb"], rt["eb"], 1.0, None, ALU.add))
            st.then(nc.vector.reciprocal(rt["eb"], rt["eb"]))
            st.then(nc.vector.tensor_scalar(rt["t1"], rt["y"], 2.0, None, ALU.add))
            st.then(nc.vector.reciprocal(rt["t1"], rt["t1"]))
            st.then(nc.vector.tensor_tensor(rt["y"], rt["y"], rt["t1"], ALU.mult))
            st.then(nc.vector.tensor_tensor(rt["t1"], rt["y"], rt["y"], ALU.mult))
            st.then(nc.vector.tensor_scalar(rt["ax"], rt["t1"], 2.0 / (2 * LOG_TERMS - 1), None, ALU.mult))
            for k in range(LOG_TERMS - 2, -1, -1):
                st.then(nc.vector.tensor_scalar(rt["ax"], rt["ax"], 2.0 / (2 * k + 1), None, ALU.add))
                st.then(nc.vector.tensor_tensor(rt["ax"], rt["ax"], rt["t1"] if k else rt["y"], ALU.mult))
            st.then(nc.vector.tensor_scalar(rt["a"], rt["a"], 0.0, None, ALU.max))
            st.then(nc.vector.tensor_tensor(rt["a"], rt["a"], rt["ax"], ALU.add))
            st.then(nc.vector.tensor_tensor(rt["a"], rt["a"], over(rt["ea"][:, None, :], TT, H), ALU.mult))
            st.then(nc.vector.tensor_scalar(rt["a"], rt["a"], -1.0, G_FLOOR, ALU.mult, ALU.max))
            gwt = hTf[:, 0:TT * 96].rearrange("p (t h q g e) -> p t h q g e", t=TT, h=4, q=3, g=2)
            v.wait_ge(S["gt_mm"], NT)
            for h in range(4):
                m4 = over(rt["lg"][:, :, None, :], TT, 2, X)
                for q, val in ((0, rt["a"]), (1, rt["eb"])):
                    nc.vector.tensor_tensor(gwt[:, :, h, q, :, :], over(val[:, :, 2 * h:2 * h + 2][:, :, :, None], TT, 2, X),
                                            m4, ALU.mult).then_inc(S["gw_ok"], 1)
                nc.vector.tensor_copy(gwt[:, :, h, 2, :, :], over(p_[:, :, None, :], TT, 2, X)).then_inc(S["gw_ok"], 1)
            def unit(m_):
                q, hp, tb = m_ // 16, m_ // 4 % 4, m_ % 4
                return kqT[:, hp, q, tb * 10:tb * 10 + 10, :]

            def as_unit(x):
                return x.rearrange("p (c i) -> p c i", c=10)

            def squares(m_):
                nc.vector.tensor_tensor(as_unit(rt["sq"][m_ % 2]), unit(m_), unit(m_), ALU.mult).then_inc(S["sq_ok"], 1)

            v.wait_ge(S["z_ok"], 32)
            squares(0)
            squares(1)
            for m_ in range(32):
                v.wait_ge(S["ss_mm"], m_ + 1)
                nc.vector.tensor_scalar(rt["nrm"][m_ % 2], psum[:, 5 + m_ % 2, 0:TBW], 1e-6, 1.0 if m_ < 16 else float(DK),
                                        ALU.add, ALU.mult).then_inc(S["ss_ok"], 1)
                if m_ + 2 < 32:
                    squares(m_ + 2)
                v.wait_ge(S["nrm_ok"], m_ + 1)
                st.then(nc.vector.reciprocal(rt["nrm"][m_ % 2], rt["nrm"][m_ % 2]))
                nc.vector.tensor_tensor(unit(m_), unit(m_), as_unit(rt["nrm"][m_ % 2]), ALU.mult).then_inc(S["kq_ok"], 1)
            for k in range(2):
                st.then(nc.vector.memset(ktb[k], 0.0))
            for t in range(TT):
                v.wait_ge(S["kT_mm"], t + 1)
                if t >= 2:
                    v.wait_ge(S[f"kt_st{t % 2}"], 16 * 4 * (t // 2))
                kt = ktb[t % 2].rearrange("p (s a g b k) -> p s a g b k", s=2, a=2, g=2, b=2)
                src = psum[:, t % 2, :].rearrange("p (g s a k) -> p s a g k", g=2, s=2, a=2)
                for h2 in range(2):
                    nc.vector.tensor_copy(kt[:, :, h2, :, h2, :], src[:, :, h2, :, :]).then_inc(S["kt_ok"], 1)
            for q in range(2):
                v.wait_ge(S[f"kt_st{q}"], 16 * 4 * TT // 2)
            v.wait_ge(S["dec_ok"], 4)
            st.did(nc.vector.tensor_tensor(bDC, bDC, gw[:, :, 8:16], ALU.mult))
            st.then(nc.vector.tensor_tensor(wGam, Gam, gw[:, :, 16:24], ALU.mult))
            v.sem_inc(S["at_ok"], 2)
            for q in range(2):
                v.sem_inc(S[f"lt_st{q}"], 16)
                v.sem_inc(S[f"at_st{q}"], 16)
            base2 = st.n
            with v.Fori(0, NC // 2) as i:
                for q in range(2):
                    c = i * 2 + q
                    c0 = base2 + i * 6 + 3 * q

                    def chain(ins, k):
                        ins.then_inc(S["dve2"], 1)
                        v.wait_ge(S["dve2"], c0 + k)

                    v.wait_ge(S["dw_mm"], c + 2)
                    for h4 in range(4):
                        r4 = slice(32 * h4, 32 * h4 + 32)
                        ins = nc.vector.tensor_tensor(kkm[r4], psum[r4, 4 + h4 % 2 + 2 * q, 0:128].rearrange("p (h q i) -> p h q i", h=2, q=2),
                                                      f["mask2"][r4].rearrange("p (q i) -> p q i", q=2)[:, None].to_broadcast([32, 2, 2, C]),
                                                      ALU.mult)
                    chain(ins, 1)
                    v.wait_ge(S["e_ok"], c + 1)
                    bch = gw[:, bass.ds(c, 1), 8:16].rearrange("p c n -> p (c n)")
                    chain(nc.vector.tensor_tensor(ex, ex, bch[:, :, None].to_broadcast([128, SG, C]), ALU.mult), 2)

                    def four(x):
                        return x.rearrange("p (h e) i -> p h e i", h=2)

                    v.wait_ge(S[f"lt_st{q}"], i * 16 + 16)
                    nc.vector.tensor_tensor(four(lt[q]), four(ex), kkm[:, :, 0, :][:, :, None, :].to_broadcast([128, 2, X, C]),
                                            ALU.mult).then_inc(S["lt_ok"], 1)
                    chain(nc.vector.tensor_tensor(four(at1), four(ex), kkm[:, :, 1, :][:, :, None, :].to_broadcast([128, 2, X, C]),
                                                  ALU.mult), 3)
                    v.wait_ge(S[f"at_st{q}"], i * 16 + 16)
                    nc.vector.tensor_tensor(four(at[q]), four(at1),
                                            psum[:, 2 * q + 1, 0:128].rearrange("p (e i) -> p e i", e=X)[:, None].to_broadcast([128, 2, X, C]),
                                            ALU.mult).then_inc(S["at_ok"], 1)
            base3 = base2 + 3 * NC
            per = 2 + 2 * (C - 1) - 1
            with v.Fori(0, 2) as hf:
                c0 = base3 + hf * per
                k_ = 0
                v.wait_ge(S["l_in"], hf * 16 + 16)
                v.wait_ge(S["xs_go"], hf + 1)
                for ins in (nc.vector.memset(XTs, 0.0), None):
                    if ins is None:
                        ins = nc.vector.memset(XTs.rearrange("p q n i -> p q (n i)")[:, :, ::C + 1], 1.0)
                    k_ += 1
                    ins.then_inc(S["dve2"], 1)
                    v.wait_ge(S["dve2"], c0 + k_)
                for r in range(1, C):
                    pr = Prod[:, 0:QG * r * r].rearrange("p (q n j) -> p q n j", q=QG, n=r)
                    nc.vector.tensor_tensor(pr, Lsys[:, :, 0:r, r][:, :, None, :].to_broadcast([128, QG, r, r]),
                                            XTs[:, :, 0:r, 0:r], ALU.mult).then_inc(S["dve2"], 1)
                    k_ += 1
                    v.wait_ge(S["dve2"], c0 + k_)
                    ins = nc.vector.tensor_reduce(XTs[:, :, 0:r, r], pr, AX.X, ALU.add)
                    if r < C - 1:
                        k_ += 1
                        ins.then_inc(S["dve2"], 1)
                        v.wait_ge(S["dve2"], c0 + k_)
                    else:
                        ins.then_inc(S["x_ok"], 1)
                assert k_ == per, (k_, per)
            v.wait_ge(S["bdz"], 2)
            for hh in range(2):
                v.sem_inc(S[f"s_ok{hh}"], 1)
            v.sem_inc(S["o_ok"], 4)
            for q in range(2):
                v.sem_inc(S[f"o_st{q}"], 64)
            base4 = base3 + 2 * per
            with v.Fori(0, NC // 2) as i:
                for q in range(2):
                    c = i * 2 + q
                    c0 = base4 + i * 12 + 6 * q

                    def step(ins):
                        ins.then_inc(S["dve2"], 1)

                    def half(x, hh):
                        return x[:, hh * 256:(hh + 1) * 256].rearrange("p (e v) -> p e v", e=X)

                    def bank(k, hh):
                        return psum[:, 4 * hh + k, 0:256].rearrange("p (e v) -> p e v", e=X)

                    def per_system(x, hh):
                        return x[:, bass.ds(c, 1), hh * X:(hh + 1) * X].rearrange("p c n -> p (c n)")[:, :, None].to_broadcast([128, X, DK])

                    for hh in range(2):
                        v.wait_ge(S[f"ks_mm{hh}"], c * 2 + 1)
                        step(nc.vector.tensor_tensor(half(ksd, hh), bank(0, hh), per_system(Gam, hh), ALU.mult))
                        v.wait_ge(S[f"ld{q}"], i * LOADS + LOADS)
                        v.wait_ge(S["dve2"], c0 + hh + 1)
                        nc.vector.tensor_tensor(half(resid, hh), vch[q][:, hh * DK:(hh + 1) * DK][:, None, :].to_broadcast([128, X, DK]),
                                                half(ksd, hh), ALU.subtract).then_inc(S[f"r_ok{hh}"], 1)
                    for hh in range(2):
                        v.wait_ge(S[f"ks_mm{hh}"], c * 2 + 2)
                        step(nc.vector.tensor_tensor(half(qsd, hh), bank(1, hh), per_system(wGam, hh), ALU.mult))
                    for hh in range(2):
                        v.wait_ge(S[f"u_mm{hh}"], c + 1)
                        nc.vector.tensor_tensor(half(ups, hh), bank(2, hh), per_system(bDC, hh), ALU.mult).then_inc(S[f"up_ok{hh}"], 1)
                    v.wait_ge(S["dve2"], c0 + 4)
                    step(nc.vector.tensor_reduce(qsr[:, 0:64], half(qsd, 0).rearrange("p e v -> p v e"), AX.X, ALU.add))
                    for hh in range(2):
                        v.wait_ge(S[f"su_mm{hh}"], c + 1)
                        v.wait_ge(S[f"sd_ok{hh}"], c + 1)
                        nc.vector.tensor_tensor(state4[:, :, hh].rearrange("p s e v -> p s (e v)"), sdec4[:, :, hh].rearrange("p s e v -> p s (e v)"),
                                                psum[:, 4 * hh:4 * hh + 2, 256:512], ALU.add).then_inc(S[f"s_ok{hh}"], 1)
                        if hh == 0:
                            step(nc.vector.tensor_reduce(qsr[:, 64:128], half(qsd, 1).rearrange("p e v -> p v e"), AX.X, ALU.add))
                        v.wait_ge(S[f"o_mm{hh}"], c + 3)
                        v.wait_ge(S[f"o_st{q}"], i * 64 + 64)
                        v.wait_ge(S["dve2"], c0 + 6)
                        nc.vector.tensor_tensor(osb[q][:, hh * 64:(hh + 1) * 64], psum[:, 4 * hh + 3, 0:64], qsr[:, hh * 64:(hh + 1) * 64],
                                                ALU.add).then_inc(S["o_ok"], 1)
            st.n = base4 + 6 * NC
            v.wait_ge(S["core_in"], 16 * TT)
            for t in range(TT):
                st.then(nc.vector.tensor_tensor(sqb, core[:, t, :], core[:, t, :], ALU.mult))
                st.then(nc.vector.tensor_reduce(cstat[:, t, :], sqb.rearrange("p (h v) -> p h v", h=H), AX.X, ALU.add))
            nc.vector.tensor_scalar(cstat, cstat, 1.0 / DK, 1e-5, ALU.mult, ALU.add).then_inc(S["cn_a"], 1)
            v.wait_ge(S["cn_b"], 1)
            st.then(nc.vector.reciprocal(cstat, cstat))
            for t in range(TT):
                ct = core[:, t, :].rearrange("p (h v) -> p h v", h=H)
                st.then(nc.vector.tensor_tensor(ct, ct, cstat[:, t, :][:, :, None].to_broadcast([128, H, DK]), ALU.mult))
                st.then(nc.vector.tensor_tensor(ct, ct, f["onorm"][:, None, :].to_broadcast([128, H, DK]), ALU.mult))
                nc.vector.tensor_tensor(core[:, t, :], core[:, t, :], ht[:, t, :], ALU.mult).then_inc(S["core_ok"], 1)
            for t in range(NT):
                v.wait_ge(S["out_mm"], t + 1)
                nc.vector.tensor_tensor(xt[:, t, :], xt[:, t, :], psum[0:TP, 3 + t % 2, :], ALU.add).then_inc(S["out_ok"], 1)


def _constants():
    p = np.arange(128)
    blk, j = p // C, p % C
    same = blk[:, None] == blk[None, :]
    i = np.arange(C)
    h2 = p // 64
    parts = [
        same & (j[:, None] > j[None, :]),
        same & (j[:, None] <= j[None, :]),
        same,
        blk[:, None] == h2[None, :],
        blk[:, None] == 2 + h2[None, :],
        h2[:, None] == h2[None, :],
        j[:, None] <= i[None, :],
        j[:, None] == i[None, :],
        np.concatenate([-1.0 * (i[None, :] > j[:, None]), i[None, :] >= j[:, None]], 1),
        np.broadcast_to((i[None, :X] < i[:X, None]).reshape(1, X * X), (128, X * X)),
    ]
    return np.ascontiguousarray(np.concatenate([x.astype(np.float32) for x in parts], 1))


def kernel(**inputs):
    import concourse.bacc as _bacc
    from concourse.bass_utils import run_bass_kernel_spmd as _run

    c = np.ascontiguousarray
    get = {k: np.asarray(v) for k, v in inputs.items()}
    w1 = get["L0_gnn_W1"]
    arrays = {
        "x": c(get["x"]),
        "src_t": c(get["src"].reshape(ET, TP).T),
        "dst_t": c(get["dst"].reshape(ET, TP).T),
        "ea_T": c(get["edge_attr_128"].T),
        "w1h_T": c(w1[:, :D].T),
        "w1e_T": c(w1[:, D:].T),
        "b1": c(get["L0_gnn_b1"][None, :]),
        "w2_T": c(get["L0_gnn_W2"].T),
        "b2": c(get["L0_gnn_b2"][None, :]),
        "wih_T": c(get["L0_gnn_W_ih"].T),
        "whh_T": c(get["L0_gnn_W_hh"].T),
    }
    for n in ("b_ih", "b_hh", "gamma", "beta", "run_mean", "run_var"):
        arrays[n] = c(get["L0_gnn_" + n][None, :])
    order = np.array([4 * hh + h4 for h4 in range(4) for hh in range(2)])

    def heads(w, axis):
        shape = list(w.shape)
        shape[axis:axis + 1] = [H, shape[axis] // H]
        return c(np.take(w.reshape(shape), order, axis=axis).reshape(w.shape))

    arrays["wq"], arrays["wk"] = c(get["L0_ffn_Wq"]), c(get["L0_ffn_Wk"])
    arrays["wv"], arrays["wg"] = heads(get["L0_ffn_Wv"], 1), heads(get["L0_ffn_Wg"], 1)
    arrays["wo"] = heads(get["L0_ffn_Wo"], 0)
    arrays["wsm"] = c(np.concatenate([heads(get["L0_ffn_Wa"], 1), heads(get["L0_ffn_Wb"], 1), get["L0_ffn_Wgate"]], 1))
    arrays["alog"], arrays["dtb"] = heads(get["L0_ffn_A_log"], 0)[None, :], heads(get["L0_ffn_dt_bias"], 0)[None, :]
    arrays["onorm"] = c(get["L0_ffn_o_norm_weight"][None, :])
    arrays["cst"] = _constants()
    nc = _bacc.Bacc("TRN2", target_bir_lowering=False, num_devices=1)
    io = {n: nc.dram_tensor(n, v.shape, mybir.dt.from_np(v.dtype), kind="ExternalInput").ap()
          for n, v in arrays.items()}
    io["out"] = nc.dram_tensor("out", (N, D), F32, kind="ExternalOutput").ap()
    build(nc, io)
    r = _run(nc, [arrays], core_ids=[0])
    return r.results[0]["out"]
```

```python
from contextlib import ExitStack

import numpy as np

import concourse.bass as bass
from concourse import mybir

F32 = mybir.dt.float32
I32 = mybir.dt.int32
ALU = mybir.AluOpType
ACT = mybir.ActivationFunctionType
AX = mybir.AxisListType
RMAX = bass.bass_isa.ReduceOp.max

N = 1250
D = 512
KC = D // 128
TP = 125
NT = N // TP
E = 41250
ED = 128
ET = E // TP
GT = 5
G = ET // GT
BODY = 2 * GT
RB = 5
AHEAD = 4
NB = ET // BODY
W = 32
NPAD = N + W
C = 32
NC = 40
NTOK = C * NC
TT = NTOK // 128
H = 8
DK = 64
X = 4
SG = 2 * X
TB = 4
TBW = NTOK // TB
QG = 5
LOG_TERMS = 10
G_FLOOR = -200.0
LN_EPS = 1e-5
BN_EPS = 1e-5


MASKS = (("gt", 128), ("leb", 128), ("bd", 128), ("s0", 128), ("s1", 128), ("bd64", 128), ("le", C), ("eye", C),
         ("mask2", 2 * C), ("lt4", X * X))
MASK_COLS = sum(n for _, n in MASKS)
FIXED = MASK_COLS + 2 * H + DK + KC * 20


class Steps:

    def __init__(self, eng, sem):
        self.eng, self.sem, self.n = eng, sem, 0

    def did(self, ins):
        ins.then_inc(self.sem, 1)
        self.n += 1
        return self.n

    def settle(self):
        self.eng.wait_ge(self.sem, self.n)

    def then(self, ins):
        self.did(ins)
        self.settle()


def build(nc, io):
    with ExitStack() as ctx:
        def sb(name, shape, dt=F32):
            return ctx.enter_context(nc.sbuf_tensor(name, shape, dt))

        def sem(name):
            return ctx.enter_context(nc.semaphore(name))

        psum = ctx.enter_context(nc.psum_tensor("psum", [128, 8, 512], F32))

        ident = sb("ident", [128, 128])
        xt = sb("xt", [TP, NT, D])
        ht = sb("ht", [128, NT, D])
        hT = sb("hT", [128, KC, NTOK])
        accT = sb("accT", [128, KC + 1, NPAD])
        stats = sb("stats", [TP, NT, 6])
        mv = sb("mv", [TP, NT, 2])
        rows = sb("rows", [1, D])
        rstd = sb("rstd", [TP, NT])
        ARENA = 24300
        arena = sb("arena", [128, ARENA])

        def carve(spec):
            out, at = {}, 0
            for name, rows, n in spec:
                out[name] = arena[0:rows, at:at + n]
                at += n
            assert at <= ARENA, at
            return out

        a = carve([("w2", 128, KC * D), ("w1h", 128, KC * D), ("rlx", 128, (BODY - KC) * D), ("w1e", 128, D), ("b1", TP, D),
                   ("ea", 128, 2 * GT * TP), ("pg", TP, BODY * D), ("sums", 128, D), ("fold", 128, W), ("deg", 1, W), ("oh", TP, 2 * GT * W),
                   ("pw", TP, 2 * D), ("rel", TP, ET), ("dstf", TP, ET), ("dsti", TP, ET), ("srci", TP, ET),
                   ("base", TP, G), ("high", TP, G), ("start", TP, G), ("starti", TP, G), ("iota", TP, W),
                   ("ones", TP, 1), ("idx", TP, BODY), ("span", TP, 1), ("npass", TP, 1)])
        w1h = a["w1h"].rearrange("p (k n) -> p k n", k=KC)
        w2 = a["w2"].rearrange("p (k n) -> p k n", k=KC)
        ea = a["ea"].rearrange("p (g n) -> p g n", g=2)
        pg = a["pg"].rearrange("p (s n) -> p s n", s=BODY)
        rl = arena[0:TP, KC * D:(KC + BODY) * D].rearrange("p (s n) -> p s n", s=BODY)
        oh = a["oh"].rearrange("p (g t w) -> p g t w", g=2, t=GT)
        pw = a["pw"].rearrange("p (s n) -> p s n", s=2)
        rel, dstf = a["rel"], a["dstf"]
        dsti, srci, starti, idx, npass = (a[x].bitcast(I32) for x in ("dsti", "srci", "starti", "idx", "npass"))

        bo = carve([("w2", 128, KC * D), ("whh", 128, KC * 3 * D), ("aggT", 128, KC * N), ("rz", TP, 2 * D),
                    ("hn", TP, D), ("in", TP, D), ("new", TP, D), ("gap", 128, 2400), ("wih", 128, KC * 3 * D)])
        wih = bo["wih"].rearrange("p (k n) -> p k n", k=KC)
        whh = bo["whh"].rearrange("p (k n) -> p k n", k=KC)
        aggT = bo["aggT"].rearrange("p (k n) -> p k n", k=KC)
        accf = accT[:, :, :].rearrange("p c n -> p (c n)")
        vec = accf[0:TP, 0:10 * D]

        f = carve([("kqT", 128, 4 * NC * 2 * C), ("wq", 128, KC * D), ("wv", 128, KC * D), ("wg", 128, KC * D),
                   ("wk", 128, KC * D), ("wo", 128, KC * D), ("dbuf", 128, 2720)])
        fixed = sb("fixed", [128, FIXED])
        at_ = 0
        for name, n in (*MASKS, ("alog", H), ("dtb", H), ("onorm", DK), ("wsm", KC * 20)):
            f[name] = fixed[:, at_:at_ + n]
            at_ += n
        gate = hT[:, :, :]
        kq = f["kqT"].rearrange("p (q t n) -> p q t n", q=2, t=TT)
        kqT = f["kqT"].rearrange("p (q c h i) -> p q c h i", q=2, c=NC, h=4)
        proj = {n: f[n].rearrange("p (k n) -> p k n", k=KC) for n in ("wq", "wk", "wv", "wg", "wo")}
        wsm = f["wsm"].rearrange("p (k n) -> p k n", k=KC)
        dbuf = f["dbuf"]
        wreg = arena[:, 4 * NC * 2 * C:4 * NC * 2 * C + 8192]
        gw = wreg[:, 0:NC * 24].rearrange("p (c n) -> p c n", c=NC)
        dec = wreg[:, 6144:6144 + 1600]
        Gam, bDC, wGam = (dec[:, k * 320:(k + 1) * 320].rearrange("p (c n) -> p c n", c=NC) for k in range(3))
        GamC = dec[:, 960:1600].rearrange("p (s c n) -> p s c n", s=2, c=NC)
        htf = ht[:, :, :].rearrange("p t n -> p (t n)")
        systems = [x[:, 0:QG * C * C].rearrange("p (q n i) -> p q n i", q=QG, n=C) for x in (accf, htf)]
        Prod = dbuf[:, 1024:1024 + QG * C * C // 4]

        KV_dram = nc.dram_tensor("KV_scratch", [NC, 128, 384], F32, kind="Internal").ap()
        GW_dram = nc.dram_tensor("GW_scratch", [NC, 128, 24], F32, kind="Internal").ap()
        L_dram = nc.dram_tensor("L_scratch", [NC * SG * 4, C * C], F32, kind="Internal").ap()
        X_dram = nc.dram_tensor("X_scratch", [NC * SG * 4, C * C], F32, kind="Internal").ap()
        A_dram = nc.dram_tensor("A_scratch", [NC, 128, SG * C], F32, kind="Internal").ap()
        O_dram = nc.dram_tensor("O_scratch", [NC, 128, 128], F32, kind="Internal").ap()
        P_dram = nc.dram_tensor("P_scratch", [N, D], F32, kind="Internal").ap()

        def take(base, at, n):
            return base[:, at:at + n]

        rg = [x.rearrange("p (g i) -> p g i", g=SG) for x in (take(dbuf, 0, 256), take(accf, 5120, 256))]
        wd = [x.rearrange("p (e i) -> p e i", e=X) for x in (take(dbuf, 256, 128), take(accf, 5376, 128))]
        ex = [x.rearrange("p (g i) -> p g i", g=SG) for x in (take(dbuf, 384, 256), take(accf, 5504, 256))]
        kkm = take(dbuf, 640, 128).rearrange("p (h q i) -> p h q i", h=2, q=2)
        at1 = take(dbuf, 768, 256).rearrange("p (g i) -> p g i", g=SG)
        kqc = [take(dbuf, 1024 + 256 * q, 256).rearrange("p (h n) -> p h n", h=4) for q in range(2)]
        lt = [take(dbuf, 1536 + 256 * q, 256).rearrange("p (g i) -> p g i", g=SG) for q in range(2)]
        at = [take(dbuf, 2048 + 256 * q, 256).rearrange("p (g i) -> p g i", g=SG) for q in range(2)]
        xbd = [take(accf, 1024 * q, 1024).rearrange("p (g i) -> p g i", g=SG) for q in range(2)]
        abd = [take(accf, 2048 + 1024 * q, 1024).rearrange("p (g i) -> p g i", g=SG) for q in range(2)]
        state = take(accf, 4096, 1024)
        sdec = take(accf, 5120, 1024)
        state4, sdec4 = (x.rearrange("p (s h e v) -> p s h e v", s=2, h=2, e=X) for x in (state, sdec))
        kvc = [take(wreg, 960 + 384 * q, 384) for q in range(2)]
        kbd = [kvc[q][:, 0:256].rearrange("p (h n) -> p h n", h=2) for q in range(2)]
        vch = [kvc[q][:, 256:384] for q in range(2)]
        kqb = [take(wreg, 1728 + 512 * q, 512).rearrange("p (h q n) -> p h q n", h=4, q=2) for q in range(2)]
        resid, ksd, usb, ups, qsd = (take(wreg, 2752 + 512 * k, 512) for k in range(5))
        osb = [take(wreg, 5312 + 128 * q, 128) for q in range(2)]
        qsr = take(wreg, 5568, 128)
        core = htf.rearrange("p (t n) -> p t n", t=TT)
        sqb = wreg[:, 0:512]
        cstat = wreg[:, 512:592].rearrange("p (t h) -> p t h", t=TT)
        coreT = accf[:, 0:KC * NTOK].rearrange("p (k n) -> p k n", k=KC)

        rt, at_ = {}, 2048
        for name, shape in (("mx", [TT]), ("lg", [TT, X]), ("p", [TT, X]), ("gt", [TT, X, X]), ("eq", [TT, X, X])):
            n = int(np.prod(shape))
            v_ = dbuf[:, at_:at_ + n]
            rt[name] = v_ if len(shape) == 1 else v_.rearrange("p (t e) -> p t e", t=TT) if len(shape) == 2 else \
                v_.rearrange("p (t e g) -> p t e g", t=TT, e=X)
            at_ += n
        small = sb("small", [128, 5 * TT * H + H])
        for k, name in enumerate(("a", "b", "ax", "eb", "y")):
            rt[name] = small[:, k * 80:(k + 1) * 80].rearrange("p (t h) -> p t h", t=TT)
        rt["ea"] = small[:, 400:408]
        rt["t1"] = sb("t1", [128, TT, H])[:, :, :]
        sq = [accf[:, k * D:(k + 1) * D] for k in range(2)]
        ktb = [accf[:, 1024 + 1024 * k:2048 + 1024 * k] for k in range(2)]
        gwt = accf[:, 3072:3072 + TT * 96].rearrange("p (t h q g e) -> p t h q g e", t=TT, h=4, q=3, g=2)
        norms = accf[:, 4032:4032 + 2 * TT * H].rearrange("p (q t h) -> p q t h", q=2, t=TT)

        S = {n: sem(n) for n in (
            *(f"tok_in{k}" for k in range(NT // 2)), "w1_in", "ids_in", "consts", "dve", "act", "pool", "ln_mv", "ln_std", "ln_h", "ln_T", "ln_hT",
            "P_mm", "P_sb", "P_out0", "P_out1", "spans", "base_ok", "pass_ok", 
            "ea_in0", "ea_in1", "pre_mm", "pre_add", "relu_free", "oh_ok", "sums_ok", "fold_mm", "deg_ok", "acc_add",
            "pg_free", "idx_ok", "out_d", "iota_ok", "gather_go", "b2_in", "wih_in", "whh_in", "vec_in",
            "agg_mm", "agg_sb", "gate_mm", "gate_rd", "rz_pre", "rz", "n_pre", "n_ok", "x1_ok", "ln2_mv", "ln2_std", "ln2_h", "ln2_T",
            "ln2_hT", "wsm_in", "wkq_in", "wvg_in", "cst_in", "z_mm", "z_ok", "ss_ok", "nrm_ok", "kq_ok", "kqT_mm", "kqT_ok", "kt_ok", "ktz", "kt_st0", "kt_st1",
            "sm_mm", "lg_pre", "p_ok", "ab_pre", "ab_ok", "gw_ok", "gw_st", "gw_in", "vg_mm", "v_ok", "v_st0", "v_st1", "gt_ok", "gn_ok",
            "dec_mm", "dec_ok", "rg_ok", "dkq_ok", "dw_mm", "d_mm", "e_ok", "lt_ok", "at_ok", "lt_st0", "lt_st1", "at_st0", "at_st1",
            "l_in0", "l_in1", "x_ok", "x_st", "x_in0", "x_in1", "kv_in0", "kv_in1", "a_in0", "a_in1", "bdz", "kqs", *(f"{x}{hh}" for x in ("ks_mm", "r_ok", "u_mm", "u_ok", "up_ok", "su_mm", "sd_ok", "s_ok", "o_mm") for hh in range(2)),
            "o_ok", "o_st0", "o_st1", "core_in", "core_last", "cn_a", "cn_b", "core_ok", "cT_mm", "cT_ok", "out_mm", "out_ok", "out_st0", "pad_ok", "dve2", "bn_std", "bn_pre")}
        gath = [sem(f"gathered{k}") for k in range(BODY)]
        block = ctx.enter_context(nc.Block())

        transposing = [(q, t) for q in (1, 0) for t in range(TT)]

        def passes(eng):
            eng.wait_ge(S["pass_ok"], 1)
            return eng.value_load(npass[0:1, 0:1], min_val=0, max_val=(N + W - 1) // W)

        @block.sync
        def _(sp):
            for t in range(0, NT, 2):
                sp.dma_start(xt[:, t:t + 2, :], io["x"][t * TP:(t + 2) * TP, :].rearrange("(t p) n -> p t n", p=TP)).then_inc(S[f"tok_in{t // 2}"], 16)
            sp.dma_start(dsti, io["dst_t"]).then_inc(S["ids_in"], 16)
            sp.dma_start(srci, io["src_t"]).then_inc(S["ids_in"], 16)
            sp.dma_start(w1h, io["w1h_T"].rearrange("(k p) n -> p k n", p=128)).then_inc(S["w1_in"], 16)
            sp.dma_start(a["w1e"], io["w1e_T"]).then_inc(S["w1_in"], 16)
            sp.dma_start(a["b1"], io["b1"].to_broadcast([TP, D])).then_inc(S["w1_in"], 16)
            sp.dma_start(w2, io["w2_T"].rearrange("(k p) n -> p k n", p=128)).then_inc(S["w1_in"], 16)
            for t in range(NT):
                sp.wait_ge(S["P_sb"], t + 1)
                sp.dma_start(P_dram[t * TP:(t + 1) * TP, :], pw[:, t % 2, :]).then_inc(S[f"P_out{t % 2}"], 16)
            n = passes(sp)
            with sp.Fori(0, n + 1) as p:
                with sp.Fori(0, NB) as i:
                    for h in range(2):
                        sp.wait_ge(S["pre_mm"], p * ET + i * BODY + (h + 1) * GT)
                        sp.dma_start(ea[:, h, :], io["ea_T"][:, bass.ds(i * (BODY * TP) + h * GT * TP, GT * TP)])\
                            .then_inc(S[f"ea_in{h}"], 16)
            sp.dma_start(rows[:, :], io["b2"]).then_inc(S["b2_in"], 16)
            sp.dma_start(wih, io["wih_T"].rearrange("(k p) n -> p k n", p=128)).then_inc(S["wih_in"], 16)
            sp.wait_ge(S["out_d"], 1)
            sp.dma_start(whh, io["whh_T"].rearrange("(k p) n -> p k n", p=128)).then_inc(S["whh_in"], 16)
            sp.wait_ge(S["agg_sb"], 12)
            for k, name in enumerate(("b_ih", "b_hh")):
                sp.dma_start(vec[:, k * 3 * D:(k + 1) * 3 * D], io[name].to_broadcast([TP, 3 * D])).then_inc(S["vec_in"], 16)
            for k, name in enumerate(("gamma", "beta", "run_mean", "run_var")):
                sp.dma_start(vec[:, (6 + k) * D:(7 + k) * D], io[name].to_broadcast([TP, D])).then_inc(S["vec_in"], 16)
            sp.dma_start(wsm, io["wsm"].rearrange("(k p) n -> p k n", p=128)).then_inc(S["wsm_in"], 16)
            sp.dma_start(fixed[:, 0:MASK_COLS], io["cst"]).then_inc(S["cst_in"], 16)
            for name, n in (("alog", H), ("dtb", H), ("onorm", DK)):
                sp.dma_start(f[name], io[name].to_broadcast([128, n])).then_inc(S["cst_in"], 16)
            sp.wait_ge(S["gate_mm"], NT)
            for name in ("wk", "wq"):
                sp.dma_start(proj[name], io[name].rearrange("(k p) n -> p k n", p=128)).then_inc(S["wkq_in"], 16)
            sp.wait_ge(S["x1_ok"], NT)
            for name in ("wv", "wg", "wo"):
                sp.dma_start(proj[name], io[name].rearrange("(k p) n -> p k n", p=128)).then_inc(S["wvg_in"], 16)

            def by_chunk(dram, t, q, tile, n, done):
                sp.dma_start(dram[4 * t + q].rearrange("(h i) n -> i h n", h=4),
                             tile[32 * q:32 * q + 32, :].rearrange("p (h n) -> p h n", h=4)).then_inc(done, 16)

            sp.wait_ge(S["gw_ok"], 12)
            for t in range(TT):
                for q in range(4):
                    by_chunk(GW_dram, t, q, gwt[:, t].rearrange("p h q g e -> p (h q g e)"), 24, S["gw_st"])
            sp.wait_ge(S["gw_st"], 16 * 4 * TT)
            sp.wait_ge(S["z_mm"], 2 * TT)
            sp.dma_start(gw, GW_dram.rearrange("c p n -> p c n")).then_inc(S["gw_in"], 16)
            for t in range(TT):
                sp.wait_ge(S["kt_ok"], 2 * (t + 1))
                for q in range(4):
                    by_chunk(KV_dram[:, :, 0:256], t, q, ktb[t % 2], 256, S[f"kt_st{t % 2}"])
            def systems_out(i, q):
                if True:
                    sp.wait_ge(S["lt_ok"], i * 2 + (q + 1))
                    sp.dma_start(L_dram[bass.ds((i * 2 + q) * (SG * 4), SG * 4), :].rearrange("(g h) (j i) -> (h j) g i", h=4, j=C),
                                 lt[q]).then_inc(S[f"lt_st{q}"], 16)
                    sp.wait_ge(S["at_ok"], i * 2 + (q + 3))
                    sp.dma_start(A_dram[bass.ds(i * 2 + q, 1), :, :].rearrange("c p n -> p (c n)"),
                                 at[q].rearrange("p g i -> p (g i)")).then_inc(S[f"at_st{q}"], 16)
            def by_system(dram, hf):
                return dram[hf * QG * 128:(hf + 1) * QG * 128, :].rearrange("(q p) n -> p q n", p=128)

            for hf in range(2):
                with sp.Fori(hf * NC // 4, (hf + 1) * NC // 4) as i:
                    for q in range(2):
                        systems_out(i, q)
                for q in range(2):
                    sp.wait_ge(S[f"lt_st{q}"], 16 * (hf + 1) * NC // 4 + 16)
                if hf == 0:
                    pass
                sp.dma_start(systems[hf].rearrange("p q n i -> p q (n i)"), by_system(L_dram, hf)).then_inc(S[f"l_in{hf}"], 16)
            for t in range(TT):
                sp.wait_ge(S["v_ok"], t + 1)
                for q in range(4):
                    by_chunk(KV_dram[:, :, 256:384], t, q, dbuf[:, (t % 2) * D:(t % 2 + 1) * D], 128, S[f"v_st{t % 2}"])

            def inverses_out(hf):
                sp.wait_ge(S["x_ok"], hf + 1)
                sp.dma_start(by_system(X_dram, hf), systems[hf].rearrange("p q n i -> p q (n i)")).then_inc(S["x_st"], 16)
                sp.wait_ge(S["x_st"], 16 * (hf + 1))

            inverses_out(0)
            for q in range(2):
                sp.wait_ge(S[f"kt_st{q}"], 16 * 4 * TT // 2)
                sp.wait_ge(S[f"v_st{q}"], 16 * 4 * TT // 2)
                sp.wait_ge(S[f"at_st{q}"], 16 * NC // 2 + 16)
            sp.wait_ge(S["bdz"], 2)
            def load_inverses(c, q):
                for h in range(4):
                    sp.dma_start(xbd[q][32 * h:32 * h + 32, :, 32 * h:32 * h + 32],
                                 X_dram[bass.ds(c * (SG * 4), SG * 4), :].rearrange("(g h) (j i) -> h j g i", h=4, j=C)[h])\
                        .then_inc(S[f"x_in{q}"], 16)

            def load_keys_values(c, q):
                sp.dma_start(kvc[q], KV_dram[bass.ds(c, 1), :, :].rearrange("c p n -> p (c n)")).then_inc(S[f"kv_in{q}"], 16)

            def load_attention(c, q):
                for h in range(4):
                    sp.dma_start(abd[q][32 * h:32 * h + 32, :, 32 * h:32 * h + 32],
                                 A_dram[bass.ds(c, 1), 32 * h:32 * h + 32, :].rearrange("c p (g i) -> p (c g) i", g=SG))\
                        .then_inc(S[f"a_in{q}"], 16)

            for q in range(2):
                load_keys_values(q, q)
                load_inverses(q, q)
                load_attention(q, q)

            inverses_out(1)

            def chunk(j, r, last):
                c, q = j * 4 + r, r % 2
                if not last:
                    sp.wait_ge(S["u_mm1"], c + 1)
                    load_inverses(c + 2, q)
                    sp.wait_ge(S["su_mm1"], c + 1)
                    load_keys_values(c + 2, q)
                    sp.wait_ge(S["o_mm1"], c + 3)
                    load_attention(c + 2, q)
                sp.wait_ge(S["o_ok"], c * 2 + 6)
                sp.dma_start(O_dram[bass.ds(c, 1), :, :].rearrange("c p n -> (c p) n"), osb[q]).then_inc(S[f"o_st{q}"], 16)

            last_tile = NC // 4 - 1

            def output_back(j, r, done):
                sp.wait_ge(S[f"o_st{r % 2}"], done)
                sp.dma_start(core[32 * r:32 * r + 32, bass.ds(j, 1), :].rearrange("p t (h n) -> p (t h) n", h=4),
                             O_dram[bass.ds(j * 4 + r, 1), :, :].rearrange("c (h i) n -> i (c h) n", h=4)).then_inc(S["core_last" if j is last_tile else "core_in"], 16)

            def stores(j, r):
                return j * 32 + (16 * (r // 2) + 32)

            with sp.Fori(0, last_tile) as j:
                for r in range(4):
                    chunk(j, r, False)
                    if r:
                        output_back(j, r - 1, stores(j, r - 1))
                output_back(j, 3, stores(j, 3))
            for r in range(4):
                chunk(last_tile, r, r >= 2)
                if r:
                    output_back(last_tile, r - 1, stores(last_tile, r - 1))
            output_back(last_tile, 3, stores(last_tile, 3))
            for t in range(NT):
                sp.wait_ge(S["out_ok"], t + 1)
                sp.dma_start(io["out"][t * TP:(t + 1) * TP, :], xt[:, t, :]).then_inc(S["out_st0"], 16)
            sp.wait_ge(S["out_st0"], 16 * NT)

        @block.gpsimd
        def _(pool):
            st = Steps(pool, S["pool"])
            nc.gpsimd.iota(a["iota"].bitcast(I32), [[1, W]], base=0, channel_multiplier=0).then_inc(S["iota_ok"], 1)
            st.then(nc.gpsimd.memset(ident[:, :], 0.0))
            nc.gpsimd.memset(a["ones"], 1.0).then_inc(S["consts"], 1)
            nc.gpsimd.affine_select(out=ident[:, :], in_=ident[:, :], compare_op=ALU.not_equal, fill=1.0, base=0,
                                    pattern=[[-1, 128]], channel_multiplier=1).then_inc(S["consts"], 1)
            nc.gpsimd.memset(accT[:, :, :], 0.0).then_inc(S["consts"], 1)
            pool.wait_ge(S["spans"], 2)
            nc.gpsimd.partition_all_reduce(a["base"], a["start"], TP, RMAX).then_inc(S["base_ok"], 1)
            nc.gpsimd.partition_all_reduce(a["high"], a["high"], TP, RMAX).then_inc(S["base_ok"], 1)
            n = passes(pool)
            pool.wait_ge(S["P_out0"], 16 * (NT // 2))
            pool.wait_ge(S["P_out1"], 16 * (NT // 2))
            pool.wait_ge(S["ids_in"], 32)
            with pool.Fori(0, n + 1) as p:
                with pool.Fori(0, NB) as i:
                    for h in range(2):
                        pool.wait_ge(S["pg_free"], p * ET + i * BODY + (h + 1) * GT)
                        pool.sem_inc(S["gather_go"], 1)
                        nc.gpsimd.tensor_copy(idx[:, h * GT:h * GT + GT],
                                              srci[:, bass.ds(i * BODY + h * GT, GT)]).then_inc(S["idx_ok"], 1)
                        pool.wait_ge(S["idx_ok"], p * (2 * NB) + i * 2 + (h + 1))
                        pool.sem_inc(S["gather_go"], 1)
                        for k in range(h * GT, h * GT + GT):
                            nc.gpsimd.indirect_dma_start(
                                pg[:, k, :], None, P_dram, bass.IndirectOffsetOnAxis(ap=idx[:, k:k + 1], axis=0)
                            ).then_inc(gath[k], 16)

            pool.wait_ge(S["out_d"], 1)
            nc.gpsimd.memset(hT[:, :, N:NTOK], 0.0).then_inc(S["pad_ok"], 1)
            pool.wait_ge(S["x1_ok"], NT)
            for k in range(2):
                nc.gpsimd.memset(ktb[k], 0.0).then_inc(S["ktz"], 1)
            pool.wait_ge(S["ktz"], 2)
            for t in range(TT):
                pool.wait_ge(S["kq_ok"], 2 * t + 1)
                if t >= 2:
                    pool.wait_ge(S[f"kt_st{t % 2}"], 16 * 4 * (t // 2))
                kt = ktb[t % 2].rearrange("p (s a g b k) -> p s a g b k", s=2, a=2, g=2, b=2)
                src = kq[:, 0, t, :].rearrange("p (g s a k) -> p s a g k", g=2, s=2, a=2)
                for h2 in range(2):
                    nc.gpsimd.tensor_copy(kt[:, :, h2, :, h2, :], src[:, :, h2, :, :]).then_inc(S["kt_ok"], 1)
            pool.wait_ge(S["gw_in"], 16)
            with pool.Fori(0, NC // 2) as i:
                for q in range(2):
                    pool.wait_ge(S["dw_mm"], i * 2 + (q + 1))
                    pool.sem_inc(S["gather_go"], 1)
                    gch = gw[:, bass.ds(i * 2 + q, 1), :].rearrange("p c n -> p (c n)")
                    nc.gpsimd.tensor_tensor(rg[q], gch[:, 0:SG][:, :, None].to_broadcast([128, SG, C]),
                                            f["le"][:, None, :].to_broadcast([128, SG, C]), ALU.mult).then_inc(S["rg_ok"], 1)
                    nc.gpsimd.tensor_tensor(wd[q], gch[:, 16:16 + X][:, :, None].to_broadcast([128, X, C]),
                                            f["eye"][:, None, :].to_broadcast([128, X, C]), ALU.mult).then_inc(S["rg_ok"], 1)
            for t in range(TT):
                pool.wait_ge(S["gt_ok"], t + 1)
                gate_t = gate[:, :, t * 128:(t + 1) * 128].rearrange("p k (g n) -> p k g n", g=2)
                nc.gpsimd.tensor_tensor(gate_t, gate_t, f["onorm"][:, None, None, :].to_broadcast([128, KC, 2, DK]), ALU.mult)\
                    .then_inc(S["gn_ok"], 1)
            pool.wait_ge(S["x_st"], 16)
            nc.gpsimd.memset(accf[:, 0:6144], 0.0).then_inc(S["bdz"], 1)
            nc.gpsimd.memset(wreg[:, 1728:2752], 0.0).then_inc(S["bdz"], 1)
            with pool.Fori(0, NC) as c:
                for hh in range(2):
                    pool.wait_ge(S[f"s_ok{hh}"], c + 1)
                    pool.sem_inc(S["gather_go"], 1)
                    nc.gpsimd.tensor_tensor(sdec4[:, :, hh], state4[:, :, hh],
                                            GamC[:, :, bass.ds(c, 1), hh * X:(hh + 1) * X].rearrange("p s c n -> p s (c n)")[:, :, :, None]
                                            .to_broadcast([128, 2, X, DK]), ALU.mult).then_inc(S[f"sd_ok{hh}"], 1)

        @block.scalar
        def _(act):
            st = Steps(act, S["act"])
            act.wait_ge(S["ln_mv"], 1)
            nc.scalar.activation(rstd[:, :], rstd[:, :], ACT.Sqrt).then_inc(S["ln_std"], 1)
            act.sem_inc(S["pg_free"], BODY)
            n = passes(act)
            with act.Fori(0, n + 1) as p:
                def relu(i, k):
                    act.wait_ge(S["pre_add"], p * ET + i * BODY + (RB + k + 1))
                    act.wait_ge(S["relu_free"], p * ET + i * BODY + (k + 1))
                    nc.scalar.activation(rl[:, k, :], pg[:, k, :], ACT.Relu).then_inc(S["pg_free"], 1)

                def sums(i, g):
                    act.wait_ge(S["relu_free"], p * ET + i * BODY + (BODY + GT * (g + 1)))
                    act.wait_ge(S["fold_mm"], p * G + i * 2 + (g + 2))
                    nc.scalar.activation(a["sums"], psum[:, 5 + g, :], ACT.Copy).then_inc(S["sums_ok"], 1)

                def body(i, first):
                    relu(i, 0)
                    relu(i, 1)
                    if not first:
                        sums(i - 1, 1)
                    for k in range(2, BODY):
                        relu(i, k)
                    sums(i, 0)

                body(0, True)
                with act.Fori(1, NB) as i:
                    body(i, False)
                sums(NB - 1, 1)

            for m_ in range(12):
                act.wait_ge(S["agg_mm"], m_ + 1)
                c_, b_ = m_ // 3, m_ % 3
                lo, hi = N * b_ // 3, N * (b_ + 1) // 3
                nc.scalar.activation(aggT[:, c_, lo:hi], psum[:, m_ % 8, 0:hi - lo], ACT.Copy).then_inc(S["agg_sb"], 1)
            act.wait_ge(S["bn_pre"], 1)
            nc.scalar.activation(vec[:, 9 * D:10 * D], vec[:, 9 * D:10 * D], ACT.Sqrt).then_inc(S["bn_std"], 1)
            def hidden_back(t):
                act.wait_ge(S["ln2_T"], t + 1)
                nc.scalar.activation(hT[:, :, t * TP:(t + 1) * TP],
                                     psum[:, 4 * (t % 2) + 3, 0:KC * TP].rearrange("p (k n) -> p k n", k=KC), ACT.Copy).then_inc(S["ln2_hT"], 1)

            for t in range(NT):
                if t:
                    hidden_back(t - 1)
                act.wait_ge(S["rz_pre"], t + 1)
                nc.scalar.activation(bo["rz"], bo["rz"], ACT.Sigmoid).then_inc(S["rz"], 1)
                act.wait_ge(S["n_pre"], t + 1)
                nc.scalar.activation(bo["in"], bo["in"], ACT.Tanh).then_inc(S["n_ok"], 1)
                act.wait_ge(S["ln2_mv"], t + 1)
                nc.scalar.activation(rstd[:, t:t + 1], rstd[:, t:t + 1], ACT.Sqrt).then_inc(S["ln2_std"], 1)
            hidden_back(NT - 1)
            act.wait_ge(S["cst_in"], 64)
            nc.scalar.activation(rt["ea"], f["alog"], ACT.Exp).then_inc(S["ab_ok"], 1)
            act.wait_ge(S["lg_pre"], 1)
            nc.scalar.activation(rt["p"], rt["lg"], ACT.Exp).then_inc(S["p_ok"], 1)
            act.wait_ge(S["ab_pre"], 2)
            nc.scalar.activation(rt["eb"], rt["b"], ACT.Exp, scale=-1.0).then_inc(S["ab_ok"], 1)
            nc.scalar.activation(rt["y"], rt["ax"], ACT.Exp, scale=-1.0).then_inc(S["ab_ok"], 1)
            for m_ in range(2 * TT):
                act.wait_ge(S["z_mm"], m_ + 1)
                nc.scalar.activation(kq[:, m_ % 2, m_ // 2, :], psum[:, 1 + m_ % 4, :], ACT.Silu).then_inc(S["z_ok"], 1)
            act.wait_ge(S["ss_ok"], 2)
            nc.scalar.activation(norms, norms, ACT.Sqrt).then_inc(S["nrm_ok"], 1)
            for m_, (q, t) in enumerate(transposing):
                act.wait_ge(S["kqT_mm"], m_ + 1)
                if q == 0:
                    act.wait_ge(S["kt_ok"], 2 * (t + 1))
                nc.scalar.activation(kqT[:, q, 4 * t:4 * t + 4], psum[:, 5 + m_ % 2, :].rearrange("p (h c i) -> p c h i", h=4, c=4),
                                     ACT.Copy).then_inc(S["kqT_ok"], 1)
            act.wait_ge(S["dec_mm"], 4)
            for k_, dst_ in enumerate((Gam, bDC, GamC[:, 0], GamC[:, 1])):
                nc.scalar.activation(dst_, psum[:, k_, 0:NC * SG].rearrange("p (c n) -> p c n", c=NC), ACT.Exp)\
                    .then_inc(S["dec_ok"], 1)
            act.wait_ge(S["kqT_ok"], 2 * TT)

            def stage_kq(i, q):
                nc.scalar.activation(kqc[q].rearrange("p h (q i) -> p h q i", q=2), kqT[:, :, bass.ds(i * 2 + q, 1)].rearrange("p q c h i -> p (c h) q i"),
                                     ACT.Copy).then_inc(S["dkq_ok"], 1)
            with act.Fori(0, NC // 2) as i:
                for q in range(2):
                    act.wait_ge(S["dw_mm"], i * 2 + (q + 1))
                    stage_kq(i, q)
                    act.wait_ge(S["d_mm"], i * 2 + (q + 1))
                    act.wait_ge(S["at_ok"], i * 2 + (q + 1))
                    nc.scalar.activation(ex[q], psum[:, 2 * q, 0:256].rearrange("p (g i) -> p g i", g=SG), ACT.Exp).then_inc(S["e_ok"], 1)
            for m_ in range(2 * TT):
                t = m_ // 2
                act.wait_ge(S["vg_mm"], m_ + 1)
                if m_ % 2 == 0:
                    if t >= 2:
                        act.wait_ge(S[f"v_st{t % 2}"], 16 * 4 * (t // 2))
                    nc.scalar.activation(dbuf[:, (t % 2) * D:(t % 2 + 1) * D], psum[:, m_ % 4, :], ACT.Silu).then_inc(S["v_ok"], 1)
                else:
                    nc.scalar.activation(gate[:, :, t * 128:(t + 1) * 128], psum[:, m_ % 4, :].rearrange("p (k n) -> p k n", k=KC), ACT.Silu)\
                        .then_inc(S["gt_ok"], 1)
            act.wait_ge(S["bdz"], 2)
            with act.Fori(0, NC // 2) as i:
                for q in range(2):
                    act.wait_ge(S["o_mm1"], i * 2 + (q + 1))
                    for h2 in range(2):
                        nc.scalar.activation(kqb[q][64 * h2:64 * h2 + 64, :, :, 32 * h2:32 * h2 + 32],
                                             kqT[64 * h2:64 * h2 + 64, :, bass.ds(i * 2 + q, 1)].rearrange("p q c h i -> p (c h) q i"),
                                             ACT.Copy).then_inc(S["kqs"], 1)
                    for hh in range(2):
                        act.wait_ge(S[f"o_mm{hh}"], i * 2 + (q + 2))
                        act.wait_ge(S[f"up_ok{hh}"], i * 2 + (q + 1))
                        nc.scalar.activation(usb[:, hh * 256:(hh + 1) * 256], psum[:, 4 * hh + 2, 0:256], ACT.Copy)\
                            .then_inc(S[f"u_ok{hh}"], 1)
            def core_back(t):
                act.wait_ge(S["cT_mm"], t + 1)
                nc.scalar.activation(coreT[:, :, t * 128:(t + 1) * 128], psum[:, t % 2, :].rearrange("p (k n) -> p k n", k=KC), ACT.Copy)\
                    .then_inc(S["cT_ok"], 1)

            for t in range(TT):
                act.wait_ge(S["cn_a"], t + 1)
                nc.scalar.activation(cstat[:, t, :], cstat[:, t, :], ACT.Sqrt).then_inc(S["cn_b"], 1)
                if t:
                    core_back(t - 1)
            core_back(TT - 1)

        @block.tensor
        def _(pe):
            pe.wait_ge(S["consts"], 2)
            for t in range(NT):
                pe.wait_ge(S["ln_h"], t + 1)
                if t >= 2:
                    pe.wait_ge(S["ln_hT"], t - 1)
                for k in range(KC):
                    m = nc.tensor.transpose(psum[:, t % 2, k * TP:(k + 1) * TP], ht[0:TP, t, k * 128:(k + 1) * 128],
                                            ident[0:TP, 0:TP])
                m.then_inc(S["ln_T"], 1)
            pe.wait_ge(S["w1_in"], 64)
            for t in range(NT):
                pe.wait_ge(S["ln_hT"], t + 1)
                if t >= 2:
                    pe.wait_ge(S["P_sb"], t - 1)
                for k in range(KC):
                    m = nc.tensor.matmul(psum[0:TP, 2 + t % 2, :], hT[:, k, t * TP:(t + 1) * TP], w1h[:, k, :],
                                         start=(k == 0), stop=(k == KC - 1))
                m.then_inc(S["P_mm"], 1)
            pe.sem_inc(S["pre_mm"], BODY)
            pe.sem_inc(S["relu_free"], BODY)
            pe.sem_inc(S["fold_mm"], 2)
            n = passes(pe)

            def pre(k, tiles, bodies):
                kk = k % BODY
                if kk % GT == 0:
                    pe.wait_ge(S[f"ea_in{kk // GT}"], bodies + 16 * (k // BODY + 1))
                pe.wait_ge(S["pre_add"], tiles + k + 1)
                nc.tensor.matmul(psum[0:TP, kk % RB, :],
                                 ea[:, kk // GT, (kk % GT) * TP:(kk % GT + 1) * TP], a["w1e"],
                                 start=True, stop=True).then_inc(S["pre_mm"], 1)

            def acc(ks, tiles, groups):
                pe.wait_ge(S["oh_ok"], groups + ks[-1] // GT + 1)
                pe.wait_ge(S["pg_free"], tiles + (BODY + ks[-1] + 1))
                for k in ks:
                    g, part = k // GT, slice(W * (k % 4), W * (k % 4) + W)
                    nc.tensor.matmul(psum[part, 5 + g, :], oh[:, g, k % GT, :], rl[:, k, :],
                                     start=(k % GT < 4), stop=(k % GT > 0),
                                     skip_group_check=True).then_inc(S["relu_free"], 1)

            def fold(g, groups):
                pe.wait_ge(S["sums_ok"], groups + g + 1)
                pe.wait_ge(S["acc_add"], groups + g + 2)
                for c in range(KC):
                    nc.tensor.matmul(psum[:, 7, c * W:(c + 1) * W], a["sums"][:, c * 128:(c + 1) * 128], a["fold"],
                                     start=True, stop=True, skip_group_check=True)
                nc.tensor.matmul(psum[0:1, 7, KC * W:(KC + GT) * W], a["ones"], oh[:, g, :, :].rearrange("p t w -> p (t w)"),
                                 start=True, stop=True, skip_group_check=True).then_inc(S["fold_mm"], 1)

            pe.wait_ge(S["P_sb"], NT)
            with pe.Fori(0, n + 1) as p:
                for k in range(AHEAD):
                    pre(k, p * ET, p * (NB * 16))

                def body(i, first, last):
                    tiles, bodies, groups = p * ET + i * BODY, p * (NB * 16) + i * 16, p * G + i * 2

                    def ahead(ks):
                        for k in ks:
                            if not (last and k >= BODY):
                                pre(k, tiles, bodies)

                    ahead(range(4, 8))
                    acc(range(0, 4), tiles, groups)
                    if not first:
                        fold(1, groups - 2)
                    ahead(range(8, 10))
                    acc(range(4, 8), tiles, groups)
                    ahead(range(10, 12))
                    fold(0, groups)
                    acc(range(8, 10), tiles, groups)
                    ahead(range(12, 14))

                body(0, True, False)
                with pe.Fori(1, NB - 1) as i:
                    body(i, False, False)
                body(NB - 1, False, True)
                fold(1, p * G + 2 * (NB - 1))

            pe.wait_ge(S["out_d"], 1)
            pe.wait_ge(S["b2_in"], 16)
            for m_ in range(12):
                c_, b_ = m_ // 3, m_ % 3
                lo, hi = N * b_ // 3, N * (b_ + 1) // 3
                if m_ >= 8:
                    pe.wait_ge(S["agg_sb"], m_ - 7)
                for k in range(KC):
                    nc.tensor.matmul(psum[:, m_ % 8, 0:hi - lo], w2[:, k, c_ * 128:(c_ + 1) * 128], accT[:, k, lo:hi],
                                     start=(k == 0), stop=False)
                nc.tensor.matmul(psum[:, m_ % 8, 0:hi - lo], rows[0:1, c_ * 128:(c_ + 1) * 128], accT[0:1, KC, lo:hi],
                                 start=False, stop=True).then_inc(S["agg_mm"], 1)
            def hidden_T(t):
                pe.wait_ge(S["ln2_h"], t + 1)
                for k in range(KC):
                    m = nc.tensor.transpose(psum[:, 4 * (t % 2) + 3, k * TP:(k + 1) * TP], ht[0:TP, t, k * 128:(k + 1) * 128],
                                            ident[0:TP, 0:TP])
                m.then_inc(S["ln2_T"], 1)

            pe.wait_ge(S["agg_sb"], 12)
            pe.wait_ge(S["wih_in"], 16)
            pe.wait_ge(S["whh_in"], 16)
            for t in range(NT):
                if t >= 2:
                    pe.wait_ge(S["gate_rd"], 3 * (t - 1))
                q = 4 * (t % 2)
                rows_ = slice(t * TP, (t + 1) * TP)
                for g_ in range(3):
                    for k in range(KC):
                        m = nc.tensor.matmul(psum[0:TP, q + g_, :], aggT[:, k, rows_], wih[:, k, g_ * D:(g_ + 1) * D],
                                             start=(k == 0), stop=(g_ == 2 and k == KC - 1))
                    if g_ == 2 and t >= 2:
                        pe.wait_ge(S["ln2_hT"], t - 1)
                    for k in range(KC):
                        m = nc.tensor.matmul(psum[0:TP, q + g_ + (g_ == 2), :], hT[:, k, rows_], whh[:, k, g_ * D:(g_ + 1) * D],
                                             start=(g_ == 2 and k == 0), stop=(k == KC - 1))
                m.then_inc(S["gate_mm"], 1)
                if t:
                    hidden_T(t - 1)
            pe.wait_ge(S["wsm_in"], 16)
            pe.wait_ge(S["pad_ok"], 1)
            pe.wait_ge(S["gate_rd"], 3 * (NT - 1))
            for t in range(TT):
                if t < NT - 2:
                    pe.wait_ge(S["ln2_hT"], t + 2)
                elif t == NT - 2:
                    hidden_T(NT - 1)
                    pe.wait_ge(S["ln2_hT"], NT)
                for k in range(KC):
                    m = nc.tensor.matmul(psum[:, 0, t * 20:(t + 1) * 20], hT[:, k, t * 128:(t + 1) * 128], wsm[:, k, :],
                                         start=(k == 0), stop=(k == KC - 1), skip_group_check=True)
            m.then_inc(S["sm_mm"], 1)
            pe.wait_ge(S["wkq_in"], 32)
            pe.wait_ge(S["gate_rd"], 3 * NT)
            for m_ in range(2 * TT):
                t = m_ // 2
                if m_ >= 4:
                    pe.wait_ge(S["z_ok"], m_ - 3)
                for k in range(KC):
                    m = nc.tensor.matmul(psum[:, 1 + m_ % 4, :], hT[:, k, t * 128:(t + 1) * 128], proj["wq" if m_ % 2 else "wk"][:, k, :],
                                         start=(k == 0), stop=(k == KC - 1))
                m.then_inc(S["z_mm"], 1)
            for m_, (q, t) in enumerate(transposing):
                pe.wait_ge(S["kq_ok"], 2 * t + q + 1)
                if m_ >= 2:
                    pe.wait_ge(S["kqT_ok"], m_ - 1)
                for hp in range(4):
                    m = nc.tensor.transpose(psum[:, 5 + m_ % 2, hp * 128:(hp + 1) * 128], kq[:, q, t, hp * 128:(hp + 1) * 128], ident[:, :])
                m.then_inc(S["kqT_mm"], 1)
            pe.wait_ge(S["gw_in"], 16)
            pe.wait_ge(S["z_ok"], 2 * TT)
            for k_, name in enumerate(("leb", "gt", "s0", "s1")):
                nc.tensor.matmul(psum[:, k_, 0:NC * SG], f[name], gw[:, :, 0:SG], start=True, stop=True).then_inc(S["dec_mm"], 1)
            pe.wait_ge(S["dec_ok"], 4)
            pe.sem_inc(S["dw_mm"], 2)
            with pe.Fori(0, NC // 2) as i:
                for q in range(2):
                    pe.wait_ge(S["rg_ok"], i * 4 + (2 * q + 2))
                    pe.wait_ge(S["dkq_ok"], i * 2 + (q + 1))
                    pe.wait_ge(S["at_ok"], i * 2 + (q + 1))
                    nc.tensor.matmul(psum[:, 2 * q, 0:256], f["gt"], rg[q].rearrange("p g i -> p (g i)"), start=True, stop=True,
                                     skip_group_check=True).then_inc(S["d_mm"], 1)
                    nc.tensor.matmul(psum[:, 2 * q + 1, 0:128], f["bd"], wd[q].rearrange("p e i -> p (e i)"), start=True, stop=True,
                                     skip_group_check=True)
                    for hd in range(H):
                        hh, h4 = hd // 4, hd % 4
                        s_, h2 = h4 // 2, h4 % 2
                        part = slice(64 * h2, 64 * h2 + 64)
                        m = nc.tensor.matmul(psum[32 * h4:32 * h4 + 32, 4 + h2 + 2 * q, hh * 64:hh * 64 + 64],
                                             kqc[q][part, 2 * hh + s_, 0:32], kqc[q][part, 2 * hh + s_, :],
                                             start=True, stop=True, skip_group_check=True)
                    m.then_inc(S["dw_mm"], 1)
            pe.wait_ge(S["wvg_in"], 48)
            pe.wait_ge(S["at_ok"], NC + 2)
            for m_ in range(2 * TT):
                t = m_ // 2
                if m_ >= 4:
                    pe.wait_ge(*((S["gt_ok"], t - 1) if m_ % 2 else (S["v_ok"], t - 1)))
                for k in range(KC):
                    m = nc.tensor.matmul(psum[:, m_ % 4, :], hT[:, k, t * 128:(t + 1) * 128], proj["wg" if m_ % 2 else "wv"][:, k, :],
                                         start=(k == 0), stop=(k == KC - 1))
                m.then_inc(S["vg_mm"], 1)
            for hh in range(2):
                pe.sem_inc(S[f"o_mm{hh}"], 2)
            pe.wait_ge(S["bdz"], 2)
            with pe.Fori(0, NC // 2) as i:
                for q in range(2):
                    c = i * 2 + q
                    pe.wait_ge(S["kqs"], c * 2 + 2)
                    for hh in range(2):
                        pe.wait_ge(S[f"s_ok{hh}"], c + 1)
                        for w_ in range(2):
                            for s_ in range(2):
                                m = nc.tensor.matmul(psum[64 * s_:64 * s_ + 64, 4 * hh + w_, 0:256], kqb[q][:, 2 * hh + s_, w_, :],
                                                     state[:, (2 * s_ + hh) * 256:(2 * s_ + hh) * 256 + 256],
                                                     start=True, stop=True, skip_group_check=True)
                            m.then_inc(S[f"ks_mm{hh}"], 1)
                    pe.wait_ge(S[f"x_in{q}"], i * 64 + 64)
                    for hh in range(2):
                        pe.wait_ge(S[f"r_ok{hh}"], c + 1)
                        for g_ in range(hh * X, hh * X + X):
                            m = nc.tensor.matmul(psum[:, 4 * hh + 2, g_ % X * 64:(g_ % X + 1) * 64], xbd[q][:, g_, :],
                                                 resid[:, g_ * 64:(g_ + 1) * 64], start=True, stop=True, skip_group_check=True)
                        m.then_inc(S[f"u_mm{hh}"], 1)
                    pe.wait_ge(S[f"kv_in{q}"], i * 16 + 16)
                    for hh in range(2):
                        pe.wait_ge(S[f"up_ok{hh}"], c + 1)
                        for s_ in range(2):
                            m = nc.tensor.matmul(psum[:, 4 * hh + s_, 256:512], kbd[q][64 * s_:64 * s_ + 64, hh, :],
                                                 ups[64 * s_:64 * s_ + 64, hh * 256:hh * 256 + 256],
                                                 start=True, stop=True, skip_group_check=True)
                        m.then_inc(S[f"su_mm{hh}"], 1)
                        pe.wait_ge(S[f"a_in{q}"], i * 64 + 64)
                        pe.wait_ge(S[f"u_ok{hh}"], c + 1)
                        pe.wait_ge(S["o_ok"], c * 2 + (hh + 3))
                        for e in range(X):
                            g_ = hh * X + e
                            m = nc.tensor.matmul(psum[:, 4 * hh + 3, 0:64], abd[q][:, g_, :], usb[:, g_ * 64:(g_ + 1) * 64],
                                                 start=(e == 0), stop=(e == X - 1), skip_group_check=True)
                        m.then_inc(S[f"o_mm{hh}"], 1)
            for t in range(TT):
                pe.wait_ge(S["core_ok"], t + 1)
                if t >= 2:
                    pe.wait_ge(S["cT_ok"], t - 1)
                for k in range(KC):
                    m = nc.tensor.transpose(psum[:, t % 2, k * 128:(k + 1) * 128], core[:, t, k * 128:(k + 1) * 128], ident[:, :])
                m.then_inc(S["cT_mm"], 1)
                pe.wait_ge(S["cT_ok"], t + 1)
                if t >= 2:
                    pe.wait_ge(S["out_ok"], t - 1)
                for k in range(KC):
                    m = nc.tensor.matmul(psum[0:TP, 3 + t % 2, :], coreT[:, k, t * TP:(t + 1) * TP], proj["wo"][:, k, :],
                                         start=(k == 0), stop=(k == KC - 1))
                m.then_inc(S["out_mm"], 1)

        @block.vector
        def _(v):
            st = Steps(v, S["dve"])
            for t in range(NT):
                if t % 2 == 0:
                    v.wait_ge(S[f"tok_in{t // 2}"], 16)
                st.did(nc.vector.bn_stats(stats[:, t, :], xt[:, t, :]))
            st.settle()
            for t in range(NT):
                st.did(nc.vector.bn_aggr(mv[:, t, :], stats[:, t, :]))
            st.settle()
            nc.vector.tensor_scalar(rstd[:, :], mv[:, :, 1], LN_EPS, None, ALU.add).then_inc(S["ln_mv"], 1)
            v.wait_ge(S["ln_std"], 1)
            st.then(nc.vector.reciprocal(rstd[:, :], rstd[:, :]))
            for t in range(NT):
                nc.vector.tensor_scalar(ht[0:TP, t, :], xt[:, t, :], mv[:, t, 0:1], rstd[:, t:t + 1],
                                        ALU.subtract, ALU.mult).then_inc(S["ln_h"], 1)
            v.wait_ge(S["ids_in"], 32)
            st.then(nc.vector.tensor_copy(dstf, dsti))
            st.then(nc.vector.tensor_scalar(rel, dstf, -1.0, None, ALU.mult))
            nc.vector.tensor_reduce(a["start"], rel.rearrange("p (g t) -> p g t", t=GT), AX.X, ALU.max)\
                .then_inc(S["spans"], 1)
            nc.vector.tensor_reduce(a["high"], dstf.rearrange("p (g t) -> p g t", t=GT), AX.X, ALU.max)\
                .then_inc(S["spans"], 1)
            for t in range(NT):
                v.wait_ge(S["ln_T"], t + 1)
                nc.vector.tensor_copy(hT[:, :, t * TP:(t + 1) * TP],
                                      psum[:, t % 2, 0:KC * TP].rearrange("p (k n) -> p k n", k=KC))\
                    .then_inc(S["ln_hT"], 1)
            v.wait_ge(S["base_ok"], 2)
            st.then(nc.vector.tensor_tensor(a["high"], a["high"], a["base"], ALU.add))
            st.then(nc.vector.tensor_reduce(a["span"], a["high"], AX.X, ALU.max))
            st.then(nc.vector.tensor_copy(npass, a["span"]))
            nc.vector.tensor_scalar(npass, npass, W.bit_length() - 1, None, ALU.logical_shift_right)\
                .then_inc(S["pass_ok"], 1)
            v.wait_ge(S["iota_ok"], 1)
            st.then(nc.vector.tensor_copy(a["iota"], a["iota"].bitcast(I32)))
            st.then(nc.vector.tensor_scalar(a["start"], a["base"], -1.0, None, ALU.mult))
            for t in range(NT):
                v.wait_ge(S["P_mm"], t + 1)
                if t >= 2:
                    v.wait_ge(S[f"P_out{t % 2}"], 16 * (t // 2))
                nc.vector.tensor_tensor(pw[:, t % 2, :], psum[0:TP, 2 + t % 2, :], a["b1"], ALU.add)\
                    .then_inc(S["P_sb"], 1)
            st.then(nc.vector.tensor_reduce(a["fold"], ident[:, :].rearrange("p (j w) -> p w j", w=W), AX.X, ALU.add))
            v.sem_inc(S["pre_add"], RB)
            v.sem_inc(S["acc_add"], 2)
            v.wait_ge(S["consts"], 3)
            n = passes(v)
            base_n = st.n
            with v.Fori(0, n + 1) as p:
                PER_PASS = 4
                c0 = base_n + p * PER_PASS

                def chain(ins, k):
                    ins.then_inc(S["dve"], 1)
                    v.wait_ge(S["dve"], c0 + k)

                startb = a["start"][:, :, None].to_broadcast([TP, G, GT])
                chain(nc.vector.tensor_tensor(rel.rearrange("p (g t) -> p g t", t=GT),
                                              dstf.rearrange("p (g t) -> p g t", t=GT), startb, ALU.subtract), 1)
                chain(nc.vector.tensor_copy(starti[0:1, :], a["start"][0:1, :]), 2)
                chain(nc.vector.tensor_scalar(a["start"], a["start"], float(W), float(N), ALU.add, ALU.min), 3)
                chain(nc.vector.tensor_copy(a["span"], a["span"]), 4)

                def add(i, k):
                    v.wait_ge(S["pre_mm"], p * ET + i * BODY + (BODY + k + 1))
                    v.wait_ge(gath[k], p * (NB * 16) + i * 16 + 16)
                    nc.vector.tensor_tensor(pg[:, k, :], psum[0:TP, k % RB, :], pg[:, k, :], ALU.add)\
                        .then_inc(S["pre_add"], 1)

                def onehot(i, g):
                    v.wait_ge(S["fold_mm"], p * G + i * 2 + (g + 1))
                    nc.vector.tensor_tensor(
                        oh[:, g, :, :],
                        a["iota"][:, None, :].to_broadcast([TP, GT, W]),
                        rel[:, bass.ds(i * BODY + g * GT, GT)][:, :, None].to_broadcast([TP, GT, W]),
                        ALU.is_equal).then_inc(S["oh_ok"], 1)

                def acc_add(i, g):
                    s = v.value_load(starti[0:1, bass.ds(i * 2 + g, 1)], min_val=0, max_val=N)
                    v.wait_ge(S["fold_mm"], p * G + i * 2 + (g + 3))
                    v.wait_ge(S["acc_add"], p * G + i * 2 + (g + 2))
                    nc.vector.tensor_reduce(a["deg"], psum[0:1, 7, KC * W:(KC + GT) * W].rearrange("p (t w) -> p w t", w=W), AX.X, ALU.add)\
                        .then_inc(S["deg_ok"], 1)
                    nc.vector.tensor_tensor(accT[:, 0:KC, bass.ds(s, W)], accT[:, 0:KC, bass.ds(s, W)],
                                            psum[:, 7, 0:KC * W].rearrange("p (c w) -> p c w", w=W), ALU.add)
                    v.wait_ge(S["deg_ok"], p * G + i * 2 + (g + 1))
                    nc.vector.tensor_tensor(accT[0:1, KC, bass.ds(s, W)], accT[0:1, KC, bass.ds(s, W)],
                                            a["deg"], ALU.add).then_inc(S["acc_add"], 1)

                def body(i, first):
                    add(i, 0)
                    add(i, 1)
                    if not first:
                        onehot(i, 0)
                        acc_add(i - 1, 0)
                    for k in range(2, 8):
                        add(i, k)
                    onehot(i, 1)
                    if not first:
                        acc_add(i - 1, 1)
                    add(i, 8)
                    add(i, 9)

                onehot(0, 0)
                body(0, True)
                with v.Fori(1, NB) as i:
                    body(i, False)
                for g in range(2):
                    acc_add(NB - 1, g)
            st = Steps(v, S["dve2"])
            v.wait_ge(S["acc_add"], n * G + (G + 2))
            v.sem_inc(S["out_d"], 1)
            v.wait_ge(S["vec_in"], 16 * 6)
            bias_rz, bias_in, bias_hn = vec[:, 0:2 * D], vec[:, 2 * D:3 * D], vec[:, 5 * D:6 * D]
            gamma, beta, rmean, rvar = (vec[:, (6 + k) * D:(7 + k) * D] for k in range(4))
            nc.vector.tensor_scalar(rvar, rvar, BN_EPS, None, ALU.add).then_inc(S["bn_pre"], 1)
            st.then(nc.vector.tensor_tensor(bias_rz, bias_rz, vec[:, 3 * D:5 * D], ALU.add))
            v.wait_ge(S["bn_std"], 1)
            st.then(nc.vector.reciprocal(rvar, rvar))
            st.then(nc.vector.tensor_tensor(gamma, gamma, rvar, ALU.mult))
            st.then(nc.vector.tensor_tensor(rmean, rmean, gamma, ALU.mult))
            st.then(nc.vector.tensor_tensor(beta, beta, rmean, ALU.subtract))
            for t in range(NT):
                q = 4 * (t % 2)
                new, hn, nn, rz = bo["new"], bo["hn"], bo["in"], bo["rz"]
                v.wait_ge(S["gate_mm"], t + 1)
                nc.vector.tensor_tensor(rz.rearrange("p (g n) -> p g n", g=2), psum[0:TP, q:q + 2, :],
                                        bias_rz.rearrange("p (g n) -> p g n", g=2), ALU.add).then_inc(S["rz_pre"], 1)
                nc.vector.tensor_tensor(hn, psum[0:TP, q + 3, :], bias_hn, ALU.add).then_inc(S["gate_rd"], 1)
                nc.vector.tensor_tensor(nn, psum[0:TP, q + 2, :], bias_in, ALU.add).then_inc(S["gate_rd"], 1)
                v.wait_ge(S["rz"], t + 1)
                v.wait_ge(S["gate_rd"], 3 * t + 2)
                nc.vector.tensor_tensor(hn, hn, rz[:, 0:D], ALU.mult).then_inc(S["gate_rd"], 1)
                v.wait_ge(S["gate_rd"], 3 * t + 3)
                nc.vector.tensor_tensor(nn, nn, hn, ALU.add).then_inc(S["n_pre"], 1)
                v.wait_ge(S["n_ok"], t + 1)
                st.then(nc.vector.tensor_tensor(new, ht[0:TP, t, :], nn, ALU.subtract))
                st.then(nc.vector.tensor_tensor(new, new, rz[:, D:2 * D], ALU.mult))
                st.then(nc.vector.tensor_tensor(new, new, nn, ALU.add))
                st.then(nc.vector.tensor_tensor(new, new, gamma, ALU.mult))
                st.then(nc.vector.tensor_tensor(new, new, beta, ALU.add))
                st.then(nc.vector.tensor_tensor(new, new, ht[0:TP, t, :], ALU.add))
                nc.vector.tensor_tensor(xt[:, t, :], xt[:, t, :], new, ALU.add).then_inc(S["x1_ok"], 1)
                v.wait_ge(S["x1_ok"], t + 1)
                st.then(nc.vector.bn_stats(stats[:, t, :], xt[:, t, :]))
                st.then(nc.vector.bn_aggr(mv[:, t, :], stats[:, t, :]))
                nc.vector.tensor_scalar(rstd[:, t:t + 1], mv[:, t, 1:2], LN_EPS, None, ALU.add).then_inc(S["ln2_mv"], 1)
                v.wait_ge(S["ln2_std"], t + 1)
                st.then(nc.vector.reciprocal(rstd[:, t:t + 1], rstd[:, t:t + 1]))
                nc.vector.tensor_scalar(ht[0:TP, t, :], xt[:, t, :], mv[:, t, 0:1], rstd[:, t:t + 1],
                                        ALU.subtract, ALU.mult).then_inc(S["ln2_h"], 1)
            v.wait_ge(S["sm_mm"], 1)
            v.wait_ge(S["cst_in"], 64)
            sm = psum[:, 0, 0:TT * 20].rearrange("p (t n) -> p t n", t=TT)

            def over(x, *shape):
                return x.to_broadcast([128, *shape])

            st.then(nc.vector.tensor_reduce(rt["mx"], sm[:, :, 16:20], AX.X, ALU.max))
            nc.vector.tensor_tensor(rt["lg"], sm[:, :, 16:20], over(rt["mx"][:, :, None], TT, X), ALU.subtract).then_inc(S["lg_pre"], 1)
            st.then(nc.vector.tensor_tensor(rt["a"], sm[:, :, 0:8], over(f["dtb"][:, None, :], TT, H), ALU.add))
            st.then(nc.vector.tensor_scalar(rt["t1"], rt["a"], -1.0, None, ALU.mult))
            nc.vector.tensor_tensor(rt["ax"], rt["a"], rt["t1"], ALU.max).then_inc(S["ab_pre"], 1)
            nc.vector.tensor_copy(rt["b"], sm[:, :, 8:16]).then_inc(S["ab_pre"], 1)
            v.wait_ge(S["p_ok"], 1)
            p_ = rt["p"]
            st.then(nc.vector.tensor_reduce(rt["mx"], p_, AX.X, ALU.add))
            st.then(nc.vector.reciprocal(rt["mx"], rt["mx"]))
            st.then(nc.vector.tensor_tensor(p_, p_, over(rt["mx"][:, :, None], TT, X), ALU.mult))
            other, own = over(p_[:, :, None, :], TT, X, X), over(p_[:, :, :, None], TT, X, X)
            st.did(nc.vector.tensor_tensor(rt["gt"], other, own, ALU.is_gt))
            st.then(nc.vector.tensor_tensor(rt["eq"], other, own, ALU.is_equal))
            st.then(nc.vector.tensor_tensor(rt["eq"], rt["eq"], over(f["lt4"].rearrange("p (a b) -> p a b", a=X)[:, None], TT, X, X), ALU.mult))
            st.then(nc.vector.tensor_tensor(rt["gt"], rt["gt"], rt["eq"], ALU.add))
            st.then(nc.vector.tensor_reduce(rt["lg"], rt["gt"], AX.X, ALU.add))
            st.then(nc.vector.tensor_scalar(rt["lg"], rt["lg"], 2.0, None, ALU.is_lt))
            st.then(nc.vector.tensor_tensor(p_, p_, rt["lg"], ALU.mult))
            st.then(nc.vector.tensor_reduce(rt["mx"], p_, AX.X, ALU.add))
            st.then(nc.vector.reciprocal(rt["mx"], rt["mx"]))
            st.then(nc.vector.tensor_tensor(p_, p_, over(rt["mx"][:, :, None], TT, X), ALU.mult))
            st.then(nc.vector.tensor_scalar(rt["lg"], p_, 0.0, None, ALU.is_gt))
            v.wait_ge(S["ab_ok"], 3)
            st.then(nc.vector.tensor_scalar(rt["eb"], rt["eb"], 1.0, None, ALU.add))
            st.then(nc.vector.reciprocal(rt["eb"], rt["eb"]))
            st.then(nc.vector.tensor_scalar(rt["t1"], rt["y"], 2.0, None, ALU.add))
            st.then(nc.vector.reciprocal(rt["t1"], rt["t1"]))
            st.then(nc.vector.tensor_tensor(rt["y"], rt["y"], rt["t1"], ALU.mult))
            st.then(nc.vector.tensor_tensor(rt["t1"], rt["y"], rt["y"], ALU.mult))
            st.then(nc.vector.tensor_scalar(rt["ax"], rt["t1"], 2.0 / (2 * LOG_TERMS - 1), None, ALU.mult))
            for k in range(LOG_TERMS - 2, -1, -1):
                st.then(nc.vector.tensor_scalar(rt["ax"], rt["ax"], 2.0 / (2 * k + 1), None, ALU.add))
                st.then(nc.vector.tensor_tensor(rt["ax"], rt["ax"], rt["t1"] if k else rt["y"], ALU.mult))
            st.then(nc.vector.tensor_scalar(rt["a"], rt["a"], 0.0, None, ALU.max))
            st.then(nc.vector.tensor_tensor(rt["a"], rt["a"], rt["ax"], ALU.add))
            st.then(nc.vector.tensor_tensor(rt["a"], rt["a"], over(rt["ea"][:, None, :], TT, H), ALU.mult))
            st.then(nc.vector.tensor_scalar(rt["a"], rt["a"], -1.0, G_FLOOR, ALU.mult, ALU.max))
            for h in range(4):
                m4 = over(rt["lg"][:, :, None, :], TT, 2, X)
                for q, val in ((0, rt["a"]), (1, rt["eb"])):
                    nc.vector.tensor_tensor(gwt[:, :, h, q, :, :], over(val[:, :, 2 * h:2 * h + 2][:, :, :, None], TT, 2, X),
                                            m4, ALU.mult).then_inc(S["gw_ok"], 1)
                nc.vector.tensor_copy(gwt[:, :, h, 2, :, :], over(p_[:, :, None, :], TT, 2, X)).then_inc(S["gw_ok"], 1)
            for m_ in range(2 * TT):
                q, t = m_ % 2, m_ // 2
                v.wait_ge(S["z_ok"], m_ + 1)
                st.then(nc.vector.tensor_tensor(sq[q], kq[:, q, t, :], kq[:, q, t, :], ALU.mult))
                st.did(nc.vector.tensor_reduce(norms[:, q, t, :], sq[q].rearrange("p (h k) -> p h k", h=H), AX.X, ALU.add))
            st.settle()
            for q in range(2):
                nc.vector.tensor_scalar(norms[:, q], norms[:, q], 1e-6, float(DK) if q else 1.0, ALU.add, ALU.mult).then_inc(S["ss_ok"], 1)
            v.wait_ge(S["nrm_ok"], 1)
            st.then(nc.vector.reciprocal(norms, norms))
            for m_ in range(2 * TT):
                q, t = m_ % 2, m_ // 2
                by_head = kq[:, q, t, :].rearrange("p (h k) -> p h k", h=H)
                nc.vector.tensor_tensor(by_head, by_head, norms[:, q, t, :][:, :, None].to_broadcast([128, H, DK]), ALU.mult)\
                    .then_inc(S["kq_ok"], 1)
            v.wait_ge(S["dec_ok"], 4)
            st.did(nc.vector.tensor_tensor(bDC, bDC, gw[:, :, 8:16], ALU.mult))
            st.then(nc.vector.tensor_tensor(wGam, Gam, gw[:, :, 16:24], ALU.mult))
            v.sem_inc(S["at_ok"], 2)
            for q in range(2):
                v.sem_inc(S[f"lt_st{q}"], 16)
                v.sem_inc(S[f"at_st{q}"], 16)
            base2 = st.n
            with v.Fori(0, NC // 2) as i:
                for q in range(2):
                    c = i * 2 + q
                    c0 = base2 + i * 6 + 3 * q

                    def chain(ins, k):
                        ins.then_inc(S["dve2"], 1)
                        v.wait_ge(S["dve2"], c0 + k)

                    v.wait_ge(S["dw_mm"], c + 3)
                    for h4 in range(4):
                        r4 = slice(32 * h4, 32 * h4 + 32)
                        ins = nc.vector.tensor_tensor(kkm[r4], psum[r4, 4 + h4 % 2 + 2 * q, 0:128].rearrange("p (h q i) -> p h q i", h=2, q=2),
                                                      f["mask2"][r4].rearrange("p (q i) -> p q i", q=2)[:, None].to_broadcast([32, 2, 2, C]),
                                                      ALU.mult)
                    chain(ins, 1)
                    v.wait_ge(S["e_ok"], c + 1)
                    bch = gw[:, bass.ds(c, 1), 8:16].rearrange("p c n -> p (c n)")
                    chain(nc.vector.tensor_tensor(ex[q], ex[q], bch[:, :, None].to_broadcast([128, SG, C]), ALU.mult), 2)

                    def four(x):
                        return x.rearrange("p (h e) i -> p h e i", h=2)

                    v.wait_ge(S[f"lt_st{q}"], i * 16 + 16)
                    nc.vector.tensor_tensor(four(lt[q]), four(ex[q]), kkm[:, :, 0, :][:, :, None, :].to_broadcast([128, 2, X, C]),
                                            ALU.mult).then_inc(S["lt_ok"], 1)
                    chain(nc.vector.tensor_tensor(four(at1), four(ex[q]), kkm[:, :, 1, :][:, :, None, :].to_broadcast([128, 2, X, C]),
                                                  ALU.mult), 3)
                    v.wait_ge(S[f"at_st{q}"], i * 16 + 16)
                    nc.vector.tensor_tensor(four(at[q]), four(at1),
                                            psum[:, 2 * q + 1, 0:128].rearrange("p (e i) -> p e i", e=X)[:, None].to_broadcast([128, 2, X, C]),
                                            ALU.mult).then_inc(S["at_ok"], 1)
            st.n = base2 + 3 * NC
            for hf in range(2):
                XT = systems[hf]
                for q in range(2):
                    v.wait_ge(S[f"at_st{q}"], 16 * NC // 2 + 16)
                v.wait_ge(S[f"l_in{hf}"], 16)
                st.then(nc.vector.memset(XT.rearrange("p q n i -> p q (n i)")[:, :, ::C + 1], 1.0))
                for j in range(1, C - 1):
                    left = C - 1 - j
                    pr = Prod[:, 0:QG * j * left].rearrange("p (q n i) -> p q n i", q=QG, n=j)
                    st.then(nc.vector.tensor_tensor(pr, XT[:, :, j, j + 1:C][:, :, None, :].to_broadcast([128, QG, j, left]),
                                                    XT[:, :, 0:j, j][:, :, :, None].to_broadcast([128, QG, j, left]), ALU.mult))
                    ins = nc.vector.tensor_tensor(XT[:, :, 0:j, j + 1:C], XT[:, :, 0:j, j + 1:C], pr, ALU.add)
                    if j < C - 2:
                        st.then(ins)
                    else:
                        ins.then_inc(S["x_ok"], 1)
            v.wait_ge(S["bdz"], 2)
            for hh in range(2):
                v.sem_inc(S[f"s_ok{hh}"], 1)
            v.sem_inc(S["o_ok"], 4)
            for q in range(2):
                v.sem_inc(S[f"o_st{q}"], 16)
            base4 = st.n
            with v.Fori(0, NC // 2) as i:
                for q in range(2):
                    c = i * 2 + q
                    c0 = base4 + i * 12 + 6 * q

                    def step(ins):
                        ins.then_inc(S["dve2"], 1)

                    def half(x, hh):
                        return x[:, hh * 256:(hh + 1) * 256].rearrange("p (e v) -> p e v", e=X)

                    def bank(k, hh):
                        return psum[:, 4 * hh + k, 0:256].rearrange("p (e v) -> p e v", e=X)

                    def per_system(x, hh):
                        return x[:, bass.ds(c, 1), hh * X:(hh + 1) * X].rearrange("p c n -> p (c n)")[:, :, None].to_broadcast([128, X, DK])

                    for hh in range(2):
                        v.wait_ge(S[f"ks_mm{hh}"], c * 2 + 1)
                        step(nc.vector.tensor_tensor(half(ksd, hh), bank(0, hh), per_system(Gam, hh), ALU.mult))
                        v.wait_ge(S[f"kv_in{q}"], i * 16 + 16)
                        v.wait_ge(S["dve2"], c0 + hh + 1)
                        nc.vector.tensor_tensor(half(resid, hh), vch[q][:, hh * DK:(hh + 1) * DK][:, None, :].to_broadcast([128, X, DK]),
                                                half(ksd, hh), ALU.subtract).then_inc(S[f"r_ok{hh}"], 1)
                    for hh in range(2):
                        v.wait_ge(S[f"ks_mm{hh}"], c * 2 + 2)
                        step(nc.vector.tensor_tensor(half(qsd, hh), bank(1, hh), per_system(wGam, hh), ALU.mult))
                    for hh in range(2):
                        v.wait_ge(S[f"u_mm{hh}"], c + 1)
                        nc.vector.tensor_tensor(half(ups, hh), bank(2, hh), per_system(bDC, hh), ALU.mult).then_inc(S[f"up_ok{hh}"], 1)
                    v.wait_ge(S["dve2"], c0 + 4)
                    step(nc.vector.tensor_reduce(qsr[:, 0:64], half(qsd, 0).rearrange("p e v -> p v e"), AX.X, ALU.add))
                    for hh in range(2):
                        v.wait_ge(S[f"su_mm{hh}"], c + 1)
                        v.wait_ge(S[f"sd_ok{hh}"], c + 1)
                        nc.vector.tensor_tensor(state4[:, :, hh].rearrange("p s e v -> p s (e v)"), sdec4[:, :, hh].rearrange("p s e v -> p s (e v)"),
                                                psum[:, 4 * hh:4 * hh + 2, 256:512], ALU.add).then_inc(S[f"s_ok{hh}"], 1)
                        if hh == 0:
                            step(nc.vector.tensor_reduce(qsr[:, 64:128], half(qsd, 1).rearrange("p e v -> p v e"), AX.X, ALU.add))
                        v.wait_ge(S[f"o_mm{hh}"], c + 3)
                        v.wait_ge(S[f"o_st{q}"], i * 16 + 16)
                        v.wait_ge(S["dve2"], c0 + 6)
                        nc.vector.tensor_tensor(osb[q][:, hh * 64:(hh + 1) * 64], psum[:, 4 * hh + 3, 0:64], qsr[:, hh * 64:(hh + 1) * 64],
                                                ALU.add).then_inc(S["o_ok"], 1)
            st.n = base4 + 6 * NC
            v.wait_ge(S["gn_ok"], TT)

            def squares(t):
                if t == 0:
                    v.wait_ge(S["core_in"], 16 * (NC - 4))
                elif t == TT - 1:
                    v.wait_ge(S["core_last"], 16 * 4)
                st.then(nc.vector.tensor_tensor(sqb, core[:, t, :], core[:, t, :], ALU.mult))
                st.then(nc.vector.tensor_reduce(cstat[:, t, :], sqb.rearrange("p (h v) -> p h v", h=H), AX.X, ALU.add))
                nc.vector.tensor_scalar(cstat[:, t, :], cstat[:, t, :], 1.0 / DK, 1e-5, ALU.mult, ALU.add).then_inc(S["cn_a"], 1)

            def add_output(t):
                v.wait_ge(S["out_mm"], t + 1)
                nc.vector.tensor_tensor(xt[:, t, :], xt[:, t, :], psum[0:TP, 3 + t % 2, :], ALU.add).then_inc(S["out_ok"], 1)

            squares(0)
            for t in range(TT):
                if t + 1 < TT:
                    squares(t + 1)
                v.wait_ge(S["cn_b"], t + 1)
                st.then(nc.vector.reciprocal(cstat[:, t, :], cstat[:, t, :]))
                ct = core[:, t, :].rearrange("p (h v) -> p h v", h=H)
                st.then(nc.vector.tensor_tensor(ct, ct, cstat[:, t, :][:, :, None].to_broadcast([128, H, DK]), ALU.mult))
                nc.vector.tensor_tensor(core[:, t, :].rearrange("p (k n) -> p k n", k=KC), core[:, t, :].rearrange("p (k n) -> p k n", k=KC),
                                        gate[:, :, t * 128:(t + 1) * 128], ALU.mult).then_inc(S["core_ok"], 1)
                if t >= 2:
                    add_output(t - 2)
            add_output(TT - 2)
            add_output(TT - 1)


def _constants():
    p = np.arange(128)
    blk, j = p // C, p % C
    same = blk[:, None] == blk[None, :]
    i = np.arange(C)
    h2 = p // 64
    parts = [
        same & (j[:, None] > j[None, :]),
        same & (j[:, None] <= j[None, :]),
        same,
        blk[:, None] == h2[None, :],
        blk[:, None] == 2 + h2[None, :],
        h2[:, None] == h2[None, :],
        j[:, None] <= i[None, :],
        j[:, None] == i[None, :],
        np.concatenate([-1.0 * (i[None, :] > j[:, None]), i[None, :] >= j[:, None]], 1),
        np.broadcast_to((i[None, :X] < i[:X, None]).reshape(1, X * X), (128, X * X)),
    ]
    return np.ascontiguousarray(np.concatenate([x.astype(np.float32) for x in parts], 1))


def kernel(**inputs):
    import concourse.bacc as _bacc
    from concourse.bass_utils import run_bass_kernel_spmd as _run

    c = np.ascontiguousarray
    get = {k: np.asarray(v) for k, v in inputs.items()}
    w1 = get["L0_gnn_W1"]
    arrays = {
        "x": c(get["x"]),
        "src_t": c(get["src"].reshape(ET, TP).T),
        "dst_t": c(get["dst"].reshape(ET, TP).T),
        "ea_T": c(get["edge_attr_128"].T),
        "w1h_T": c(w1[:, :D].T),
        "w1e_T": c(w1[:, D:].T),
        "b1": c(get["L0_gnn_b1"][None, :]),
        "w2_T": c(get["L0_gnn_W2"].T),
        "b2": c(get["L0_gnn_b2"][None, :]),
        "wih_T": c(get["L0_gnn_W_ih"].T),
        "whh_T": c(get["L0_gnn_W_hh"].T),
    }
    for n in ("b_ih", "b_hh", "gamma", "beta", "run_mean", "run_var"):
        arrays[n] = c(get["L0_gnn_" + n][None, :])
    order = np.array([4 * hh + h4 for h4 in range(4) for hh in range(2)])

    def heads(w, axis):
        shape = list(w.shape)
        shape[axis:axis + 1] = [H, shape[axis] // H]
        return c(np.take(w.reshape(shape), order, axis=axis).reshape(w.shape))

    arrays["wq"], arrays["wk"] = c(get["L0_ffn_Wq"]), c(get["L0_ffn_Wk"])
    arrays["wv"], arrays["wg"] = heads(get["L0_ffn_Wv"], 1), heads(get["L0_ffn_Wg"], 1)
    arrays["wo"] = heads(get["L0_ffn_Wo"], 0)
    arrays["wsm"] = c(np.concatenate([heads(get["L0_ffn_Wa"], 1), heads(get["L0_ffn_Wb"], 1), get["L0_ffn_Wgate"]], 1))
    arrays["alog"], arrays["dtb"] = heads(get["L0_ffn_A_log"], 0)[None, :], heads(get["L0_ffn_dt_bias"], 0)[None, :]
    arrays["onorm"] = c(get["L0_ffn_o_norm_weight"][None, :])
    arrays["cst"] = _constants()
    nc = _bacc.Bacc("TRN2", target_bir_lowering=False, num_devices=1)
    io = {n: nc.dram_tensor(n, v.shape, mybir.dt.from_np(v.dtype), kind="ExternalInput").ap()
          for n, v in arrays.items()}
    io["out"] = nc.dram_tensor("out", (N, D), F32, kind="ExternalOutput").ap()
    build(nc, io)
    r = _run(nc, [arrays], core_ids=[0])
    return r.results[0]["out"]
```

```python
from contextlib import ExitStack

import numpy as np

import concourse.bass as bass
from concourse import mybir

F32 = mybir.dt.float32
I32 = mybir.dt.int32
ALU = mybir.AluOpType
ACT = mybir.ActivationFunctionType
AX = mybir.AxisListType
RMAX = bass.bass_isa.ReduceOp.max

N = 1250
D = 512
KC = D // 128
TP = 125
NT = N // TP
E = 41250
ED = 128
ET = E // TP
GT = 5
G = ET // GT
BODY = 2 * GT
RB = 5
AHEAD = 4
NB = ET // BODY
W = 32
NPAD = N + W
C = 32
NC = 40
NTOK = C * NC
TT = NTOK // 128
H = 8
DK = 64
X = 4
SG = 2 * X
QG = 5
LOG_TERMS = 10
G_FLOOR = -200.0
LN_EPS = 1e-5
BN_EPS = 1e-5

MASKS = (("gt", 128), ("leb", 128), ("bd", 128), ("s0", 128), ("s1", 128), ("le", C), ("eye", C),
         ("mask2", 2 * C), ("lt4", X * X))
MASK_COLS = sum(n for _, n in MASKS)
FIXED = MASK_COLS + 2 * H + DK + KC * 20


class Steps:

    def __init__(self, eng, sem):
        self.eng, self.sem, self.n = eng, sem, 0

    def did(self, ins):
        ins.then_inc(self.sem, 1)
        self.n += 1
        return self.n

    def settle(self):
        self.eng.wait_ge(self.sem, self.n)

    def then(self, ins):
        self.did(ins)
        self.settle()


def build(nc, io):
    with ExitStack() as ctx:
        def sb(name, shape, dt=F32):
            return ctx.enter_context(nc.sbuf_tensor(name, shape, dt))

        def sem(name):
            return ctx.enter_context(nc.semaphore(name))

        psum = ctx.enter_context(nc.psum_tensor("psum", [128, 8, 512], F32))

        ident = sb("ident", [128, 128])
        xt = sb("xt", [TP, NT, D])
        ht = sb("ht", [128, NT, D])
        hT = sb("hT", [128, KC, NTOK])
        accT = sb("accT", [128, KC + 1, NPAD])
        stats = sb("stats", [TP, NT, 6])
        mv = sb("mv", [TP, NT, 2])
        b2_row = sb("b2_row", [1, D])
        rstd = sb("rstd", [TP, NT])
        ARENA = 24584
        arena = sb("arena", [128, ARENA])

        def carve(spec):
            out, at = {}, 0
            for name, rows, n in spec:
                out[name] = arena[0:rows, at:at + n]
                at += n
            assert at <= ARENA, at
            return out

        a = carve([("w2", 128, KC * D), ("w1h", 128, KC * D), ("rlx", 128, (BODY - KC) * D), ("w1e", 128, D), ("b1", TP, D),
                   ("ea", 128, 2 * GT * TP), ("pg", TP, BODY * D), ("sums", 128, D), ("fold", 128, 2 * W), ("deg", 1, 2 * W), ("oh", TP, 2 * GT * W),
                   ("pw", TP, 2 * D), ("rel", TP, ET), ("dstf", TP, ET), ("dsti", TP, ET), ("srci", TP, ET),
                   ("base", TP, G), ("high", TP, G), ("start", TP, G), ("starti", TP, G), ("iota", TP, W),
                   ("ones", TP, 1), ("idx", TP, BODY), ("span", TP, 1), ("npass", TP, 1)])
        w1h = a["w1h"].rearrange("p (k n) -> p k n", k=KC)
        w2 = a["w2"].rearrange("p (k n) -> p k n", k=KC)
        ea = a["ea"].rearrange("p (g n) -> p g n", g=2)
        pg = a["pg"].rearrange("p (s n) -> p s n", s=BODY)
        rl = arena[0:TP, KC * D:(KC + BODY) * D].rearrange("p (s n) -> p s n", s=BODY)
        oh = a["oh"].rearrange("p (g t w) -> p g t w", g=2, t=GT)
        pw = a["pw"].rearrange("p (s n) -> p s n", s=2)
        rel, dstf = a["rel"], a["dstf"]
        dsti, srci, starti, idx, npass = (a[x].bitcast(I32) for x in ("dsti", "srci", "starti", "idx", "npass"))

        bo = carve([("w2", 128, KC * D), ("whh", 128, KC * 3 * D), ("aggT", 128, KC * N), ("rz", TP, 2 * D),
                    ("hn", TP, D), ("in", TP, D), ("new", TP, D), ("gap", 128, 2688), ("wih", 128, KC * 3 * D)])
        wih = bo["wih"].rearrange("p (k n) -> p k n", k=KC)
        whh = bo["whh"].rearrange("p (k n) -> p k n", k=KC)
        aggT = bo["aggT"].rearrange("p (k n) -> p k n", k=KC)
        accf = accT[:, :, :].rearrange("p c n -> p (c n)")
        vec = accf[0:TP, 0:10 * D]

        f = carve([("kqT", 128, 4 * NC * 2 * C), ("wq", 128, KC * D), ("wv", 128, KC * D), ("wg", 128, KC * D),
                   ("wk", 128, KC * D), ("wo", 128, KC * D), ("dbuf", 128, 2720)])
        fixed = sb("fixed", [128, FIXED])
        at_ = 0
        for name, n in (*MASKS, ("alog", H), ("dtb", H), ("onorm", DK), ("wsm", KC * 20)):
            f[name] = fixed[:, at_:at_ + n]
            at_ += n
        gate = hT[:, :, :]
        kq = f["kqT"].rearrange("p (q t n) -> p q t n", q=2, t=TT)
        kqT = f["kqT"].rearrange("p (q c h i) -> p q c h i", q=2, c=NC, h=4)
        proj = {n: f[n].rearrange("p (k n) -> p k n", k=KC) for n in ("wq", "wk", "wv", "wg", "wo")}
        wsm = f["wsm"].rearrange("p (k n) -> p k n", k=KC)
        dbuf = f["dbuf"]
        wreg = arena[:, 4 * NC * 2 * C:4 * NC * 2 * C + 8192]
        gw = wreg[:, 0:NC * 24].rearrange("p (c n) -> p c n", c=NC)
        dec = wreg[:, 6144:6144 + 1600]
        Gam, bDC, wGam = (dec[:, k * 320:(k + 1) * 320].rearrange("p (c n) -> p c n", c=NC) for k in range(3))
        GamC = dec[:, 960:1600].rearrange("p (s c n) -> p s c n", s=2, c=NC)
        htf = ht[:, :, :].rearrange("p t n -> p (t n)")
        systems = [x[:, 0:QG * C * C].rearrange("p (q n i) -> p q n i", q=QG, n=C) for x in (accf, htf)]
        Prod = dbuf[:, 1024:1024 + QG * C * C // 4]

        KV_dram = nc.dram_tensor("KV_scratch", [NC, 128, 384], F32, kind="Internal").ap()
        GW_dram = nc.dram_tensor("GW_scratch", [4, NTOK, 24], F32, kind="Internal").ap()
        L_dram = nc.dram_tensor("L_scratch", [NC * SG * 4, C * C], F32, kind="Internal").ap()
        X_dram = nc.dram_tensor("X_scratch", [NC * SG * 4, C * C], F32, kind="Internal").ap()
        A_dram = nc.dram_tensor("A_scratch", [NC, 128, SG * C], F32, kind="Internal").ap()
        O_dram = nc.dram_tensor("O_scratch", [NC, 128, 128], F32, kind="Internal").ap()
        P_dram = nc.dram_tensor("P_scratch", [N, D], F32, kind="Internal").ap()

        def take(base, at, n):
            return base[:, at:at + n]

        rg = [x.rearrange("p (g i) -> p g i", g=SG) for x in (take(dbuf, 0, 256), take(accf, 5120, 256))]
        wd = [x.rearrange("p (e i) -> p e i", e=X) for x in (take(dbuf, 256, 128), take(accf, 5376, 128))]
        ex = [x.rearrange("p (g i) -> p g i", g=SG) for x in (take(dbuf, 384, 256), take(accf, 5504, 256))]
        kkm = take(dbuf, 640, 128).rearrange("p (h q i) -> p h q i", h=2, q=2)
        at1 = take(dbuf, 768, 256).rearrange("p (g i) -> p g i", g=SG)
        kqc = [take(dbuf, 1024 + 256 * q, 256).rearrange("p (h n) -> p h n", h=4) for q in range(2)]
        kbc = [take(accf, 5760 + 256 * q, 256).rearrange("p (h n) -> p h n", h=4) for q in range(2)]
        lt = [take(dbuf, 1536 + 256 * q, 256).rearrange("p (g i) -> p g i", g=SG) for q in range(2)]
        at = [take(dbuf, 2048 + 256 * q, 256).rearrange("p (g i) -> p g i", g=SG) for q in range(2)]
        xbd = [take(accf, 1024 * q, 1024).rearrange("p (g i) -> p g i", g=SG) for q in range(2)]
        abd = [take(accf, 2048 + 1024 * q, 1024).rearrange("p (g i) -> p g i", g=SG) for q in range(2)]
        state = take(accf, 4096, 1024)
        sdec = take(accf, 5120, 1024)
        state4, sdec4 = (x.rearrange("p (s h e v) -> p s h e v", s=2, h=2, e=X) for x in (state, sdec))
        kvc = [take(wreg, 960 + 384 * q, 384) for q in range(2)]
        kbd = [kvc[q][:, 0:256].rearrange("p (h n) -> p h n", h=2) for q in range(2)]
        vch = [kvc[q][:, 256:384] for q in range(2)]
        kqb = [take(wreg, 1728 + 512 * q, 512).rearrange("p (h q n) -> p h q n", h=4, q=2) for q in range(2)]
        resid, ksd, usb, ups, qsd = (take(wreg, 2752 + 512 * k, 512) for k in range(5))
        osb = [take(wreg, 5312 + 128 * q, 128) for q in range(2)]
        qsr = take(wreg, 5568, 128)
        core = htf.rearrange("p (t n) -> p t n", t=TT)
        sqb = wreg[:, 0:512]
        cstat = wreg[:, 512:592].rearrange("p (t h) -> p t h", t=TT)
        coreT = accf[:, 0:KC * NTOK].rearrange("p (k n) -> p k n", k=KC)

        rt, at_ = {}, 2048
        for name, shape in (("mx", [TT]), ("lg", [TT, X]), ("p", [TT, X]), ("gt", [TT, X, X]), ("eq", [TT, X, X])):
            n = int(np.prod(shape))
            v_ = dbuf[:, at_:at_ + n]
            rt[name] = v_ if len(shape) == 1 else v_.rearrange("p (t e) -> p t e", t=TT) if len(shape) == 2 else \
                v_.rearrange("p (t e g) -> p t e g", t=TT, e=X)
            at_ += n
        small = sb("small", [128, 5 * TT * H + H])
        for k, name in enumerate(("a", "b", "ax", "eb", "y")):
            rt[name] = small[:, k * 80:(k + 1) * 80].rearrange("p (t h) -> p t h", t=TT)
        rt["ea"] = small[:, 400:408]
        rt["t1"] = sb("t1", [128, TT, H])[:, :, :]
        sq = [accf[:, k * D:(k + 1) * D] for k in range(2)]
        ktb = [accf[:, 1024 + 1024 * k:2048 + 1024 * k] for k in range(2)]
        gwt = accf[:, 3072:3072 + TT * 96].rearrange("p (t h q g e) -> p t h q g e", t=TT, h=4, q=3, g=2)
        norms = accf[:, 4032:4032 + 2 * TT * H].rearrange("p (q t h) -> p q t h", q=2, t=TT)

        S = {n: sem(n) for n in (
            *(f"tok_in{k}" for k in range(2)), "w1_in", "ids_in", "consts", "dve", "pool", "ln_mv", "ln_std", "ln_h", "ln_T", "ln_hT",
            "P_mm", "P_sb", "P_out0", "P_out1", "spans", "base_ok", "pass_ok",
            "ea_in0", "ea_in1", "pre_mm", "pre_add", "relu_free", "oh_ok", "sums_ok", "fold_mm", "deg_mm", "deg_ok", "acc_add",
            "pg_free", "idx_ok", "out_d", "iota_ok", "gather_go", "wih_in", "whh_in", "vec_in",
            "agg_mm", "agg_sb", "gate_mm", "gate_rd", "rz_pre", "rz", "n_pre", "n_ok", "x1_ok", "ln2_mv", "ln2_std", "ln2_h", "ln2_T",
            "ln2_hT", "wsm_in", "wk_in", "wq_in", "wvg_in", "cst_in", "z_mm", "z_ok", "ss_ok", "nrm_ok", "kq_ok", "kqT_mm", "kqT_ok", "kt_ok", "ktz", "kt_st0", "kt_st1",
            "sm_mm", "lg_pre", "p_ok", "ab_pre", "ab_ok", "gw_ok", "gw_st", "gw_in", "vg_mm", "v_ok", "v_st0", "v_st1", "gt_ok", "gn_ok",
            "dec_mm", "dec_ok", "rg_ok", "dkq_ok", "kbz", "kk_mm", "w_mm", "kk_rd", "at1_ok", "d_mm", "e_ok", "lt_ok", "at_ok", "lt_st0", "lt_st1", "at_st0", "at_st1",
            "l_in0", "l_in1", "x_ok", "x_st", "x_in0", "x_in1", "kv_in0", "kv_in1", "a_in0", "a_in1", "bdz", "kqs", *(f"{x}{hh}" for x in ("ks_mm", "r_ok", "u_mm", "u_ok", "up_ok", "su_mm", "sd_ok", "s_ok", "o_mm") for hh in range(2)),
            "o_ok", "o_st0", "o_st1", "core_in", "core_last", "cn_a", "cn_b", "core_ok", "cT_mm", "cT_ok", "out_mm", "out_ok", "out_st", "pad_ok", "dve2", "bn_std", "bn_pre")}
        gath = [sem(f"gathered{k}") for k in range(BODY)]
        block = ctx.enter_context(nc.Block())

        def passes(eng):
            eng.wait_ge(S["pass_ok"], 1)
            return eng.value_load(npass[0:1, 0:1], min_val=0, max_val=(N + W - 1) // W)

        @block.sync
        def _(sp):
            for k in range(2):
                t = k * NT // 2
                sp.dma_start(xt[:, t:t + NT // 2, :], io["x"][t * TP:(t + NT // 2) * TP, :].rearrange("(t p) n -> p t n", p=TP)).then_inc(S[f"tok_in{k}"], 16)
            sp.dma_start(dsti, io["dst_t"]).then_inc(S["ids_in"], 16)
            sp.dma_start(srci, io["src_t"]).then_inc(S["ids_in"], 16)
            sp.dma_start(w1h, io["w1h_T"].rearrange("(k p) n -> p k n", p=128)).then_inc(S["w1_in"], 16)
            sp.dma_start(a["w1e"], io["w1e_T"]).then_inc(S["w1_in"], 16)
            sp.dma_start(a["b1"], io["b1"].to_broadcast([TP, D])).then_inc(S["w1_in"], 16)
            sp.dma_start(w2, io["w2_T"].rearrange("(k p) n -> p k n", p=128)).then_inc(S["w1_in"], 16)
            for t in range(NT):
                sp.wait_ge(S["P_sb"], t + 1)
                sp.dma_start(P_dram[t * TP:(t + 1) * TP, :], pw[:, t % 2, :]).then_inc(S[f"P_out{t % 2}"], 16)
            n = passes(sp)
            with sp.Fori(0, n + 1) as p:
                with sp.Fori(0, NB) as i:
                    for h in range(2):
                        sp.wait_ge(S["pre_mm"], p * ET + i * BODY + (h + 1) * GT)
                        sp.dma_start(ea[:, h, :], io["ea_T"][:, bass.ds(i * (BODY * TP) + h * GT * TP, GT * TP)])\
                            .then_inc(S[f"ea_in{h}"], 16)
            sp.dma_start(b2_row[:, :], io["b2"]).then_inc(S["wih_in"], 16)
            sp.dma_start(wih, io["wih_T"].rearrange("(k p) n -> p k n", p=128)).then_inc(S["wih_in"], 16)
            sp.wait_ge(S["out_d"], 1)
            sp.dma_start(whh, io["whh_T"].rearrange("(k p) n -> p k n", p=128)).then_inc(S["whh_in"], 16)
            sp.wait_ge(S["agg_sb"], 12)
            for k, name in enumerate(("b_ih", "b_hh")):
                sp.dma_start(vec[:, k * 3 * D:(k + 1) * 3 * D], io[name].to_broadcast([TP, 3 * D])).then_inc(S["vec_in"], 16)
            for k, name in enumerate(("gamma", "beta", "run_mean", "run_var")):
                sp.dma_start(vec[:, (6 + k) * D:(7 + k) * D], io[name].to_broadcast([TP, D])).then_inc(S["vec_in"], 16)
            sp.dma_start(wsm, io["wsm"].rearrange("(k p) n -> p k n", p=128)).then_inc(S["wsm_in"], 16)
            sp.dma_start(fixed[:, 0:MASK_COLS], io["cst"]).then_inc(S["cst_in"], 16)
            for name, n in (("alog", H), ("dtb", H), ("onorm", DK)):
                sp.dma_start(f[name], io[name].to_broadcast([128, n])).then_inc(S["cst_in"], 16)
            sp.dma_start(proj["wk"], io["wk"].rearrange("(k p) n -> p k n", p=128)).then_inc(S["wk_in"], 16)
            sp.wait_ge(S["gate_mm"], NT)
            sp.dma_start(proj["wq"], io["wq"].rearrange("(k p) n -> p k n", p=128)).then_inc(S["wq_in"], 16)
            sp.wait_ge(S["x1_ok"], NT)
            for name in ("wv", "wg", "wo"):
                sp.dma_start(proj[name], io[name].rearrange("(k p) n -> p k n", p=128)).then_inc(S["wvg_in"], 16)

            def by_chunk(dram, t, q, tile, n, done):
                sp.dma_start(dram[4 * t + q].rearrange("(h i) n -> i h n", h=4),
                             tile[32 * q:32 * q + 32, :].rearrange("p (h n) -> p h n", h=4)).then_inc(done, 16)

            for t in range(TT):
                sp.wait_ge(S["kt_ok"], 2 * (t + 1))
                for q in range(4):
                    by_chunk(KV_dram[:, :, 0:256], t, q, ktb[t % 2], 256, S[f"kt_st{t % 2}"])
            sp.wait_ge(S["gw_ok"], 12)
            for t in range(TT):
                sp.dma_start(GW_dram[:, t * 128:(t + 1) * 128, :].rearrange("h p n -> p h n"),
                             gwt[:, t].rearrange("p h q g e -> p h (q g e)")).then_inc(S["gw_st"], 16)
            sp.wait_ge(S["gw_st"], 16 * TT)
            sp.wait_ge(S["z_mm"], 2 * TT)
            for h in range(4):
                sp.dma_start(gw[32 * h:32 * h + 32], GW_dram[h].rearrange("(c i) n -> i c n", c=NC)).then_inc(S["gw_in"], 16)
            def systems_out(i, q):
                sp.wait_ge(S["lt_ok"], i * 2 + (q + 1))
                sp.dma_start(L_dram[bass.ds((i * 2 + q) * (SG * 4), SG * 4), :].rearrange("(g h) (j i) -> (h j) g i", h=4, j=C),
                             lt[q]).then_inc(S[f"lt_st{q}"], 16)
                sp.wait_ge(S["at_ok"], i * 2 + (q + 3))
                sp.dma_start(A_dram[bass.ds(i * 2 + q, 1), :, :].rearrange("c p n -> p (c n)"),
                             at[q].rearrange("p g i -> p (g i)")).then_inc(S[f"at_st{q}"], 16)

            def by_system(dram, hf):
                return dram[hf * QG * 128:(hf + 1) * QG * 128, :].rearrange("(q p) n -> p q n", p=128)

            def four_out(hf, g):
                for i in range(2):
                    for q in range(2):
                        systems_out(g * 2 + (hf * 2 * QG + i), q)

            def four_in(hf, g):
                for q in range(2):
                    sp.wait_ge(S[f"lt_st{q}"], g * 32 + (hf * 32 * QG + 48))
                sp.dma_start(systems[hf][:, bass.ds(g, 1)].rearrange("p q n i -> p (q n i)"),
                             L_dram[bass.ds(g * 128 + hf * QG * 128, 128), :]).then_inc(S[f"l_in{hf}"], 16)

            for hf in range(2):
                four_out(hf, 0)
                if hf:
                    four_in(0, QG - 1)
                with sp.Fori(1, QG) as g:
                    four_out(hf, g)
                    four_in(hf, g - 1)
            four_in(1, QG - 1)
            for t in range(TT):
                sp.wait_ge(S["v_ok"], t + 1)
                for q in range(4):
                    by_chunk(KV_dram[:, :, 256:384], t, q, dbuf[:, (t % 2) * D:(t % 2 + 1) * D], 128, S[f"v_st{t % 2}"])

            def inverses_out(hf):
                sp.wait_ge(S["x_ok"], hf + 1)
                sp.dma_start(by_system(X_dram, hf), systems[hf].rearrange("p q n i -> p q (n i)")).then_inc(S["x_st"], 16)
                sp.wait_ge(S["x_st"], 16 * (hf + 1))

            inverses_out(0)
            for q in range(2):
                sp.wait_ge(S[f"kt_st{q}"], 16 * 4 * TT // 2)
                sp.wait_ge(S[f"v_st{q}"], 16 * 4 * TT // 2)
                sp.wait_ge(S[f"at_st{q}"], 16 * NC // 2 + 16)
            sp.wait_ge(S["bdz"], 2)
            def load_inverses(c, q):
                for h in range(4):
                    sp.dma_start(xbd[q][32 * h:32 * h + 32, :, 32 * h:32 * h + 32],
                                 X_dram[bass.ds(c * (SG * 4), SG * 4), :].rearrange("(g h) (j i) -> h j g i", h=4, j=C)[h])\
                        .then_inc(S[f"x_in{q}"], 16)

            def load_keys_values(c, q):
                sp.dma_start(kvc[q], KV_dram[bass.ds(c, 1), :, :].rearrange("c p n -> p (c n)")).then_inc(S[f"kv_in{q}"], 16)

            def load_attention(c, q):
                for h in range(4):
                    sp.dma_start(abd[q][32 * h:32 * h + 32, :, 32 * h:32 * h + 32],
                                 A_dram[bass.ds(c, 1), 32 * h:32 * h + 32, :].rearrange("c p (g i) -> p (c g) i", g=SG))\
                        .then_inc(S[f"a_in{q}"], 16)

            for q in range(2):
                load_keys_values(q, q)
                load_inverses(q, q)
                load_attention(q, q)

            inverses_out(1)

            def chunk(j, r, last):
                c, q = j * 4 + r, r % 2
                if not last:
                    sp.wait_ge(S["u_mm1"], c + 1)
                    load_inverses(c + 2, q)
                    sp.wait_ge(S["su_mm1"], c + 1)
                    load_keys_values(c + 2, q)
                    sp.wait_ge(S["o_mm1"], c + 3)
                    load_attention(c + 2, q)
                sp.wait_ge(S["o_ok"], c * 2 + 6)
                sp.dma_start(O_dram[bass.ds(c, 1), :, :].rearrange("c p n -> (c p) n"), osb[q]).then_inc(S[f"o_st{q}"], 16)

            last_tile = NC // 4 - 1

            def output_back(j, r, done):
                sp.wait_ge(S[f"o_st{r % 2}"], done)
                sp.dma_start(core[32 * r:32 * r + 32, bass.ds(j, 1), :].rearrange("p t (h n) -> p (t h) n", h=4),
                             O_dram[bass.ds(j * 4 + r, 1), :, :].rearrange("c (h i) n -> i (c h) n", h=4))\
                    .then_inc(S["core_last" if j is last_tile else "core_in"], 16)

            def stores(j, r):
                return j * 32 + (16 * (r // 2) + 32)

            with sp.Fori(0, last_tile) as j:
                for r in range(4):
                    chunk(j, r, False)
                    if r:
                        output_back(j, r - 1, stores(j, r - 1))
                output_back(j, 3, stores(j, 3))
            for r in range(4):
                chunk(last_tile, r, r >= 2)
                if r:
                    output_back(last_tile, r - 1, stores(last_tile, r - 1))
            output_back(last_tile, 3, stores(last_tile, 3))
            for t in range(NT):
                sp.wait_ge(S["out_ok"], t + 1)
                sp.dma_start(io["out"][t * TP:(t + 1) * TP, :], xt[:, t, :]).then_inc(S["out_st"], 16)
            sp.wait_ge(S["out_st"], 16 * NT)

        @block.gpsimd
        def _(pool):
            st = Steps(pool, S["pool"])
            nc.gpsimd.iota(a["iota"].bitcast(I32), [[1, W]], base=0, channel_multiplier=0).then_inc(S["iota_ok"], 1)
            st.then(nc.gpsimd.memset(ident[:, :], 0.0))
            nc.gpsimd.memset(a["ones"], 1.0).then_inc(S["consts"], 1)
            nc.gpsimd.affine_select(out=ident[:, :], in_=ident[:, :], compare_op=ALU.not_equal, fill=1.0, base=0,
                                    pattern=[[-1, 128]], channel_multiplier=1).then_inc(S["consts"], 1)
            nc.gpsimd.memset(accT[:, :, :], 0.0).then_inc(S["consts"], 1)
            pool.wait_ge(S["spans"], 2)
            nc.gpsimd.partition_all_reduce(a["base"], a["start"], TP, RMAX).then_inc(S["base_ok"], 1)
            nc.gpsimd.partition_all_reduce(a["high"], a["high"], TP, RMAX).then_inc(S["base_ok"], 1)
            n = passes(pool)
            pool.wait_ge(S["P_out0"], 16 * (NT // 2))
            pool.wait_ge(S["P_out1"], 16 * (NT // 2))
            pool.wait_ge(S["ids_in"], 32)
            with pool.Fori(0, n + 1) as p:
                with pool.Fori(0, NB) as i:
                    for h in range(2):
                        pool.wait_ge(S["pg_free"], p * ET + i * BODY + (h + 1) * GT)
                        pool.sem_inc(S["gather_go"], 1)
                        nc.gpsimd.tensor_copy(idx[:, h * GT:h * GT + GT],
                                              srci[:, bass.ds(i * BODY + h * GT, GT)]).then_inc(S["idx_ok"], 1)
                        pool.wait_ge(S["idx_ok"], p * (2 * NB) + i * 2 + (h + 1))
                        pool.sem_inc(S["gather_go"], 1)
                        for k in range(h * GT, h * GT + GT):
                            nc.gpsimd.indirect_dma_start(
                                pg[:, k, :], None, P_dram, bass.IndirectOffsetOnAxis(ap=idx[:, k:k + 1], axis=0)
                            ).then_inc(gath[k], 16)

            pool.wait_ge(S["out_d"], 1)
            nc.gpsimd.memset(hT[:, :, N:NTOK], 0.0).then_inc(S["pad_ok"], 1)
            pool.wait_ge(S["x1_ok"], NT)
            nc.gpsimd.memset(accf[:, 5760:6272], 0.0).then_inc(S["kbz"], 1)
            pool.wait_ge(S["x1_ok"], NT)
            for k in range(2):
                nc.gpsimd.memset(ktb[k], 0.0).then_inc(S["ktz"], 1)
            pool.wait_ge(S["ktz"], 2)
            for t in range(TT):
                pool.wait_ge(S["kq_ok"], t + 1)
                if t >= 2:
                    pool.wait_ge(S[f"kt_st{t % 2}"], 16 * 4 * (t // 2))
                kt = ktb[t % 2].rearrange("p (s a g b k) -> p s a g b k", s=2, a=2, g=2, b=2)
                src = kq[:, 0, t, :].rearrange("p (g s a k) -> p s a g k", g=2, s=2, a=2)
                for h2 in range(2):
                    nc.gpsimd.tensor_copy(kt[:, :, h2, :, h2, :], src[:, :, h2, :, :]).then_inc(S["kt_ok"], 1)
            pool.wait_ge(S["gw_in"], 16 * 4)
            with pool.Fori(0, NC // 2) as i:
                for q in range(2):
                    pool.wait_ge(S["w_mm"], i * 2 + (q + 1))
                    pool.sem_inc(S["gather_go"], 1)
                    gch = gw[:, bass.ds(i * 2 + q, 1), :].rearrange("p c n -> p (c n)")
                    nc.gpsimd.tensor_tensor(rg[q], gch[:, 0:SG][:, :, None].to_broadcast([128, SG, C]),
                                            f["le"][:, None, :].to_broadcast([128, SG, C]), ALU.mult).then_inc(S["rg_ok"], 1)
                    nc.gpsimd.tensor_tensor(wd[q], gch[:, 16:16 + X][:, :, None].to_broadcast([128, X, C]),
                                            f["eye"][:, None, :].to_broadcast([128, X, C]), ALU.mult).then_inc(S["rg_ok"], 1)
            for t in range(TT):
                pool.wait_ge(S["gt_ok"], t + 1)
                gate_t = gate[:, :, t * 128:(t + 1) * 128].rearrange("p k (g n) -> p k g n", g=2)
                nc.gpsimd.tensor_tensor(gate_t, gate_t, f["onorm"][:, None, None, :].to_broadcast([128, KC, 2, DK]), ALU.mult)\
                    .then_inc(S["gn_ok"], 1)
            pool.wait_ge(S["x_st"], 16)
            nc.gpsimd.memset(accf[:, 0:6144], 0.0).then_inc(S["bdz"], 1)
            nc.gpsimd.memset(wreg[:, 1728:2752], 0.0).then_inc(S["bdz"], 1)
            with pool.Fori(0, NC) as c:
                for hh in range(2):
                    pool.wait_ge(S[f"s_ok{hh}"], c + 1)
                    pool.sem_inc(S["gather_go"], 1)
                    nc.gpsimd.tensor_tensor(sdec4[:, :, hh], state4[:, :, hh],
                                            GamC[:, :, bass.ds(c, 1), hh * X:(hh + 1) * X].rearrange("p s c n -> p s (c n)")[:, :, :, None]
                                            .to_broadcast([128, 2, X, DK]), ALU.mult).then_inc(S[f"sd_ok{hh}"], 1)

        @block.scalar
        def _(act):
            act.wait_ge(S["ln_mv"], 1)
            nc.scalar.activation(rstd[:, :], rstd[:, :], ACT.Sqrt).then_inc(S["ln_std"], 1)
            act.sem_inc(S["pg_free"], BODY)
            n = passes(act)
            with act.Fori(0, n + 1) as p:
                def relu(i, k):
                    act.wait_ge(S["pre_add"], p * ET + i * BODY + (RB + k + 1))
                    act.wait_ge(S["relu_free"], p * ET + i * BODY + (k + 1))
                    nc.scalar.activation(rl[:, k, :], pg[:, k, :], ACT.Relu).then_inc(S["pg_free"], 1)

                def sums(i):
                    act.wait_ge(S["relu_free"], p * ET + i * BODY + 2 * BODY)
                    act.wait_ge(S["fold_mm"], p * NB + i + 1)
                    nc.scalar.activation(a["sums"], psum[:, 5, :], ACT.Copy).then_inc(S["sums_ok"], 1)

                def body(i, first):
                    relu(i, 0)
                    relu(i, 1)
                    if not first:
                        sums(i - 1)
                    for k in range(2, BODY):
                        relu(i, k)

                body(0, True)
                with act.Fori(1, NB) as i:
                    body(i, False)
                sums(NB - 1)

            for m_ in range(12):
                act.wait_ge(S["agg_mm"], m_ + 1)
                c_, b_ = m_ // 3, m_ % 3
                lo, hi = N * b_ // 3, N * (b_ + 1) // 3
                nc.scalar.activation(aggT[:, c_, lo:hi], psum[:, m_ % 8, 0:hi - lo], ACT.Copy).then_inc(S["agg_sb"], 1)
            act.wait_ge(S["bn_pre"], 1)
            nc.scalar.activation(vec[:, 9 * D:10 * D], vec[:, 9 * D:10 * D], ACT.Sqrt).then_inc(S["bn_std"], 1)
            def hidden_back(t):
                act.wait_ge(S["ln2_T"], t + 1)
                nc.scalar.activation(hT[:, :, t * TP:(t + 1) * TP],
                                     psum[:, 4 * (t % 2) + 3, 0:KC * TP].rearrange("p (k n) -> p k n", k=KC), ACT.Copy).then_inc(S["ln2_hT"], 1)

            for t in range(NT):
                if t:
                    hidden_back(t - 1)
                act.wait_ge(S["rz_pre"], t + 1)
                nc.scalar.activation(bo["rz"], bo["rz"], ACT.Sigmoid).then_inc(S["rz"], 1)
                act.wait_ge(S["n_pre"], t + 1)
                nc.scalar.activation(bo["in"], bo["in"], ACT.Tanh).then_inc(S["n_ok"], 1)
                act.wait_ge(S["ln2_mv"], t + 1)
                nc.scalar.activation(rstd[:, t:t + 1], rstd[:, t:t + 1], ACT.Sqrt).then_inc(S["ln2_std"], 1)

            def routing_exp():
                act.wait_ge(S["cst_in"], 64)
                nc.scalar.activation(rt["ea"], f["alog"], ACT.Exp).then_inc(S["ab_ok"], 1)
                act.wait_ge(S["lg_pre"], 1)
                nc.scalar.activation(rt["p"], rt["lg"], ACT.Exp).then_inc(S["p_ok"], 1)
                act.wait_ge(S["ab_pre"], 2)
                nc.scalar.activation(rt["eb"], rt["b"], ACT.Exp, scale=-1.0).then_inc(S["ab_ok"], 1)
                nc.scalar.activation(rt["y"], rt["ax"], ACT.Exp, scale=-1.0).then_inc(S["ab_ok"], 1)

            def silu(q, t):
                m_ = q * TT + t
                act.wait_ge(S["z_mm"], m_ + 1)
                nc.scalar.activation(kq[:, q, t, :], psum[:, (0, 1, 2, 4)[m_ % 4], :], ACT.Silu).then_inc(S["z_ok"], 1)

            def transposed(q, t):
                m_ = q * TT + t
                act.wait_ge(S["kqT_mm"], m_ + 1)
                if q == 0:
                    act.wait_ge(S["kt_ok"], 2 * (t + 1))
                nc.scalar.activation(kqT[:, q, 4 * t:4 * t + 4], psum[:, 5 + m_ % 2, :].rearrange("p (h c i) -> p c h i", h=4, c=4),
                                     ACT.Copy).then_inc(S["kqT_ok"], 1)

            for t in range(TT):
                if t == NT - 2:
                    hidden_back(NT - 1)
                silu(0, t)
            for q in range(2):
                act.wait_ge(S["ss_ok"], q + 1)
                nc.scalar.activation(norms[:, q], norms[:, q], ACT.Sqrt).then_inc(S["nrm_ok"], 1)
                if q == 0:
                    routing_exp()
                    for t in range(TT):
                        silu(1, t)
                        if t:
                            transposed(0, t - 1)
                    transposed(0, TT - 1)
            for t in range(TT):
                transposed(1, t)
            act.wait_ge(S["dec_mm"], 4)
            for k_, dst_ in enumerate((Gam, bDC, GamC[:, 0], GamC[:, 1])):
                nc.scalar.activation(dst_, psum[:, k_, 0:NC * SG].rearrange("p (c n) -> p c n", c=NC), ACT.Exp)\
                    .then_inc(S["dec_ok"], 1)
            act.wait_ge(S["kqT_ok"], 2 * TT)

            act.wait_ge(S["kbz"], 1)
            act.sem_inc(S["e_ok"], 2)

            def stage_kq(i, q):
                for h2 in range(2):
                    part = slice(64 * h2, 64 * h2 + 64)
                    nc.scalar.activation(kbc[q][part, :, 32 * h2:32 * h2 + 32],
                                         kqT[part, 0, bass.ds(i * 2 + q, 1)].rearrange("p c h i -> p (c h) i"),
                                         ACT.Copy).then_inc(S["dkq_ok"], 1)
                nc.scalar.activation(kqc[q].rearrange("p h (q i) -> p h q i", q=2), kqT[:, :, bass.ds(i * 2 + q, 1)].rearrange("p q c h i -> p (c h) q i"),
                                     ACT.Copy).then_inc(S["dkq_ok"], 1)
            with act.Fori(0, NC // 2) as i:
                for q in range(2):
                    act.wait_ge(S["kk_mm"], i * 2 + (q + 1))
                    stage_kq(i, q)
                    act.wait_ge(S["d_mm"], i * 2 + (q + 1))
                    act.wait_ge(S["at1_ok"], i * 2 + (q + 1))
                    nc.scalar.activation(ex[q], psum[:, 2 * q, 0:256].rearrange("p (g i) -> p g i", g=SG), ACT.Exp).then_inc(S["e_ok"], 1)
            for m_ in range(2 * TT):
                t = m_ // 2
                act.wait_ge(S["vg_mm"], m_ + 1)
                if m_ % 2 == 0:
                    if t >= 2:
                        act.wait_ge(S[f"v_st{t % 2}"], 16 * 4 * (t // 2))
                    nc.scalar.activation(dbuf[:, (t % 2) * D:(t % 2 + 1) * D], psum[:, m_ % 4, :], ACT.Silu).then_inc(S["v_ok"], 1)
                else:
                    nc.scalar.activation(gate[:, :, t * 128:(t + 1) * 128], psum[:, m_ % 4, :].rearrange("p (k n) -> p k n", k=KC), ACT.Silu)\
                        .then_inc(S["gt_ok"], 1)
            act.wait_ge(S["bdz"], 2)
            with act.Fori(0, NC // 2) as i:
                for q in range(2):
                    act.wait_ge(S["o_mm1"], i * 2 + (q + 1))
                    for h2 in range(2):
                        nc.scalar.activation(kqb[q][64 * h2:64 * h2 + 64, :, :, 32 * h2:32 * h2 + 32],
                                             kqT[64 * h2:64 * h2 + 64, :, bass.ds(i * 2 + q, 1)].rearrange("p q c h i -> p (c h) q i"),
                                             ACT.Copy).then_inc(S["kqs"], 1)
                    for hh in range(2):
                        act.wait_ge(S[f"o_mm{hh}"], i * 2 + (q + 2))
                        act.wait_ge(S[f"up_ok{hh}"], i * 2 + (q + 1))
                        nc.scalar.activation(usb[:, hh * 256:(hh + 1) * 256], psum[:, 4 * hh + 2, 0:256], ACT.Copy)\
                            .then_inc(S[f"u_ok{hh}"], 1)
            def core_back(t):
                act.wait_ge(S["cT_mm"], t + 1)
                nc.scalar.activation(coreT[:, :, t * 128:(t + 1) * 128], psum[:, t % 2, :].rearrange("p (k n) -> p k n", k=KC), ACT.Copy)\
                    .then_inc(S["cT_ok"], 1)

            for t in range(TT):
                act.wait_ge(S["cn_a"], t + 1)
                nc.scalar.activation(cstat[:, t, :], cstat[:, t, :], ACT.Sqrt).then_inc(S["cn_b"], 1)
                if t:
                    core_back(t - 1)
            core_back(TT - 1)

        @block.tensor
        def _(pe):
            pe.wait_ge(S["consts"], 2)
            for t in range(NT):
                pe.wait_ge(S["ln_h"], t + 1)
                if t >= 2:
                    pe.wait_ge(S["ln_hT"], t - 1)
                for k in range(KC):
                    m = nc.tensor.transpose(psum[:, t % 2, k * TP:(k + 1) * TP], ht[0:TP, t, k * 128:(k + 1) * 128],
                                            ident[0:TP, 0:TP])
                m.then_inc(S["ln_T"], 1)
            pe.wait_ge(S["w1_in"], 64)
            for t in range(NT):
                pe.wait_ge(S["ln_hT"], t + 1)
                if t >= 2:
                    pe.wait_ge(S["P_sb"], t - 1)
                for k in range(KC):
                    m = nc.tensor.matmul(psum[0:TP, 2 + t % 2, :], hT[:, k, t * TP:(t + 1) * TP], w1h[:, k, :],
                                         start=(k == 0), stop=(k == KC - 1))
                m.then_inc(S["P_mm"], 1)
            pe.sem_inc(S["pre_mm"], BODY)
            pe.sem_inc(S["relu_free"], BODY)
            pe.sem_inc(S["fold_mm"], 1)
            pe.sem_inc(S["deg_mm"], 1)
            n = passes(pe)

            def pre(k, tiles, bodies):
                kk = k % BODY
                if kk % GT == 0:
                    pe.wait_ge(S[f"ea_in{kk // GT}"], bodies + 16 * (k // BODY + 1))
                pe.wait_ge(S["pre_add"], tiles + k + 1)
                nc.tensor.matmul(psum[0:TP, kk % RB, :],
                                 ea[:, kk // GT, (kk % GT) * TP:(kk % GT + 1) * TP], a["w1e"],
                                 start=True, stop=True).then_inc(S["pre_mm"], 1)

            def acc(ks, tiles, groups):
                if ks[0] == 0:
                    pe.wait_ge(S["oh_ok"], groups + 2)
                pe.wait_ge(S["pg_free"], tiles + (BODY + ks[-1] + 1))
                for k in ks:
                    t, g = k // 2, k % 2
                    at_ = W * (2 * g + t % 2)
                    nc.tensor.matmul(psum[at_:at_ + W, 5, :], oh[:, g, t, :], rl[:, k, :],
                                     start=(t < 2), stop=(t >= GT - 2), skip_group_check=True).then_inc(S["relu_free"], 1)

            def degrees(groups):
                pe.wait_ge(S["acc_add"], groups + 2)
                nc.tensor.matmul(psum[W:W + 1, 6, 0:BODY * W], a["ones"], oh.rearrange("p g t w -> p (g t w)"),
                                 start=True, stop=True, skip_group_check=True).then_inc(S["deg_mm"], 1)

            def fold(done, groups):
                pe.wait_ge(S["sums_ok"], done)
                pe.wait_ge(S["acc_add"], groups + 2)
                for c in range(KC):
                    m = nc.tensor.matmul(psum[:, 7, c * 2 * W:(c + 1) * 2 * W], a["sums"][:, c * 128:(c + 1) * 128], a["fold"],
                                         start=True, stop=True, skip_group_check=True)
                m.then_inc(S["fold_mm"], 1)

            pe.wait_ge(S["P_sb"], NT)
            with pe.Fori(0, n + 1) as p:
                for k in range(AHEAD):
                    pre(k, p * ET, p * (NB * 16))

                def body(i, first, last):
                    tiles, bodies, groups = p * ET + i * BODY, p * (NB * 16) + i * 16, p * G + i * 2

                    def ahead(ks):
                        for k in ks:
                            if not (last and k >= BODY):
                                pre(k, tiles, bodies)

                    ahead(range(4, 8))
                    if not first:
                        fold(p * NB + i, groups - 2)
                    acc(range(0, 4), tiles, groups)
                    ahead(range(8, 10))
                    acc(range(4, 8), tiles, groups)
                    ahead(range(10, 12))
                    acc(range(8, 10), tiles, groups)
                    degrees(groups)
                    ahead(range(12, 14))

                body(0, True, False)
                with pe.Fori(1, NB - 1) as i:
                    body(i, False, False)
                body(NB - 1, False, True)
                fold(p * NB + NB, p * G + 2 * (NB - 1))

            pe.wait_ge(S["out_d"], 1)
            pe.wait_ge(S["wih_in"], 32)
            for m_ in range(12):
                c_, b_ = m_ // 3, m_ % 3
                lo, hi = N * b_ // 3, N * (b_ + 1) // 3
                if m_ >= 8:
                    pe.wait_ge(S["agg_sb"], m_ - 7)
                for k in range(KC):
                    nc.tensor.matmul(psum[:, m_ % 8, 0:hi - lo], w2[:, k, c_ * 128:(c_ + 1) * 128], accT[:, k, lo:hi],
                                     start=(k == 0), stop=False)
                nc.tensor.matmul(psum[:, m_ % 8, 0:hi - lo], b2_row[0:1, c_ * 128:(c_ + 1) * 128], accT[0:1, KC, lo:hi],
                                 start=False, stop=True).then_inc(S["agg_mm"], 1)
            def hidden_T(t):
                pe.wait_ge(S["ln2_h"], t + 1)
                for k in range(KC):
                    m = nc.tensor.transpose(psum[:, 4 * (t % 2) + 3, k * TP:(k + 1) * TP], ht[0:TP, t, k * 128:(k + 1) * 128],
                                            ident[0:TP, 0:TP])
                m.then_inc(S["ln2_T"], 1)

            pe.wait_ge(S["agg_sb"], 12)
            pe.wait_ge(S["whh_in"], 16)
            for t in range(NT):
                if t >= 2:
                    pe.wait_ge(S["gate_rd"], 3 * (t - 1))
                q = 4 * (t % 2)
                rows_ = slice(t * TP, (t + 1) * TP)
                for g_ in range(3):
                    for k in range(KC):
                        m = nc.tensor.matmul(psum[0:TP, q + g_, :], aggT[:, k, rows_], wih[:, k, g_ * D:(g_ + 1) * D],
                                             start=(k == 0), stop=(g_ == 2 and k == KC - 1))
                    if g_ == 2 and t >= 2:
                        pe.wait_ge(S["ln2_hT"], t - 1)
                    for k in range(KC):
                        m = nc.tensor.matmul(psum[0:TP, q + g_ + (g_ == 2), :], hT[:, k, rows_], whh[:, k, g_ * D:(g_ + 1) * D],
                                             start=(g_ == 2 and k == 0), stop=(k == KC - 1))
                m.then_inc(S["gate_mm"], 1)
                if t:
                    hidden_T(t - 1)
            RING = (0, 1, 2, 4)

            def project(q, t):
                m_ = q * TT + t
                if m_ >= 4:
                    pe.wait_ge(S["z_ok"], m_ - 3)
                elif m_ == 3:
                    pe.wait_ge(S["gate_rd"], 3 * NT)
                for k in range(KC):
                    hT_t = hT[:, k, t * 128:(t + 1) * 128]
                    m = nc.tensor.matmul(psum[:, RING[m_ % 4], :], hT_t, proj["wq" if q else "wk"][:, k, :],
                                         start=(k == 0), stop=(k == KC - 1))
                    if q == 0:
                        if k == KC - 1:
                            m.then_inc(S["z_mm"], 1)
                        m = nc.tensor.matmul(psum[:, 3, t * 20:(t + 1) * 20], hT_t, wsm[:, k, :],
                                             start=(k == 0), stop=(k == KC - 1), skip_group_check=True)
                m.then_inc(S["z_mm"] if q else S["sm_mm"], 1)

            def transpose_tile(q, t):
                m_ = q * TT + t
                pe.wait_ge(S["kq_ok"], m_ + 1)
                if m_ >= 2:
                    pe.wait_ge(S["kqT_ok"], m_ - 1)
                for hp in range(4):
                    m = nc.tensor.transpose(psum[:, 5 + m_ % 2, hp * 128:(hp + 1) * 128], kq[:, q, t, hp * 128:(hp + 1) * 128], ident[:, :])
                m.then_inc(S["kqT_mm"], 1)

            pe.wait_ge(S["wk_in"], 16)
            pe.wait_ge(S["gate_rd"], 3 * (NT - 1))
            pe.wait_ge(S["wsm_in"], 16)
            pe.wait_ge(S["ln2_hT"], NT - 1)
            for t in range(NT - 2):
                project(0, t)
            hidden_T(NT - 1)
            pe.wait_ge(S["ln2_hT"], NT)
            pe.wait_ge(S["pad_ok"], 1)
            for t in range(NT - 2, TT):
                project(0, t)
            pe.wait_ge(S["wq_in"], 16)
            for t in range(TT):
                project(1, t)
                if t:
                    transpose_tile(0, t - 1)
            transpose_tile(0, TT - 1)
            for t in range(TT):
                transpose_tile(1, t)
            pe.wait_ge(S["gw_in"], 16 * 4)
            pe.wait_ge(S["ab_pre"], 2)
            for k_, name in enumerate(("leb", "gt", "s0", "s1")):
                nc.tensor.matmul(psum[:, k_, 0:NC * SG], f[name], gw[:, :, 0:SG], start=True, stop=True).then_inc(S["dec_mm"], 1)
            pe.wait_ge(S["dec_ok"], 4)
            pe.sem_inc(S["kk_mm"], 2)
            pe.sem_inc(S["w_mm"], 2)
            with pe.Fori(0, NC // 2) as i:
                for q in range(2):
                    pe.wait_ge(S["rg_ok"], i * 4 + (2 * q + 2))
                    pe.wait_ge(S["e_ok"], i * 2 + (q + 1))
                    nc.tensor.matmul(psum[:, 2 * q, 0:256], f["gt"], rg[q].rearrange("p g i -> p (g i)"), start=True, stop=True,
                                     skip_group_check=True).then_inc(S["d_mm"], 1)
                    pe.wait_ge(S["dkq_ok"], i * 6 + (3 * q + 3))
                    pe.wait_ge(S["kk_rd"], i * 2 + (q + 1))
                    for hp in range(4):
                        hh, s_ = hp // 2, hp % 2
                        m = nc.tensor.matmul(psum[64 * s_:64 * s_ + 64, 4 + q, hh * 64:hh * 64 + 64],
                                             kbc[q][:, hp, :], kqc[q][:, hp, :],
                                             start=True, stop=True, skip_group_check=True)
                    m.then_inc(S["kk_mm"], 1)
                    pe.wait_ge(S["at_ok"], i * 2 + (q + 1))
                    nc.tensor.matmul(psum[:, 2 * q + 1, 0:128], f["bd"], wd[q].rearrange("p e i -> p (e i)"), start=True, stop=True,
                                     skip_group_check=True).then_inc(S["w_mm"], 1)
            pe.wait_ge(S["wvg_in"], 48)
            pe.wait_ge(S["at_ok"], NC + 2)
            for m_ in range(2 * TT):
                t = m_ // 2
                if m_ >= 4:
                    pe.wait_ge(*((S["gt_ok"], t - 1) if m_ % 2 else (S["v_ok"], t - 1)))
                for k in range(KC):
                    m = nc.tensor.matmul(psum[:, m_ % 4, :], hT[:, k, t * 128:(t + 1) * 128], proj["wg" if m_ % 2 else "wv"][:, k, :],
                                         start=(k == 0), stop=(k == KC - 1))
                m.then_inc(S["vg_mm"], 1)
            for hh in range(2):
                pe.sem_inc(S[f"o_mm{hh}"], 2)
            pe.wait_ge(S["bdz"], 2)
            with pe.Fori(0, NC // 2) as i:
                for q in range(2):
                    c = i * 2 + q
                    pe.wait_ge(S["kqs"], c * 2 + 2)
                    for hh in range(2):
                        pe.wait_ge(S[f"s_ok{hh}"], c + 1)
                        for w_ in range(2):
                            for s_ in range(2):
                                m = nc.tensor.matmul(psum[64 * s_:64 * s_ + 64, 4 * hh + w_, 0:256], kqb[q][:, 2 * hh + s_, w_, :],
                                                     state[:, (2 * s_ + hh) * 256:(2 * s_ + hh) * 256 + 256],
                                                     start=True, stop=True, skip_group_check=True)
                            m.then_inc(S[f"ks_mm{hh}"], 1)
                    pe.wait_ge(S[f"x_in{q}"], i * 64 + 64)
                    for hh in range(2):
                        pe.wait_ge(S[f"r_ok{hh}"], c + 1)
                        for g_ in range(hh * X, hh * X + X):
                            m = nc.tensor.matmul(psum[:, 4 * hh + 2, g_ % X * 64:(g_ % X + 1) * 64], xbd[q][:, g_, :],
                                                 resid[:, g_ * 64:(g_ + 1) * 64], start=True, stop=True, skip_group_check=True)
                        m.then_inc(S[f"u_mm{hh}"], 1)
                    pe.wait_ge(S[f"kv_in{q}"], i * 16 + 16)
                    for hh in range(2):
                        pe.wait_ge(S[f"up_ok{hh}"], c + 1)
                        for s_ in range(2):
                            m = nc.tensor.matmul(psum[:, 4 * hh + s_, 256:512], kbd[q][64 * s_:64 * s_ + 64, hh, :],
                                                 ups[64 * s_:64 * s_ + 64, hh * 256:hh * 256 + 256],
                                                 start=True, stop=True, skip_group_check=True)
                        m.then_inc(S[f"su_mm{hh}"], 1)
                        pe.wait_ge(S[f"a_in{q}"], i * 64 + 64)
                        pe.wait_ge(S[f"u_ok{hh}"], c + 1)
                        pe.wait_ge(S["o_ok"], c * 2 + (hh + 3))
                        for e in range(X):
                            g_ = hh * X + e
                            m = nc.tensor.matmul(psum[:, 4 * hh + 3, 0:64], abd[q][:, g_, :], usb[:, g_ * 64:(g_ + 1) * 64],
                                                 start=(e == 0), stop=(e == X - 1), skip_group_check=True)
                        m.then_inc(S[f"o_mm{hh}"], 1)
            def core_T(t):
                pe.wait_ge(S["core_ok"], t + 1)
                if t >= 2:
                    pe.wait_ge(S["cT_ok"], t - 1)
                for k in range(KC):
                    m = nc.tensor.transpose(psum[:, t % 2, k * 128:(k + 1) * 128], core[:, t, k * 128:(k + 1) * 128], ident[:, :])
                m.then_inc(S["cT_mm"], 1)

            core_T(0)
            for t in range(NT):
                if t + 1 < TT:
                    core_T(t + 1)
                pe.wait_ge(S["cT_ok"], t + 1)
                if t >= 2:
                    pe.wait_ge(S["out_ok"], t - 1)
                for k in range(KC):
                    m = nc.tensor.matmul(psum[0:TP, 3 + t % 2, :], coreT[:, k, t * TP:(t + 1) * TP], proj["wo"][:, k, :],
                                         start=(k == 0), stop=(k == KC - 1))
                m.then_inc(S["out_mm"], 1)

        @block.vector
        def _(v):
            st = Steps(v, S["dve"])
            for t in range(NT):
                if t % (NT // 2) == 0:
                    v.wait_ge(S[f"tok_in{t // (NT // 2)}"], 16)
                st.did(nc.vector.bn_stats(stats[:, t, :], xt[:, t, :]))
            st.settle()
            for t in range(NT):
                st.did(nc.vector.bn_aggr(mv[:, t, :], stats[:, t, :]))
            st.settle()
            nc.vector.tensor_scalar(rstd[:, :], mv[:, :, 1], LN_EPS, None, ALU.add).then_inc(S["ln_mv"], 1)
            v.wait_ge(S["ln_std"], 1)
            st.then(nc.vector.reciprocal(rstd[:, :], rstd[:, :]))
            for t in range(NT):
                nc.vector.tensor_scalar(ht[0:TP, t, :], xt[:, t, :], mv[:, t, 0:1], rstd[:, t:t + 1],
                                        ALU.subtract, ALU.mult).then_inc(S["ln_h"], 1)
            v.wait_ge(S["ids_in"], 32)
            st.then(nc.vector.tensor_copy(dstf, dsti))
            st.then(nc.vector.tensor_scalar(rel, dstf, -1.0, None, ALU.mult))
            nc.vector.tensor_reduce(a["start"].rearrange("p (b g) -> p b g", g=2), rel.rearrange("p (b t g) -> p b g t", t=GT, g=2), AX.X, ALU.max)\
                .then_inc(S["spans"], 1)
            nc.vector.tensor_reduce(a["high"].rearrange("p (b g) -> p b g", g=2), dstf.rearrange("p (b t g) -> p b g t", t=GT, g=2), AX.X, ALU.max)\
                .then_inc(S["spans"], 1)
            for t in range(NT):
                v.wait_ge(S["ln_T"], t + 1)
                nc.vector.tensor_copy(hT[:, :, t * TP:(t + 1) * TP],
                                      psum[:, t % 2, 0:KC * TP].rearrange("p (k n) -> p k n", k=KC))\
                    .then_inc(S["ln_hT"], 1)
            v.wait_ge(S["base_ok"], 2)
            st.then(nc.vector.tensor_tensor(a["high"], a["high"], a["base"], ALU.add))
            st.then(nc.vector.tensor_reduce(a["span"], a["high"], AX.X, ALU.max))
            st.then(nc.vector.tensor_copy(npass, a["span"]))
            nc.vector.tensor_scalar(npass, npass, W.bit_length() - 1, None, ALU.logical_shift_right)\
                .then_inc(S["pass_ok"], 1)
            v.wait_ge(S["iota_ok"], 1)
            st.then(nc.vector.tensor_copy(a["iota"], a["iota"].bitcast(I32)))
            st.then(nc.vector.tensor_scalar(a["start"], a["base"], -1.0, None, ALU.mult))
            for t in range(NT):
                v.wait_ge(S["P_mm"], t + 1)
                if t >= 2:
                    v.wait_ge(S[f"P_out{t % 2}"], 16 * (t // 2))
                nc.vector.tensor_tensor(pw[:, t % 2, :], psum[0:TP, 2 + t % 2, :], a["b1"], ALU.add)\
                    .then_inc(S["P_sb"], 1)
            st.then(nc.vector.tensor_reduce(a["fold"].rearrange("p (g w) -> p g w", g=2),
                                            ident[:, :].rearrange("p (g j w) -> p g w j", g=2, w=W), AX.X, ALU.add))
            v.sem_inc(S["pre_add"], RB)
            v.sem_inc(S["acc_add"], 2)
            v.wait_ge(S["consts"], 3)
            n = passes(v)
            base_n = st.n
            with v.Fori(0, n + 1) as p:
                PER_PASS = 3
                c0 = base_n + p * PER_PASS

                def chain(ins, k):
                    ins.then_inc(S["dve"], 1)
                    v.wait_ge(S["dve"], c0 + k)

                startb = a["start"].rearrange("p (b g) -> p b g", g=2)[:, :, None, :].to_broadcast([TP, NB, GT, 2])
                chain(nc.vector.tensor_tensor(rel.rearrange("p (b t g) -> p b t g", t=GT, g=2),
                                              dstf.rearrange("p (b t g) -> p b t g", t=GT, g=2), startb, ALU.subtract), 1)
                chain(nc.vector.tensor_copy(starti[0:1, :], a["start"][0:1, :]), 2)
                chain(nc.vector.tensor_scalar(a["start"], a["start"], float(W), float(N), ALU.add, ALU.min), 3)

                def add(i, k):
                    v.wait_ge(S["pre_mm"], p * ET + i * BODY + (BODY + k + 1))
                    v.wait_ge(gath[k], p * (NB * 16) + i * 16 + 16)
                    nc.vector.tensor_tensor(pg[:, k, :], psum[0:TP, k % RB, :], pg[:, k, :], ALU.add)\
                        .then_inc(S["pre_add"], 1)

                def onehot(i):
                    v.wait_ge(S["deg_mm"], p * NB + i + 1)
                    for g in range(2):
                        nc.vector.tensor_tensor(
                            oh[:, g, :, :],
                            a["iota"][:, None, :].to_broadcast([TP, GT, W]),
                            rel[:, bass.ds(i * BODY, BODY)].rearrange("p (t g) -> p g t", g=2)[:, g][:, :, None].to_broadcast([TP, GT, W]),
                            ALU.is_equal).then_inc(S["oh_ok"], 1)

                def acc_add(i, g):
                    s = v.value_load(starti[0:1, bass.ds(i * 2 + g, 1)], min_val=0, max_val=N)
                    if g == 0:
                        v.wait_ge(S["fold_mm"], p * NB + i + 2)
                        v.wait_ge(S["deg_mm"], p * NB + i + 2)
                    v.wait_ge(S["acc_add"], p * G + i * 2 + (g + 2))
                    if g == 0:
                        nc.vector.tensor_reduce(a["deg"].rearrange("p (g w) -> p g w", g=2),
                                                psum[W:W + 1, 6, 0:BODY * W].rearrange("p (g t w) -> p g w t", g=2, w=W), AX.X, ALU.add)\
                            .then_inc(S["deg_ok"], 1)
                    nc.vector.tensor_tensor(accT[:, 0:KC, bass.ds(s, W)], accT[:, 0:KC, bass.ds(s, W)],
                                            psum[:, 7, 0:2 * KC * W].rearrange("p (c g w) -> p c g w", g=2, w=W)[:, :, g, :], ALU.add)
                    v.wait_ge(S["deg_ok"], p * NB + i + 1)
                    nc.vector.tensor_tensor(accT[0:1, KC, bass.ds(s, W)], accT[0:1, KC, bass.ds(s, W)],
                                            a["deg"][:, g * W:(g + 1) * W], ALU.add).then_inc(S["acc_add"], 1)

                def body(i, first):
                    add(i, 0)
                    add(i, 1)
                    if not first:
                        onehot(i)
                    for k in range(2, 8):
                        add(i, k)
                    if not first:
                        for g in range(2):
                            acc_add(i - 1, g)
                    add(i, 8)
                    add(i, 9)

                onehot(0)
                body(0, True)
                with v.Fori(1, NB) as i:
                    body(i, False)
                for g in range(2):
                    acc_add(NB - 1, g)
            st = Steps(v, S["dve2"])
            v.wait_ge(S["acc_add"], n * G + (G + 2))
            v.sem_inc(S["out_d"], 1)
            v.wait_ge(S["vec_in"], 16 * 6)
            bias_rz, bias_in, bias_hn = vec[:, 0:2 * D], vec[:, 2 * D:3 * D], vec[:, 5 * D:6 * D]
            gamma, beta, rmean, rvar = (vec[:, (6 + k) * D:(7 + k) * D] for k in range(4))
            nc.vector.tensor_scalar(rvar, rvar, BN_EPS, None, ALU.add).then_inc(S["bn_pre"], 1)
            st.then(nc.vector.tensor_tensor(bias_rz, bias_rz, vec[:, 3 * D:5 * D], ALU.add))
            v.wait_ge(S["bn_std"], 1)
            st.then(nc.vector.reciprocal(rvar, rvar))
            st.then(nc.vector.tensor_tensor(gamma, gamma, rvar, ALU.mult))
            st.then(nc.vector.tensor_tensor(rmean, rmean, gamma, ALU.mult))
            st.then(nc.vector.tensor_tensor(beta, beta, rmean, ALU.subtract))
            for t in range(NT):
                q = 4 * (t % 2)
                new, hn, nn, rz = bo["new"], bo["hn"], bo["in"], bo["rz"]
                v.wait_ge(S["gate_mm"], t + 1)
                nc.vector.tensor_tensor(rz.rearrange("p (g n) -> p g n", g=2), psum[0:TP, q:q + 2, :],
                                        bias_rz.rearrange("p (g n) -> p g n", g=2), ALU.add).then_inc(S["rz_pre"], 1)
                nc.vector.tensor_tensor(hn, psum[0:TP, q + 3, :], bias_hn, ALU.add).then_inc(S["gate_rd"], 1)
                nc.vector.tensor_tensor(nn, psum[0:TP, q + 2, :], bias_in, ALU.add).then_inc(S["gate_rd"], 1)
                v.wait_ge(S["rz"], t + 1)
                v.wait_ge(S["gate_rd"], 3 * t + 2)
                nc.vector.tensor_tensor(hn, hn, rz[:, 0:D], ALU.mult).then_inc(S["gate_rd"], 1)
                v.wait_ge(S["gate_rd"], 3 * t + 3)
                nc.vector.tensor_tensor(nn, nn, hn, ALU.add).then_inc(S["n_pre"], 1)
                v.wait_ge(S["n_ok"], t + 1)
                st.then(nc.vector.tensor_tensor(new, ht[0:TP, t, :], nn, ALU.subtract))
                st.then(nc.vector.tensor_tensor(new, new, rz[:, D:2 * D], ALU.mult))
                st.then(nc.vector.tensor_tensor(new, new, nn, ALU.add))
                st.then(nc.vector.tensor_tensor(new, new, gamma, ALU.mult))
                st.then(nc.vector.tensor_tensor(new, new, beta, ALU.add))
                st.then(nc.vector.tensor_tensor(new, new, ht[0:TP, t, :], ALU.add))
                nc.vector.tensor_tensor(xt[:, t, :], xt[:, t, :], new, ALU.add).then_inc(S["x1_ok"], 1)
                v.wait_ge(S["x1_ok"], t + 1)
                st.then(nc.vector.bn_stats(stats[:, t, :], xt[:, t, :]))
                st.then(nc.vector.bn_aggr(mv[:, t, :], stats[:, t, :]))
                nc.vector.tensor_scalar(rstd[:, t:t + 1], mv[:, t, 1:2], LN_EPS, None, ALU.add).then_inc(S["ln2_mv"], 1)
                v.wait_ge(S["ln2_std"], t + 1)
                st.then(nc.vector.reciprocal(rstd[:, t:t + 1], rstd[:, t:t + 1]))
                nc.vector.tensor_scalar(ht[0:TP, t, :], xt[:, t, :], mv[:, t, 0:1], rstd[:, t:t + 1],
                                        ALU.subtract, ALU.mult).then_inc(S["ln2_h"], 1)
            def square(q, t):
                v.wait_ge(S["z_ok"], q * TT + t + 1)
                st.then(nc.vector.tensor_tensor(sq[t % 2], kq[:, q, t, :], kq[:, q, t, :], ALU.mult))
                st.did(nc.vector.tensor_reduce(norms[:, q, t, :], sq[t % 2].rearrange("p (h k) -> p h k", h=H), AX.X, ALU.add))

            def routing():
                v.wait_ge(S["sm_mm"], TT)
                v.wait_ge(S["cst_in"], 64)
                sm = psum[:, 3, 0:TT * 20].rearrange("p (t n) -> p t n", t=TT)

                def over(x, *shape):
                    return x.to_broadcast([128, *shape])

                st.then(nc.vector.tensor_reduce(rt["mx"], sm[:, :, 16:20], AX.X, ALU.max))
                nc.vector.tensor_tensor(rt["lg"], sm[:, :, 16:20], over(rt["mx"][:, :, None], TT, X), ALU.subtract).then_inc(S["lg_pre"], 1)
                st.then(nc.vector.tensor_tensor(rt["a"], sm[:, :, 0:8], over(f["dtb"][:, None, :], TT, H), ALU.add))
                st.then(nc.vector.tensor_scalar(rt["t1"], rt["a"], -1.0, None, ALU.mult))
                nc.vector.tensor_tensor(rt["ax"], rt["a"], rt["t1"], ALU.max).then_inc(S["ab_pre"], 1)
                nc.vector.tensor_copy(rt["b"], sm[:, :, 8:16]).then_inc(S["ab_pre"], 1)
                v.wait_ge(S["p_ok"], 1)
                p_ = rt["p"]
                st.then(nc.vector.tensor_reduce(rt["mx"], p_, AX.X, ALU.add))
                st.then(nc.vector.reciprocal(rt["mx"], rt["mx"]))
                st.then(nc.vector.tensor_tensor(p_, p_, over(rt["mx"][:, :, None], TT, X), ALU.mult))
                other, own = over(p_[:, :, None, :], TT, X, X), over(p_[:, :, :, None], TT, X, X)
                st.did(nc.vector.tensor_tensor(rt["gt"], other, own, ALU.is_gt))
                st.then(nc.vector.tensor_tensor(rt["eq"], other, own, ALU.is_equal))
                st.then(nc.vector.tensor_tensor(rt["eq"], rt["eq"], over(f["lt4"].rearrange("p (a b) -> p a b", a=X)[:, None], TT, X, X), ALU.mult))
                st.then(nc.vector.tensor_tensor(rt["gt"], rt["gt"], rt["eq"], ALU.add))
                st.then(nc.vector.tensor_reduce(rt["lg"], rt["gt"], AX.X, ALU.add))
                st.then(nc.vector.tensor_scalar(rt["lg"], rt["lg"], 2.0, None, ALU.is_lt))
                st.then(nc.vector.tensor_tensor(p_, p_, rt["lg"], ALU.mult))
                st.then(nc.vector.tensor_reduce(rt["mx"], p_, AX.X, ALU.add))
                st.then(nc.vector.reciprocal(rt["mx"], rt["mx"]))
                st.then(nc.vector.tensor_tensor(p_, p_, over(rt["mx"][:, :, None], TT, X), ALU.mult))
                st.then(nc.vector.tensor_scalar(rt["lg"], p_, 0.0, None, ALU.is_gt))
                v.wait_ge(S["ab_ok"], 3)
                st.then(nc.vector.tensor_scalar(rt["eb"], rt["eb"], 1.0, None, ALU.add))
                st.then(nc.vector.reciprocal(rt["eb"], rt["eb"]))
                st.then(nc.vector.tensor_scalar(rt["t1"], rt["y"], 2.0, None, ALU.add))
                st.then(nc.vector.reciprocal(rt["t1"], rt["t1"]))
                st.then(nc.vector.tensor_tensor(rt["y"], rt["y"], rt["t1"], ALU.mult))
                st.then(nc.vector.tensor_tensor(rt["t1"], rt["y"], rt["y"], ALU.mult))
                st.then(nc.vector.tensor_scalar(rt["ax"], rt["t1"], 2.0 / (2 * LOG_TERMS - 1), None, ALU.mult))
                for k in range(LOG_TERMS - 2, -1, -1):
                    st.then(nc.vector.tensor_scalar(rt["ax"], rt["ax"], 2.0 / (2 * k + 1), None, ALU.add))
                    st.then(nc.vector.tensor_tensor(rt["ax"], rt["ax"], rt["t1"] if k else rt["y"], ALU.mult))
                st.then(nc.vector.tensor_scalar(rt["a"], rt["a"], 0.0, None, ALU.max))
                st.then(nc.vector.tensor_tensor(rt["a"], rt["a"], rt["ax"], ALU.add))
                st.then(nc.vector.tensor_tensor(rt["a"], rt["a"], over(rt["ea"][:, None, :], TT, H), ALU.mult))
                st.then(nc.vector.tensor_scalar(rt["a"], rt["a"], -1.0, G_FLOOR, ALU.mult, ALU.max))
                for h in range(4):
                    m4 = over(rt["lg"][:, :, None, :], TT, 2, X)
                    for q, val in ((0, rt["a"]), (1, rt["eb"])):
                        nc.vector.tensor_tensor(gwt[:, :, h, q, :, :], over(val[:, :, 2 * h:2 * h + 2][:, :, :, None], TT, 2, X),
                                                m4, ALU.mult).then_inc(S["gw_ok"], 1)
                    nc.vector.tensor_copy(gwt[:, :, h, 2, :, :], over(p_[:, :, None, :], TT, 2, X)).then_inc(S["gw_ok"], 1)

            for q in range(2):
                for t in range(TT):
                    square(q, t)
                st.settle()
                nc.vector.tensor_scalar(norms[:, q], norms[:, q], 1e-6, float(DK) if q else 1.0, ALU.add, ALU.mult).then_inc(S["ss_ok"], 1)
                v.wait_ge(S["nrm_ok"], q + 1)
                st.then(nc.vector.reciprocal(norms[:, q], norms[:, q]))
                for t in range(TT):
                    by_head = kq[:, q, t, :].rearrange("p (h k) -> p h k", h=H)
                    nc.vector.tensor_tensor(by_head, by_head, norms[:, q, t, :][:, :, None].to_broadcast([128, H, DK]), ALU.mult)\
                        .then_inc(S["kq_ok"], 1)
                if q == 0:
                    routing()
            v.wait_ge(S["dec_ok"], 4)
            st.did(nc.vector.tensor_tensor(bDC, bDC, gw[:, :, 8:16], ALU.mult))
            st.then(nc.vector.tensor_tensor(wGam, Gam, gw[:, :, 16:24], ALU.mult))
            v.sem_inc(S["at_ok"], 2)
            for q in range(2):
                v.sem_inc(S[f"lt_st{q}"], 16)
                v.sem_inc(S[f"at_st{q}"], 16)
            v.sem_inc(S["kk_rd"], 2)
            v.sem_inc(S["at1_ok"], 2)
            base2 = st.n

            def four(x):
                return x.rearrange("p (h e) i -> p h e i", h=2)

            def attention(i, q):
                c = i * 2 + q
                v.wait_ge(S["w_mm"], c + 3)
                v.wait_ge(S[f"at_st{q}"], i * 16 + 16)
                v.wait_ge(S["at1_ok"], c + 3)
                nc.vector.tensor_tensor(four(at[q]), four(at1),
                                        psum[:, 2 * q + 1, 0:128].rearrange("p (e i) -> p e i", e=X)[:, None].to_broadcast([128, 2, X, C]),
                                        ALU.mult).then_inc(S["at_ok"], 1)

            def in_chunk(i, first):
                for q in range(2):
                    c = i * 2 + q
                    v.wait_ge(S["e_ok"], c + 3)
                    bch = gw[:, bass.ds(c, 1), 8:16].rearrange("p c n -> p (c n)")
                    nc.vector.tensor_tensor(ex[q], ex[q], bch[:, :, None].to_broadcast([128, SG, C]), ALU.mult).then_inc(S["dve2"], 1)
                    if not (first and q == 0):
                        attention(i - 1 + q, 1 - q)
                    v.wait_ge(S["kk_mm"], c + 3)
                    nc.vector.tensor_tensor(kkm, psum[:, 4 + q, 0:128].rearrange("p (h q i) -> p h q i", h=2, q=2),
                                            f["mask2"].rearrange("p (q i) -> p q i", q=2)[:, None].to_broadcast([128, 2, 2, C]),
                                            ALU.mult).then_inc(S["kk_rd"], 1)
                    v.wait_ge(S["dve2"], i * 2 + (base2 + q + 1))
                    v.wait_ge(S["kk_rd"], c + 3)
                    v.wait_ge(S[f"lt_st{q}"], i * 16 + 16)
                    nc.vector.tensor_tensor(four(lt[q]), four(ex[q]), kkm[:, :, 0, :][:, :, None, :].to_broadcast([128, 2, X, C]),
                                            ALU.mult).then_inc(S["lt_ok"], 1)
                    nc.vector.tensor_tensor(four(at1), four(ex[q]), kkm[:, :, 1, :][:, :, None, :].to_broadcast([128, 2, X, C]),
                                            ALU.mult).then_inc(S["at1_ok"], 1)

            in_chunk(0, True)
            with v.Fori(1, NC // 2) as i:
                in_chunk(i, False)
            attention(NC // 2 - 1, 1)
            st.n = base2 + NC
            for hf in range(2):
                XT = systems[hf]
                for q in range(2):
                    v.wait_ge(S[f"at_st{q}"], 16 * NC // 2 + 16)
                v.wait_ge(S[f"l_in{hf}"], 16 * QG)
                st.then(nc.vector.memset(XT.rearrange("p q n i -> p q (n i)")[:, :, ::C + 1], 1.0))
                for j in range(1, C - 1):
                    left = C - 1 - j
                    pr = Prod[:, 0:QG * j * left].rearrange("p (q n i) -> p q n i", q=QG, n=j)
                    st.then(nc.vector.tensor_tensor(pr, XT[:, :, j, j + 1:C][:, :, None, :].to_broadcast([128, QG, j, left]),
                                                    XT[:, :, 0:j, j][:, :, :, None].to_broadcast([128, QG, j, left]), ALU.mult))
                    ins = nc.vector.tensor_tensor(XT[:, :, 0:j, j + 1:C], XT[:, :, 0:j, j + 1:C], pr, ALU.add)
                    if j < C - 2:
                        st.then(ins)
                    else:
                        ins.then_inc(S["x_ok"], 1)
            v.wait_ge(S["bdz"], 2)
            for hh in range(2):
                v.sem_inc(S[f"s_ok{hh}"], 1)
            v.sem_inc(S["o_ok"], 4)
            for q in range(2):
                v.sem_inc(S[f"o_st{q}"], 16)
            base4 = st.n
            with v.Fori(0, NC // 2) as i:
                for q in range(2):
                    c = i * 2 + q
                    c0 = base4 + i * 12 + 6 * q

                    def step(ins):
                        ins.then_inc(S["dve2"], 1)

                    def half(x, hh):
                        return x[:, hh * 256:(hh + 1) * 256].rearrange("p (e v) -> p e v", e=X)

                    def bank(k, hh):
                        return psum[:, 4 * hh + k, 0:256].rearrange("p (e v) -> p e v", e=X)

                    def per_system(x, hh):
                        return x[:, bass.ds(c, 1), hh * X:(hh + 1) * X].rearrange("p c n -> p (c n)")[:, :, None].to_broadcast([128, X, DK])

                    for hh in range(2):
                        v.wait_ge(S[f"ks_mm{hh}"], c * 2 + 1)
                        step(nc.vector.tensor_tensor(half(ksd, hh), bank(0, hh), per_system(Gam, hh), ALU.mult))
                        v.wait_ge(S[f"kv_in{q}"], i * 16 + 16)
                        v.wait_ge(S["dve2"], c0 + hh + 1)
                        nc.vector.tensor_tensor(half(resid, hh), vch[q][:, hh * DK:(hh + 1) * DK][:, None, :].to_broadcast([128, X, DK]),
                                                half(ksd, hh), ALU.subtract).then_inc(S[f"r_ok{hh}"], 1)
                    for hh in range(2):
                        v.wait_ge(S[f"ks_mm{hh}"], c * 2 + 2)
                        step(nc.vector.tensor_tensor(half(qsd, hh), bank(1, hh), per_system(wGam, hh), ALU.mult))
                    for hh in range(2):
                        v.wait_ge(S[f"u_mm{hh}"], c + 1)
                        nc.vector.tensor_tensor(half(ups, hh), bank(2, hh), per_system(bDC, hh), ALU.mult).then_inc(S[f"up_ok{hh}"], 1)
                    v.wait_ge(S["dve2"], c0 + 4)
                    step(nc.vector.tensor_reduce(qsr[:, 0:64], half(qsd, 0).rearrange("p e v -> p v e"), AX.X, ALU.add))
                    for hh in range(2):
                        v.wait_ge(S[f"su_mm{hh}"], c + 1)
                        v.wait_ge(S[f"sd_ok{hh}"], c + 1)
                        nc.vector.tensor_tensor(state4[:, :, hh].rearrange("p s e v -> p s (e v)"), sdec4[:, :, hh].rearrange("p s e v -> p s (e v)"),
                                                psum[:, 4 * hh:4 * hh + 2, 256:512], ALU.add).then_inc(S[f"s_ok{hh}"], 1)
                        if hh == 0:
                            step(nc.vector.tensor_reduce(qsr[:, 64:128], half(qsd, 1).rearrange("p e v -> p v e"), AX.X, ALU.add))
                        v.wait_ge(S[f"o_mm{hh}"], c + 3)
                        v.wait_ge(S[f"o_st{q}"], i * 16 + 16)
                        v.wait_ge(S["dve2"], c0 + 6)
                        nc.vector.tensor_tensor(osb[q][:, hh * 64:(hh + 1) * 64], psum[:, 4 * hh + 3, 0:64], qsr[:, hh * 64:(hh + 1) * 64],
                                                ALU.add).then_inc(S["o_ok"], 1)
            st.n = base4 + 6 * NC
            v.wait_ge(S["gn_ok"], TT)

            def squares(t):
                if t == 0:
                    v.wait_ge(S["core_in"], 16 * (NC - 4))
                elif t == TT - 1:
                    v.wait_ge(S["core_last"], 16 * 4)
                st.then(nc.vector.tensor_tensor(sqb, core[:, t, :], core[:, t, :], ALU.mult))
                st.then(nc.vector.tensor_reduce(cstat[:, t, :], sqb.rearrange("p (h v) -> p h v", h=H), AX.X, ALU.add))
                nc.vector.tensor_scalar(cstat[:, t, :], cstat[:, t, :], 1.0 / DK, 1e-5, ALU.mult, ALU.add).then_inc(S["cn_a"], 1)

            def add_output(t):
                v.wait_ge(S["out_mm"], t + 1)
                nc.vector.tensor_tensor(xt[:, t, :], xt[:, t, :], psum[0:TP, 3 + t % 2, :], ALU.add).then_inc(S["out_ok"], 1)

            squares(0)
            for t in range(TT):
                if t + 1 < TT:
                    squares(t + 1)
                v.wait_ge(S["cn_b"], t + 1)
                st.then(nc.vector.reciprocal(cstat[:, t, :], cstat[:, t, :]))
                ct = core[:, t, :].rearrange("p (h v) -> p h v", h=H)
                st.then(nc.vector.tensor_tensor(ct, ct, cstat[:, t, :][:, :, None].to_broadcast([128, H, DK]), ALU.mult))
                nc.vector.tensor_tensor(core[:, t, :].rearrange("p (k n) -> p k n", k=KC), core[:, t, :].rearrange("p (k n) -> p k n", k=KC),
                                        gate[:, :, t * 128:(t + 1) * 128], ALU.mult).then_inc(S["core_ok"], 1)
                if t >= 2:
                    add_output(t - 2)
            add_output(TT - 2)
            add_output(TT - 1)


def _constants():
    p = np.arange(128)
    blk, j = p // C, p % C
    same = blk[:, None] == blk[None, :]
    i = np.arange(C)
    h2 = p // 64
    parts = [
        same & (j[:, None] > j[None, :]),
        same & (j[:, None] <= j[None, :]),
        same,
        blk[:, None] == h2[None, :],
        blk[:, None] == 2 + h2[None, :],
        j[:, None] <= i[None, :],
        j[:, None] == i[None, :],
        np.concatenate([-1.0 * (i[None, :] > j[:, None]), i[None, :] >= j[:, None]], 1),
        np.broadcast_to((i[None, :X] < i[:X, None]).reshape(1, X * X), (128, X * X)),
    ]
    return np.ascontiguousarray(np.concatenate([x.astype(np.float32) for x in parts], 1))


def kernel(**inputs):
    import concourse.bacc as _bacc
    from concourse.bass_utils import run_bass_kernel_spmd as _run

    c = np.ascontiguousarray
    get = {k: np.asarray(v) for k, v in inputs.items()}
    w1 = get["L0_gnn_W1"]

    def tiles(x):
        rest = x.shape[1:]
        return np.swapaxes(x.reshape(NB, 2, GT, TP, *rest), 1, 2).reshape(ET, TP, *rest)

    arrays = {
        "x": c(get["x"]),
        "src_t": tiles(get["src"]).T.copy(),
        "dst_t": tiles(get["dst"]).T.copy(),
        "ea_T": c(tiles(get["edge_attr_128"]).reshape(E, ED).T),
        "w1h_T": c(w1[:, :D].T),
        "w1e_T": c(w1[:, D:].T),
        "b1": c(get["L0_gnn_b1"][None, :]),
        "w2_T": c(get["L0_gnn_W2"].T),
        "b2": c(get["L0_gnn_b2"][None, :]),
        "wih_T": c(get["L0_gnn_W_ih"].T),
        "whh_T": c(get["L0_gnn_W_hh"].T),
    }
    for n in ("b_ih", "b_hh", "gamma", "beta", "run_mean", "run_var"):
        arrays[n] = c(get["L0_gnn_" + n][None, :])
    order = np.array([4 * hh + h4 for h4 in range(4) for hh in range(2)])

    def heads(w, axis):
        shape = list(w.shape)
        shape[axis:axis + 1] = [H, shape[axis] // H]
        return c(np.take(w.reshape(shape), order, axis=axis).reshape(w.shape))

    arrays["wq"], arrays["wk"] = c(get["L0_ffn_Wq"]), c(get["L0_ffn_Wk"])
    arrays["wv"], arrays["wg"] = heads(get["L0_ffn_Wv"], 1), heads(get["L0_ffn_Wg"], 1)
    arrays["wo"] = heads(get["L0_ffn_Wo"], 0)
    arrays["wsm"] = c(np.concatenate([heads(get["L0_ffn_Wa"], 1), heads(get["L0_ffn_Wb"], 1), get["L0_ffn_Wgate"]], 1))
    arrays["alog"], arrays["dtb"] = heads(get["L0_ffn_A_log"], 0)[None, :], heads(get["L0_ffn_dt_bias"], 0)[None, :]
    arrays["onorm"] = c(get["L0_ffn_o_norm_weight"][None, :])
    arrays["cst"] = _constants()
    nc = _bacc.Bacc("TRN2", target_bir_lowering=False, num_devices=1)
    io = {n: nc.dram_tensor(n, v.shape, mybir.dt.from_np(v.dtype), kind="ExternalInput").ap()
          for n, v in arrays.items()}
    io["out"] = nc.dram_tensor("out", (N, D), F32, kind="ExternalOutput").ap()
    build(nc, io)
    r = _run(nc, [arrays], core_ids=[0])
    return r.results[0]["out"]
```
